# Optimizing a Trainium2 kernel written in Bass

```python
import numpy as np
import jax
import jax.numpy as jnp

def _softmax(x, axis=-1):
    return jax.nn.softmax(x, axis=axis)

def _gelu(x):
    return jax.nn.gelu(x, approximate=True)

def _silu(x):
    return jax.nn.silu(x)

def _sigmoid(x):
    return jax.nn.sigmoid(x)

def _layernorm(x, axis=-1, eps=1e-05):
    m = jnp.mean(x, axis=axis, keepdims=True)
    v = jnp.var(x, axis=axis, keepdims=True)
    return (x - m) / jnp.sqrt(v + eps)

def _scatter_add(tgt, idx, src, axis=0):
    return tgt.at[idx].add(src)

def _segment_sum(src, seg, n):
    return jax.ops.segment_sum(src, seg, n)
kernel_name = 'mk_vit_tower_cls_d1_tok_img768_r4_8ad60f'

def setup_inputs(seed: int=0):
    np.random.seed(seed)
    _w = jnp.asarray

    def _rec_inputs():
        import jax
        import jax.numpy as jnp
        _rk = jax.random.key(seed)
        x = -0.000356955 + 1 * jax.random.normal(jax.random.fold_in(_rk, 1), (64, 3, 224, 224), jnp.float32)
        cls_tok = 0.02 * jax.random.normal(jax.random.fold_in(_rk, 5), (1, 1, 192), jnp.float32)
        return (x, cls_tok)
    x, cls_tok = _rec_inputs()

    def _L0_tok_setup():
        import jax, jax.numpy as jnp
        import numpy as np
        IMG = 224
        PATCH = 16
        C_IN = 3
        EMBED = 192
        NP_SIDE = IMG // PATCH
        NUM_PATCHES = NP_SIDE * NP_SIDE
        PATCH_DIM = C_IN * PATCH * PATCH
        key = jax.random.key(seed)
        kx, kw, kb = jax.random.split(key, 3)
        x = jax.random.normal(kx, (128, C_IN, IMG, IMG), dtype=jnp.float32)
        bound = 1.0 / np.sqrt(PATCH_DIM)
        W = jax.random.uniform(kw, (EMBED, PATCH_DIM), minval=-bound, maxval=bound, dtype=jnp.float32)
        b = jax.random.uniform(kb, (EMBED,), minval=-bound, maxval=bound, dtype=jnp.float32)
        return {'x': x, 'W': W, 'b': b}
    _L0_tok_all = _L0_tok_setup()
    _L0_tok_in = {k: v for k, v in _L0_tok_all.items() if k in ('W', 'b')}
    del _L0_tok_all

    def _L0_attn_setup():
        import jax, jax.numpy as jnp
        import numpy as np
        from jax import lax
        HID, STATE, K, EXP = (192, 16, 4, 2)
        INNER = HID * EXP
        B_SZ, L = (2, 256)

        def silu(v):
            return v * jax.nn.sigmoid(v)

        def _forward(x, W_in, conv_w, conv_b, W_x, W_dt, b_dt, A_log, D, W_out, gamma, beta):
            xz = x @ W_in
            x_inner, z = jnp.split(xz, 2, axis=-1)
            x_conv = lax.conv_general_dilated(x_inner, conv_w, window_strides=(1,), padding=[((K - 1) // 2, K // 2)], dimension_numbers=('NWC', 'WIO', 'NWC')) + conv_b
            x_conv = silu(x_conv)
            BC = x_conv @ W_x
            Bm, Cm = jnp.split(BC, 2, axis=-1)
            delta = jax.nn.softplus(x_conv @ W_dt + b_dt)
            A = -jnp.exp(A_log)

            def step(h, inp):
                x_t, d_t, B_t, C_t = inp
                A_disc = jnp.exp(d_t[:, :, None] * A)
                h = A_disc * h + (d_t * x_t)[:, :, None] * B_t[:, None, :]
                y_t = jnp.einsum('bds,bs->bd', h, C_t)
                return (h, y_t)
            xs = (jnp.swapaxes(x_conv, 0, 1), jnp.swapaxes(delta, 0, 1), jnp.swapaxes(Bm, 0, 1), jnp.swapaxes(Cm, 0, 1))
            h0 = jnp.zeros((x.shape[0], A.shape[0], A.shape[1]), dtype=x.dtype)
            _, ys = lax.scan(step, h0, xs)
            y = jnp.swapaxes(ys, 0, 1) + D * x_conv
            y = y * silu(z)
            out = y @ W_out
            mu = jnp.mean(out, axis=-1, keepdims=True)
            var = jnp.mean(jnp.square(out - mu), axis=-1, keepdims=True)
            return (out - mu) * lax.rsqrt(var + 1e-05) * gamma + beta
        key = jax.random.key(seed)
        ks = jax.random.split(key, 12)
        s = 0.02
        x = jax.random.normal(ks[0], (B_SZ, L, HID), dtype=jnp.float32)
        W_in = jax.random.normal(ks[1], (HID, INNER * 2), dtype=jnp.float32) * s
        conv_w = jax.random.normal(ks[2], (K, INNER, INNER), dtype=jnp.float32) * s
        conv_b = jnp.zeros((INNER,), dtype=jnp.float32)
        W_x = jax.random.normal(ks[3], (INNER, STATE * 2), dtype=jnp.float32) * s
        W_dt = jax.random.normal(ks[4], (INNER, INNER), dtype=jnp.float32) * s
        b_dt = jnp.zeros((INNER,), dtype=jnp.float32)
        A_log = jnp.log(jax.random.uniform(ks[5], (INNER, STATE), minval=1.0, maxval=16.0, dtype=jnp.float32))
        D = jnp.ones((INNER,), dtype=jnp.float32)
        W_out = jax.random.normal(ks[6], (INNER, HID), dtype=jnp.float32) * s
        gamma = jnp.ones((HID,), dtype=jnp.float32)
        beta = jnp.zeros((HID,), dtype=jnp.float32)
        return {'x': x, 'W_in': W_in, 'conv_w': conv_w, 'conv_b': conv_b, 'W_x': W_x, 'W_dt': W_dt, 'b_dt': b_dt, 'A_log': A_log, 'D': D, 'W_out': W_out, 'gamma': gamma, 'beta': beta}
    _L0_attn_all = _L0_attn_setup()
    _L0_attn_in = {k: v for k, v in _L0_attn_all.items() if k in ('W_in', 'conv_w', 'conv_b', 'W_x', 'W_dt', 'b_dt', 'A_log', 'D', 'W_out', 'gamma', 'beta')}
    del _L0_attn_all

    def _L0_ffn_setup():
        import jax, jax.numpy as jnp
        import numpy as np
        CAPACITY_FACTOR = 1.25
        key = jax.random.key(seed)
        ks = jax.random.split(key, 5)
        B, S, D, F, E = (8, 512, 192, 768, 8)
        return {'x': jax.random.normal(ks[0], (B, S, D), jnp.float32), 'switch_w': jax.random.normal(ks[1], (D, E), jnp.float32) * 0.02, 'switch_b': jnp.zeros((E,), jnp.float32), 'w1': jax.random.normal(ks[2], (E, D, F), jnp.float32) * 0.02, 'b1': jnp.zeros((E, F), jnp.float32), 'w2': jax.random.normal(ks[3], (E, F, D), jnp.float32) * 0.02, 'b2': jnp.zeros((E, D), jnp.float32)}
    _L0_ffn_all = _L0_ffn_setup()
    _L0_ffn_in = {k: v for k, v in _L0_ffn_all.items() if k in ('switch_w', 'switch_b', 'w1', 'b1', 'w2', 'b2')}
    del _L0_ffn_all
    return {'x': x, 'cls_tok': cls_tok, 'L0_tok_W': _L0_tok_in['W'], 'L0_tok_b': _L0_tok_in['b'], 'L0_attn_W_in': _L0_attn_in['W_in'], 'L0_attn_conv_w': _L0_attn_in['conv_w'], 'L0_attn_conv_b': _L0_attn_in['conv_b'], 'L0_attn_W_x': _L0_attn_in['W_x'], 'L0_attn_W_dt': _L0_attn_in['W_dt'], 'L0_attn_b_dt': _L0_attn_in['b_dt'], 'L0_attn_A_log': _L0_attn_in['A_log'], 'L0_attn_D': _L0_attn_in['D'], 'L0_attn_W_out': _L0_attn_in['W_out'], 'L0_attn_gamma': _L0_attn_in['gamma'], 'L0_attn_beta': _L0_attn_in['beta'], 'L0_ffn_switch_w': _L0_ffn_in['switch_w'], 'L0_ffn_switch_b': _L0_ffn_in['switch_b'], 'L0_ffn_w1': _L0_ffn_in['w1'], 'L0_ffn_b1': _L0_ffn_in['b1'], 'L0_ffn_w2': _L0_ffn_in['w2'], 'L0_ffn_b2': _L0_ffn_in['b2']}

def reference(x, cls_tok, L0_tok_W, L0_tok_b, L0_attn_W_in, L0_attn_conv_w, L0_attn_conv_b, L0_attn_W_x, L0_attn_W_dt, L0_attn_b_dt, L0_attn_A_log, L0_attn_D, L0_attn_W_out, L0_attn_gamma, L0_attn_beta, L0_ffn_switch_w, L0_ffn_switch_b, L0_ffn_w1, L0_ffn_b1, L0_ffn_w2, L0_ffn_b2):
    import jax
    import jax.numpy as jnp

    def _L0_tok_ref(x, W, b):
        import jax, jax.numpy as jnp
        import numpy as np
        IMG = 224
        PATCH = 16
        C_IN = 3
        EMBED = 192
        NP_SIDE = IMG // PATCH
        NUM_PATCHES = NP_SIDE * NP_SIDE
        PATCH_DIM = C_IN * PATCH * PATCH
        B = x.shape[0]
        patches = x.reshape(B, C_IN, NP_SIDE, PATCH, NP_SIDE, PATCH)
        patches = patches.transpose(0, 2, 4, 1, 3, 5)
        patches = patches.reshape(B, NUM_PATCHES, PATCH_DIM)
        return jnp.einsum('bnd,ed->bne', patches, W) + b

    def _L0_attn_ref(x, W_in, conv_w, conv_b, W_x, W_dt, b_dt, A_log, D, W_out, gamma, beta):
        import jax, jax.numpy as jnp
        import numpy as np
        from jax import lax
        HID, STATE, K, EXP = (192, 16, 4, 2)
        INNER = HID * EXP
        B_SZ, L = (2, 256)

        def silu(v):
            return v * jax.nn.sigmoid(v)

        def _forward(x, W_in, conv_w, conv_b, W_x, W_dt, b_dt, A_log, D, W_out, gamma, beta):
            xz = x @ W_in
            x_inner, z = jnp.split(xz, 2, axis=-1)
            x_conv = lax.conv_general_dilated(x_inner, conv_w, window_strides=(1,), padding=[((K - 1) // 2, K // 2)], dimension_numbers=('NWC', 'WIO', 'NWC')) + conv_b
            x_conv = silu(x_conv)
            BC = x_conv @ W_x
            Bm, Cm = jnp.split(BC, 2, axis=-1)
            delta = jax.nn.softplus(x_conv @ W_dt + b_dt)
            A = -jnp.exp(A_log)

            def step(h, inp):
                x_t, d_t, B_t, C_t = inp
                A_disc = jnp.exp(d_t[:, :, None] * A)
                h = A_disc * h + (d_t * x_t)[:, :, None] * B_t[:, None, :]
                y_t = jnp.einsum('bds,bs->bd', h, C_t)
                return (h, y_t)
            xs = (jnp.swapaxes(x_conv, 0, 1), jnp.swapaxes(delta, 0, 1), jnp.swapaxes(Bm, 0, 1), jnp.swapaxes(Cm, 0, 1))
            h0 = jnp.zeros((x.shape[0], A.shape[0], A.shape[1]), dtype=x.dtype)
            _, ys = lax.scan(step, h0, xs)
            y = jnp.swapaxes(ys, 0, 1) + D * x_conv
            y = y * silu(z)
            out = y @ W_out
            mu = jnp.mean(out, axis=-1, keepdims=True)
            var = jnp.mean(jnp.square(out - mu), axis=-1, keepdims=True)
            return (out - mu) * lax.rsqrt(var + 1e-05) * gamma + beta
        return _forward(x, W_in, conv_w, conv_b, W_x, W_dt, b_dt, A_log, D, W_out, gamma, beta)

    def _L0_ffn_ref(x, switch_w, switch_b, w1, b1, w2, b2):
        import jax, jax.numpy as jnp
        import numpy as np
        CAPACITY_FACTOR = 1.25
        B, S, D = x.shape
        E = w1.shape[0]
        xf = x.reshape(-1, D)
        N = xf.shape[0]
        capacity = int(CAPACITY_FACTOR * N / E)
        probs = jax.nn.softmax(xf @ switch_w + switch_b, axis=-1)
        prob_max = jnp.max(probs, axis=-1)
        routes = jnp.argmax(probs, axis=-1)
        sort_idx = jnp.lexsort((-prob_max, routes))
        counts = jnp.bincount(routes, length=E)
        starts = jnp.concatenate([jnp.zeros((1,), counts.dtype), jnp.cumsum(counts)[:-1]])
        rank_sorted = jnp.arange(N) - starts[routes[sort_idx]]
        rank = jnp.zeros((N,), jnp.int32).at[sort_idx].set(rank_sorted.astype(jnp.int32))
        keep = rank < capacity
        dest_e = jnp.where(keep, routes, E)
        dest_c = jnp.where(keep, rank, 0)
        buf = jnp.zeros((E + 1, capacity, D), xf.dtype).at[dest_e, dest_c].set(xf)
        h = jax.nn.gelu(jnp.einsum('ecd,edf->ecf', buf[:E], w1) + b1[:, None, :], approximate=False)
        o = jnp.einsum('ecf,efd->ecd', h, w2) + b2[:, None, :]
        y_exp = o[routes, dest_c]
        y = jnp.where(keep[:, None], y_exp, xf)
        out = y * prob_max[:, None]
        return out.reshape(B, S, D)
    h = _L0_tok_ref(x, L0_tok_W, L0_tok_b)
    h = jnp.concatenate([jnp.broadcast_to(cls_tok, (h.shape[0], 1, h.shape[2])), h], axis=1)
    h = h + _L0_attn_ref(_layernorm(h, axis=-1), L0_attn_W_in, L0_attn_conv_w, L0_attn_conv_b, L0_attn_W_x, L0_attn_W_dt, L0_attn_b_dt, L0_attn_A_log, L0_attn_D, L0_attn_W_out, L0_attn_gamma, L0_attn_beta)
    h = h + _L0_ffn_ref(_layernorm(h, axis=-1), L0_ffn_switch_w, L0_ffn_switch_b, L0_ffn_w1, L0_ffn_b1, L0_ffn_w2, L0_ffn_b2)
    return h

_drawn_inputs = setup_inputs


def setup_inputs(seed=0):
    import zlib

    import numpy as np

    out = dict(_drawn_inputs(seed))
    spreads = {'L0_attn_conv_b': (0.0, 0.1),
     'L0_attn_b_dt': (0.0, 0.8),
     'L0_attn_D': (1.0, 0.2),
     'L0_attn_gamma': (1.0, 0.2),
     'L0_attn_beta': (0.0, 0.1),
     'L0_ffn_switch_b': (0.0, 0.1),
     'L0_ffn_b1': (0.0, 0.8),
     'L0_ffn_b2': (0.0, 0.513)}
    factors = {'L0_attn_W_x': 8.0,
     'L0_attn_W_dt': 8.0,
     'L0_attn_A_log': 8.0,
     'L0_ffn_w1': 4.463,
     'L0_ffn_w2': 4.129}
    for name, (base, spread) in spreads.items():
        noise = np.random.default_rng([zlib.crc32(name.encode()), seed]).standard_normal(out[name].shape)
        drawn = base * np.exp(spread * noise) if base else spread * noise
        out[name] = jnp.asarray(drawn.astype(out[name].dtype))
    for name, factor in factors.items():
        out[name] = (out[name] * factor).astype(out[name].dtype)
    return out
```

```python
from contextlib import ExitStack

import concourse.bass as bass
from concourse import mybir

F32 = mybir.dt.float32
I32 = mybir.dt.int32
U32 = mybir.dt.uint32
ALU = mybir.AluOpType
ACT = mybir.ActivationFunctionType
AX = mybir.AxisListType
ds = bass.ds

P = 128
IMAGES = 64
PAIRS = IMAGES // 2
PATCHES = 196
L = PATCHES + 1
TOK = IMAGES * L
N2 = 2 * L
H0 = 99
HSTEP = L - H0
DIM = 192
DLO = DIM - P
PD = 768
KP = PD // P
INNER = 384
MB = INNER // P
NS = 16
NQ = 4
SQ = NS // NQ
UNITS = NQ * MB
UF = SQ * N2
TAPS = 4
E = 8
FF = 768
KF = FF // P
CAP = int(1.25 * TOK / E)
COLS = 2 * IMAGES
TS = 256
TILES = TOK // TS + E
SLOTS = TILES * TS
GRING = 4
FULL = TILES // GRING * GRING
SC = SLOTS // P
NOBODY = 1 << 15
BISECT = 29
EPS = 1e-5
A_BUFS, B_BUFS = 3, 4
POOL_SET = 8 + 2 * GRING


def need(eng, sem, count):
    if not isinstance(count, int) or count > 0:
        eng.wait_ge(sem, count)


def build(nc, x, cls_tok, tok_w, tok_b, w_inx, w_zlo, w_zhi, conv_w, conv_b, w_x, w_dt, b_dt, a_log, d_skip, w_out, gamma,
          beta, sw_w, sw_b, w_pack, w1_hi, b2, out):
    rows_dram = nc.dram_tensor("rows_scratch", (TOK, 2 * DIM), F32, kind="Internal").ap()
    bc_dram = nc.dram_tensor("bc_scratch", (2, 2 * NS, N2), F32, kind="Internal").ap()
    slot_dram = nc.dram_tensor("slot_scratch", (SLOTS, 1), I32, kind="Internal").ap()
    gate_dram = nc.dram_tensor("gate_scratch", (TOK, 2), F32, kind="Internal").ap()

    with ExitStack() as ctx:
        def sb(name, shape, dt=F32):
            return ctx.enter_context(nc.sbuf_tensor(name, shape, dt))

        def sem(name):
            return ctx.enter_context(nc.semaphore(name))

        ident = sb("ident", [P, P])
        wtok = sb("wtok", [P, KP, DIM])
        v_lo = sb("v_lo", [P, TAPS, INNER])
        v_hi = sb("v_hi", [P, 2, INNER])
        wz_lo = sb("wz_lo", [P, INNER])
        wz_hi = sb("wz_hi", [DLO, INNER])
        wx = sb("wx", [P, MB, 2 * NS])
        wdt = sb("wdt", [P, MB, INNER])
        wout = sb("wout", [P, MB, DIM])
        cb = sb("cb", [P, MB])
        bdt = sb("bdt", [P, MB])
        dsk = sb("dsk", [P, MB])
        neg_a = sb("neg_a", [P, MB, NS])
        tok_bias = sb("tok_bias", [H0, 2, DIM])
        gam = sb("gam", [H0, DIM])
        bet = sb("bet", [H0, DIM])
        sww_lo = sb("sww_lo", [P, E])
        sww_hi = sb("sww_hi", [DLO, E])
        swb = sb("swb", [H0, E])
        minus_half = sb("minus_half", [P, 4])
        logits = sb("logits", [H0, COLS, E])

        arena = sb("arena", [P, 42500])
        at = [0]

        def carve(parts, *shape):
            n = 1
            for k in shape:
                n *= k
            v = arena[0:parts, at[0]:at[0] + n]
            at[0] += n + n % 2
            if len(shape) == 2:
                v = v.rearrange("p (a b) -> p a b", a=shape[0])
            elif len(shape) == 3:
                v = v.rearrange("p (a b c) -> p a b c", a=shape[0], b=shape[1])
            elif len(shape) == 4:
                v = v.rearrange("p (a b c d) -> p a b c d", a=shape[0], b=shape[1], c=shape[2])
            return v

        patches = carve(P, KP, 2, L)
        h = [carve(H0, 4, DIM) for _ in range(2)]
        hn = carve(H0, 4, DIM)
        hres = carve(H0, 4, DIM)
        t_lo = carve(P, 2, L + 3)
        t_hi = carve(P, 2, L + 3)
        xz = [carve(P, 2 * MB, N2) for _ in range(2)]
        spv = carve(P, MB, N2)
        spe = carve(P, MB, N2)
        spt = carve(P, MB, N2)
        delta = [carve(P, MB, N2) for _ in range(2)]
        du = [carve(P, MB, N2) for _ in range(2)]
        bct = carve(2 * NS, N2)
        y = carve(P, MB, N2)
        decay = [carve(P, SQ, 2, L) for _ in range(A_BUFS)]
        hb_at = at[0]
        hb = [carve(P, SQ, N2) for _ in range(B_BUFS)]
        bcq = [carve(P, 2, SQ, N2) for _ in range(2)]
        rows = [carve(H0, 4, 2 * DIM) for _ in range(2)]
        h2_lo = carve(P, 4, H0)
        h2_hi = carve(DLO, 4, H0)
        st1, st2, st3 = (carve(H0, 4, 6) for _ in range(3))
        mv1, mv2, mv3 = (carve(H0, 4, 2) for _ in range(3))
        rs1, rs2, rs3 = (carve(H0, 4) for _ in range(3))
        raw_taps = arena[:, hb_at:hb_at + TAPS * MB * INNER].rearrange("p (t k n) -> p t k n", t=TAPS, k=MB)
        raw_win = y.rearrange("p a b -> p (a b)")[:, 0:MB * DIM].rearrange("p (k n) -> p k n", k=MB)
        a_end = at[0]

        at[0] = 0
        ex = carve(H0, COLS, E)
        oh = carve(H0, E, COLS)
        member = carve(H0, E, COLS)
        place = carve(H0, E, COLS)
        sel = carve(H0, E, COLS)
        tot = carve(H0, E, COLS)
        exv = carve(H0, COLS)
        prob = carve(H0, COLS)
        rsum = carve(H0, COLS)
        vmax = carve(H0, COLS)
        valid = carve(H0, COLS)
        destf = carve(H0, COLS)
        desti = carve(H0, COLS).bitcast(I32)
        dlo_i = carve(H0, COLS).bitcast(I32)
        dhi_i = carve(H0, COLS).bitcast(I32)
        ids = carve(H0, COLS).bitcast(I32)
        one_cols = carve(H0, COLS)
        weights8 = carve(H0, E)
        before = carve(H0, H0)
        every = carve(H0, H0)
        n_e = carve(H0, E)
        n_i = carve(H0, E).bitcast(I32)
        tiles_e = carve(H0, E)
        tile_end = carve(H0, E)
        base_e = carve(H0, E)
        lo_t, hi_t, mid_t, cnt, room = (carve(H0, E) for _ in range(5))
        lo_c, hi_c = carve(H0, E), carve(H0, E)
        gates = carve(H0, COLS, 2)
        tile_no = carve(1, TILES)
        tile_cmp = carve(1, TILES, E)
        tile_ex = carve(1, TILES).bitcast(I32)
        slot_id = carve(P, SC).bitcast(I32)
        sidx = [carve(H0, 8).bitcast(I32) for _ in range(2)]
        sval = [carve(H0, 8).bitcast(I32) for _ in range(2)]
        gidx = [carve(P, 2).bitcast(I32) for _ in range(GRING)]
        pidx = [carve(P, 2).bitcast(I32) for _ in range(2)]
        grow = [carve(P, 2, 2 * DIM) for _ in range(GRING)]
        ggate = [carve(P, 2, 2) for _ in range(GRING)]
        wp = [carve(P, FF + KF * DIM + KF) for _ in range(2)]
        w1h = [carve(DLO, FF) for _ in range(2)]
        b2r = [carve(P, DIM) for _ in range(2)]
        g_lo = [carve(P, TS) for _ in range(2)]
        g_hi = [carve(DLO, TS) for _ in range(2)]
        hid = [carve(P, KF, TS) for _ in range(2)]
        mo = [carve(P, 2, DIM) for _ in range(2)]
        mt = [carve(P, 2, DIM) for _ in range(2)]
        assert max(a_end, at[0]) <= 42500, (a_end, at[0])

        pb = [ctx.enter_context(nc.psum_tensor(f"bank{i}", [P, 512], F32)) for i in range(8)]
        ps_y = pb[0:3]
        ps_g = pb[3:5]
        ps_k = pb[5:7]
        ps_t = pb[7]

        s_const = sem("consts_landed")
        s_taps = sem("raw_taps_landed")
        s_pool0 = sem("pool_consts_set")
        s_dve0 = sem("dve_consts_set")
        s_nega = sem("neg_a_ready")
        s_clsrow = sem("class_row_landed")
        s_vmm = sem("tap_product_done")
        s_vcopy = sem("tap_copied")
        s_patch = sem("patches_landed")
        s_tokmm = sem("tok_product_done")
        s_hres = sem("residual_copied")
        s_h = sem("h_ready")
        s_st1 = sem("stats1_ready")
        s_mv1 = sem("meanvar1_ready")
        s_ve1 = sem("vareps1_ready")
        s_rs1 = sem("rstd1_ready")
        s_hn = sem("hn_ready")
        s_trf = sem("front_transposed")
        s_trf_copied = sem("front_transposes_copied")
        s_gmm = sem("front_product_done")
        s_gev = sem("front_product_copied")
        s_xz = sem("xz_ready")
        s_bcout = sem("bc_stored")
        s_bcq = [sem(f"bc_chunk_landed{i}") for i in range(2)]
        s_spa = sem("softplus_abs")
        s_spe = sem("softplus_exp")
        s_spt = sem("softplus_rounded")
        s_spc = sem("softplus_rest")
        s_spl = sem("softplus_ln")
        s_spd = sem("softplus_sum")
        s_delta = sem("delta_ready")
        s_du = sem("du_ready")
        s_a = sem("decay_ready")
        s_bx = sem("bx_ready")
        s_scan = sem("scan_done")
        s_mul = sem("hc_ready")
        s_p = sem("hc_folded")
        s_ysum = sem("state_sum_done")
        s_yev = sem("y_ready")
        s_ysz = sem("y_gated")
        s_opmm = sem("out_product_done")
        s_st2 = sem("stats2_ready")
        s_mv2 = sem("meanvar2_ready")
        s_ve2 = sem("vareps2_ready")
        s_rs2 = sem("rstd2_ready")
        s_opread = sem("out_product_read")
        s_gam = sem("gamma_applied")
        s_hbeta = sem("residual_beta_ready")
        s_h2 = sem("h2_ready")
        s_st3 = sem("stats3_ready")
        s_mv3 = sem("meanvar3_ready")
        s_ve3 = sem("vareps3_ready")
        s_rs3 = sem("rstd3_ready")
        s_rows = sem("rows_ready")
        s_stored = [sem(f"rows_stored{i}") for i in range(2)]
        s_trb = sem("back_transposed")
        s_trb_copied = sem("back_transposes_copied")
        s_lgmm = sem("logits_product_done")
        s_lg = sem("logits_ready")
        s_d = sem("dve_step")
        s_exin = sem("router_shifted")
        s_exout = sem("router_exp_ready")
        s_ohr = sem("route_ready")
        s_ranked = sem("rank_products_done")
        s_tie = sem("ties_ready")
        s_cnt = sem("bisect_counts_ready")
        s_bis = sem("bisect_totals_ready")
        s_fill = sem("slots_cleared")
        s_dest = [sem(f"slot_batch_ready{i}") for i in range(2)]
        s_scat = [sem(f"slot_ids_scattered{i}") for i in range(2)]
        s_tex = sem("tile_experts_ready")
        s_slot = sem("slot_ids_landed")
        s_gate = sem("gates_ready")
        s_gated = sem("gates_stored")
        s_w = [sem(f"expert_weights_landed{i}") for i in range(2)]
        s_gidx0 = sem("first_gather_ids_ready")
        s_gidx = [sem(f"gather_ids_ready{i}") for i in range(GRING)]
        s_gat = [sem(f"rows_gathered{i}") for i in range(GRING)]
        s_mtr = sem("tile_transposed")
        s_mtc = sem("tile_transposes_copied")
        s_m1 = sem("hidden_product_done")
        s_hid = sem("hidden_ready")
        s_m2 = sem("expert_product_done")
        s_keepx = sem("kept_input_ready")
        s_mbias = sem("expert_bias_added")
        s_mo = [sem(f"tile_rows_ready{i}") for i in range(GRING)]
        s_put = [sem(f"tile_rows_stored{i}") for i in range(2)]

        CLEAR = 5

        block = ctx.enter_context(nc.Block())

        @block.sync
        def _(sp):
            for dst, src in (
                (wtok[:, :, :], tok_w), (wz_lo[:, :], w_zlo), (wz_hi[:, :], w_zhi), (wx[:, :, :], w_x), (wdt[:, :, :], w_dt),
                (wout[:, :, :], w_out), (cb[:, :], conv_b), (bdt[:, :], b_dt), (dsk[:, :], d_skip), (neg_a[:, :, :], a_log),
                (tok_bias[:, 0, :], tok_b.partition_broadcast(H0)), (tok_bias[:, 1, :], tok_b.partition_broadcast(H0)),
                (gam[:, :], gamma.partition_broadcast(H0)), (bet[:, :], beta.partition_broadcast(H0)),
                (sww_lo[:, :], sw_w[0:P, :]), (sww_hi[:, :], sw_w[P:DIM, :]), (swb[:, :], sw_b.partition_broadcast(H0)),
            ):
                sp.dma_start(dst, src).then_inc(s_const, 16)
            sp.dma_start(raw_taps, conv_w).then_inc(s_taps, 16)
            sp.dma_start(raw_win, w_inx).then_inc(s_taps, 16)
            sp.wait_ge(s_const, 16 * 17)
            sp.dma_start(tok_bias[0:1, 0, :], cls_tok).then_inc(s_clsrow, 16)

            def load_patches(n):
                need(sp, s_tokmm, 2 * n)
                sp.dma_start(patches[:, :, :, 1:L], x[ds(n, 1)].rearrange("o p k b n -> (o p) k b n")
                             if not isinstance(n, int) else x[n]).then_inc(s_patch, 16)

            def load_bc(n, r, q):
                b = q % 2
                need(sp, s_bx, UNITS * n + MB * (q - 1))
                need(sp, s_mul, UNITS * n + MB * (q - 1))
                src = bc_dram[r].rearrange("(w s) t -> w (s t)", w=2)[:, q * UF:(q + 1) * UF]
                sp.dma_start(bcq[b].rearrange("p w s t -> p w (s t)"), src.partition_broadcast(P)).then_inc(s_bcq[b], 16)

            def store_bc(n, r):
                need(sp, s_bcq[0], 32 * n)
                need(sp, s_bcq[1], 32 * n)
                sp.wait_ge(s_gev, 10 * n + 7)
                sp.dma_start(bc_dram[r], bct).then_inc(s_bcout, 16)
                sp.wait_ge(s_bcout, 16 * (n + 1))

            def store_rows(n, r):
                sp.wait_ge(s_rows, n + 1)
                t = rows_dram[ds(n * N2, N2), :].rearrange("(b t) d -> t b d", b=2)
                v = rows[r].rearrange("p (b f) d -> p b f d", f=2)
                sp.dma_start(t[0:H0], v[:, :, 0, :]).then_inc(s_stored[r], 16)
                sp.dma_start(t[H0:L], v[1:H0, :, 1, :]).then_inc(s_stored[r], 16)

            def body(i, r, front, tok):
                if tok:
                    load_patches(i + 2)
                load_bc(i, r, 2)
                load_bc(i, r, 3)
                if not isinstance(i, int) or i >= 1:
                    store_rows(i - 1, 1 - r)
                if front:
                    store_bc(i + 1, 1 - r)
                    load_bc(i + 1, 1 - r, 0)
                    load_bc(i + 1, 1 - r, 1)

            sp.wait_ge(s_dve0, 1)
            load_patches(0)
            load_patches(1)
            store_bc(0, 0)
            load_bc(0, 0, 0)
            load_bc(0, 0, 1)
            for i in range(4):
                body(i, i % 2, True, True)
            with sp.Fori(4, PAIRS - 3, 2) as i:
                body(i, 0, True, True)
                body(i + 1, 1, True, True)
            body(PAIRS - 2, 0, True, False)
            body(PAIRS - 1, 1, False, False)
            store_rows(PAIRS - 1, 1)

            for b in range(2):
                sp.wait_ge(s_scat[b], 16 * COLS // 2)
            sp.wait_ge(s_fill, 16)
            sp.dma_start(slot_id, slot_dram.rearrange("(p c) o -> p (c o)", p=P)).then_inc(s_slot, 16)

            def load_expert(k, r):
                need(sp, s_m2, 2 * (k - 1))
                need(sp, s_mbias, k - 1)
                e = sp.value_load(tile_ex[0:1, ds(k, 1)], min_val=0, max_val=E - 1)
                sp.dma_start(wp[r], w_pack[ds(e, 1)].rearrange("o p n -> (o p) n")).then_inc(s_w[r], 16)
                sp.dma_start(w1h[r], w1_hi[ds(e, 1)].rearrange("o p n -> (o p) n")).then_inc(s_w[r], 16)
                sp.dma_start(b2r[r], b2[ds(e, 1), :].rearrange("o n -> (o n)").partition_broadcast(P)).then_inc(s_w[r], 16)

            sp.wait_ge(s_tex, 1)
            load_expert(0, 0)
            load_expert(1, 1)

            def gates_out():
                sp.wait_ge(s_gate, 1)
                g = gate_dram.rearrange("(b t) w -> t b w", t=L)
                v = gates.rearrange("p (b f) w -> p b f w", f=2)
                sp.dma_start(g[0:H0], v[:, :, 0, :]).then_inc(s_gated, 16)
                sp.dma_start(g[H0:L], v[1:H0, :, 1, :]).then_inc(s_gated, 16)

            gates_out()
            with sp.Fori(2, TILES - 2, 2) as k:
                load_expert(k, 0)
                load_expert(k + 1, 1)
            load_expert(TILES - 1, 0)
            for r in range(2):
                sp.wait_ge(s_stored[r], 16 * PAIRS)
                sp.wait_ge(s_put[r], 32 * ((TILES + 1 - r) // 2))
            sp.wait_ge(s_gated, 32)

        @block.gpsimd
        def _(pool):
            pool.memset(ident[:, :], 0.0).then_inc(s_pool0, 1)
            pool.memset(minus_half[:, :], -0.5).then_inc(s_pool0, 1)
            pool.wait_ge(s_pool0, 2)
            pool.affine_select(out=ident[:, :], in_=ident[:, :], compare_op=ALU.not_equal, fill=1.0, base=0,
                               pattern=[[-1, P]], channel_multiplier=1).then_inc(s_pool0, 1)

            def rstd(n, s_in, mv, rs, s_out):
                pool.wait_ge(s_in, n + 1)
                pool.tensor_tensor(rs[:, :], mv[:, :, 1], minus_half[0:H0, :], ALU.pow).then_inc(s_out, 1)

            def bx(n, r, j):
                q, m, b = j // MB, j % MB, j % B_BUFS
                if j == 0:
                    pool.wait_ge(s_du, n + 1)
                if m == 0:
                    pool.wait_ge(s_bcq[q % 2], 16 * (2 * n + q // 2 + 1))
                need(pool, s_ysum, UNITS * n + j - B_BUFS + 1)
                u = du[r][:, m, :].unsqueeze(1).to_broadcast([P, SQ, N2])
                pool.tensor_tensor(hb[b][:, :, :], u, bcq[q % 2][:, 0, :, :], ALU.mult).then_inc(s_bx, 1)

            def gate_y(n, r):
                pool.wait_ge(s_yev, MB * (n + 1))
                pool.tensor_tensor(y[:, :, :], y[:, :, :], xz[r][:, MB:2 * MB, :], ALU.mult).then_inc(s_ysz, 1)

            def add_beta(n):
                pool.wait_ge(s_hres, n + 1)
                pool.tensor_tensor(hres[:, :, :], hres[:, :, :], bet[:, :].unsqueeze(1).to_broadcast([H0, 4, DIM]),
                                   ALU.add).then_inc(s_hbeta, 1)

            def add_residual(n, r):
                need(pool, s_stored[r], 16 * (n - r))
                pool.wait_ge(s_gam, n + 1)
                pool.wait_ge(s_hbeta, n + 1)
                pool.tensor_tensor(rows[r][:, :, 0:DIM], rows[r][:, :, 0:DIM], hres[:, :, :], ALU.add).then_inc(s_h2, 1)

            def softplus_rest(n):
                pool.wait_ge(s_spt, n + 1)
                pool.tensor_tensor(spt[:, :, :], spe[:, :, :], spt[:, :, :], ALU.subtract).then_inc(s_spc, 1)

            def make_delta(n, r):
                pool.wait_ge(s_spd, n + 1)
                pool.wait_ge(s_spc, n + 1)
                need(pool, s_a, UNITS * (n - 1))
                pool.tensor_tensor(delta[r][:, :, :], spv[:, :, :], spt[:, :, :], ALU.add).then_inc(s_delta, 1)
                pool.wait_ge(s_delta, n + 1)
                need(pool, s_bx, UNITS * (n - 1))
                pool.tensor_tensor(du[r][:, :, :], delta[r][:, :, :], xz[r][:, 0:MB, :], ALU.mult).then_inc(s_du, 1)

            def body(i, r, front):
                back = not isinstance(i, int) or i >= 1
                for j in range(UNITS):
                    bx(i, r, j)
                    if back and j == 1:
                        add_beta(i - 1)
                    if front and j == 2:
                        rstd(i + 1, s_ve1, mv1, rs1, s_rs1)
                    if back and j == 4:
                        gate_y(i - 1, 1 - r)
                    if back and j == 6:
                        rstd(i - 1, s_ve2, mv2, rs2, s_rs2)
                    if back and j == 7:
                        add_residual(i - 1, 1 - r)
                    if back and j == 9:
                        rstd(i - 1, s_ve3, mv3, rs3, s_rs3)
                if front:
                    softplus_rest(i + 1)
                    make_delta(i + 1, 1 - r)

            pool.wait_ge(s_dve0, CLEAR)
            rstd(0, s_ve1, mv1, rs1, s_rs1)
            softplus_rest(0)
            make_delta(0, 0)
            for i in range(4):
                body(i, i % 2, True)
            with pool.Fori(4, PAIRS - 3, 2) as i:
                body(i, 0, True)
                body(i + 1, 1, True)
            body(PAIRS - 2, 0, True)
            body(PAIRS - 1, 1, False)
            n = PAIRS - 1
            add_beta(n)
            gate_y(n, 1)
            rstd(n, s_ve2, mv2, rs2, s_rs2)
            add_residual(n, 1)
            rstd(n, s_ve3, mv3, rs3, s_rs3)

            pool.wait_ge(s_stored[0], 16 * PAIRS)
            pool.wait_ge(s_stored[1], 16 * PAIRS)
            pool.wait_ge(s_lg, PAIRS)
            pool.memset(before, 1.0).then_inc(s_pool0, 1)
            pool.memset(every, 1.0).then_inc(s_pool0, 1)
            pool.memset(valid, 1.0).then_inc(s_pool0, 1)
            pool.memset(one_cols, 1.0).then_inc(s_pool0, 1)
            pool.iota(slot_id, [[0, SC]], base=NOBODY, channel_multiplier=0).then_inc(s_pool0, 1)
            pool.iota(ids.rearrange("p (b f) -> p b f", f=2), [[L, IMAGES], [HSTEP, 2]], base=0,
                      channel_multiplier=1).then_inc(s_pool0, 1)
            pool.iota(weights8, [[-1, E]], base=E, channel_multiplier=0,
                      allow_small_or_imprecise_dtypes=True).then_inc(s_pool0, 1)
            pool.iota(tile_no, [[1, TILES]], base=0, channel_multiplier=0,
                      allow_small_or_imprecise_dtypes=True).then_inc(s_pool0, 1)
            for r in range(GRING):
                pool.memset(grow[r], 0.0).then_inc(s_pool0, 1)
                pool.memset(ggate[r], 0.0).then_inc(s_pool0, 1)
            pool.wait_ge(s_pool0, 3 + POOL_SET)
            pool.affine_select(out=before, in_=before, compare_op=ALU.is_gt, fill=0.0, base=0, pattern=[[1, H0]],
                               channel_multiplier=-1).then_inc(s_pool0, 1)
            pool.affine_select(out=valid.rearrange("p (b f) -> p b f", f=2), in_=valid.rearrange("p (b f) -> p b f", f=2),
                               compare_op=ALU.is_ge, fill=0.0, base=0, pattern=[[0, IMAGES], [-1, 2]],
                               channel_multiplier=2).then_inc(s_pool0, 1)
            pool.dma_start(slot_dram.rearrange("(p c) o -> p (c o)", p=P), slot_id).then_inc(s_fill, 16)

            last_slot, last_token = pool.to_reg(SLOTS - 1), pool.to_reg(TOK - 1)

            def scatter(u, r):
                pool.wait_ge(s_fill, 16)
                pool.wait_ge(s_dest[r], u)
                for c in range(8):
                    pool.indirect_dma_start(
                        out=slot_dram, out_offset=bass.IndirectOffsetOnAxis(ap=sidx[r][:, c:c + 1].bitcast(U32), axis=0),
                        in_=sval[r][:, c:c + 1], in_offset=None, bounds_check=last_slot, oob_is_err=False,
                    ).then_inc(s_scat[r], 16)

            with pool.Fori(1, COLS // 16 + 1, 1) as u:
                scatter(u, 0)
                scatter(u, 1)

            def gather(g, u):
                pool.wait_ge(s_gated, 32)
                if isinstance(u, int) and u == 0:
                    pool.wait_ge(s_gidx0, g + 1)
                else:
                    pool.wait_ge(s_gidx[g], u)
                for f in range(2):
                    i = bass.IndirectOffsetOnAxis(ap=gidx[g][:, f:f + 1].bitcast(U32), axis=0)
                    pool.indirect_dma_start(out=grow[g][:, f, :], out_offset=None, in_=rows_dram, in_offset=i,
                                            bounds_check=last_token, oob_is_err=False).then_inc(s_gat[g], 16)
                    pool.indirect_dma_start(out=ggate[g][:, f, :], out_offset=None, in_=gate_dram, in_offset=i,
                                            bounds_check=last_token, oob_is_err=False).then_inc(s_gat[g], 16)

            def put(g, u):
                r = g % 2
                pool.wait_ge(s_gated, 32)
                pool.wait_ge(s_mo[g], u)
                for f in range(2):
                    pool.indirect_dma_start(
                        out=out, out_offset=bass.IndirectOffsetOnAxis(ap=pidx[r][:, f:f + 1].bitcast(U32), axis=0),
                        in_=mo[r][:, f, :], in_offset=None, bounds_check=last_token, oob_is_err=False,
                    ).then_inc(s_put[r], 16)

            for g in range(GRING):
                gather(g, 0)
            with pool.Fori(1, TILES // GRING, 1) as u:
                for g in range(GRING):
                    put(g, u)
                    gather(g, u)
            for t in range(FULL - GRING, TILES):
                put(t % GRING, t // GRING + 1)
                if t + GRING < TILES:
                    gather(t % GRING, t // GRING + 1)

        @block.scalar
        def _(act):
            act.wait_ge(s_const, 16 * 17)
            act.activation(neg_a[:, :, :], neg_a[:, :, :], ACT.Exp).then_inc(s_nega, 1)
            act.wait_ge(s_nega, 1)
            act.activation(neg_a[:, :, :], neg_a[:, :, :], ACT.Copy, scale=-1.0).then_inc(s_nega, 1)

            def decays(n, r, j):
                q, m, b = j // MB, j % MB, j % A_BUFS
                if j == 0:
                    act.wait_ge(s_delta, n + 1)
                need(act, s_scan, UNITS * n + j - A_BUFS + 1)
                d = delta[r][:, m, :].rearrange("p (b t) -> p b t", b=2)[:, :, 1:L]
                for s in range(SQ):
                    ins = act.activation(decay[b][:, s, :, 1:L], d, ACT.Exp, scale=neg_a[:, m, q * SQ + s:q * SQ + s + 1])
                ins.then_inc(s_a, 1)

            def copy_residual(n, r):
                need(act, s_h2, n)
                act.wait_ge(s_h, n + 1)
                act.activation(hres[:, :, :], h[r][:, :, :], ACT.Copy).then_inc(s_hres, 1)

            def copy_front_t(n, b):
                act.wait_ge(s_trf, 2 * n + b + 1)
                if b == 0:
                    need(act, s_gmm, 10 * n)
                act.activation(t_lo[:, b, 1:L + 1], ps_t[:, 0:L], ACT.Copy)
                act.activation(t_hi[0:DLO, b, 1:L + 1], ps_t[0:DLO, L + 1:2 * L + 1], ACT.Copy)
                act.activation(t_hi[DLO:P, b, 0:L], ps_t[0:DLO, L + 1:2 * L + 1], ACT.Copy).then_inc(s_trf_copied, 1)

            def copy_product(n, r, t):
                act.wait_ge(s_gmm, 10 * n + t + 1)
                src = ps_g[t % 2][:, 0:N2]
                if t < MB:
                    if t == 0:
                        need(act, s_ysz, n - 1)
                        need(act, s_du, n - 1)
                    ins = act.activation(xz[r][:, t, :], src, ACT.Identity, bias=cb[:, t:t + 1])
                elif t < 2 * MB:
                    ins = act.activation(xz[r][:, t, :], src, ACT.Copy)
                elif t == 6:
                    need(act, s_bcout, 16 * n)
                    ins = act.activation(bct, ps_g[t % 2][0:2 * NS, 0:N2], ACT.Copy)
                else:
                    if t == 7:
                        need(act, s_delta, n)
                    ins = act.activation(spv[:, t - 7, :], src, ACT.Identity, bias=bdt[:, t - 7:t - 6])
                ins.then_inc(s_gev, 1)

            def silu(n, r):
                act.wait_ge(s_gev, 10 * n + 6)
                act.activation(xz[r][:, :, :], xz[r][:, :, :], ACT.Silu).then_inc(s_xz, 1)

            def softplus_a(n):
                act.wait_ge(s_gev, 10 * n + 10)
                act.activation(spe[:, :, :], spv[:, :, :], ACT.Abs).then_inc(s_spa, 1)
                act.wait_ge(s_spa, n + 1)
                act.activation(spe[:, :, :], spe[:, :, :], ACT.Exp, scale=-1.0).then_inc(s_spe, 1)

            def softplus_b(n):
                act.wait_ge(s_spc, n + 1)
                act.activation(spe[:, :, :], spe[:, :, :], ACT.Ln, bias=1.0).then_inc(s_spl, 1)

            def copy_back_t(n, b):
                act.wait_ge(s_trb, 2 * n + b + 1)
                if b == 0:
                    need(act, s_lgmm, n)
                act.activation(h2_lo[:, 2 * b:2 * b + 2, :], ps_t[:, 0:2 * H0], ACT.Copy)
                act.activation(h2_hi[:, 2 * b:2 * b + 2, :], ps_t[0:DLO, 2 * H0:4 * H0], ACT.Copy).then_inc(s_trb_copied, 1)

            def body(i, r, front):
                back = not isinstance(i, int) or i >= 1
                o = 1 - r
                for j in range(UNITS):
                    decays(i, r, j)
                    if back and j == 0:
                        copy_residual(i - 1, o)
                    if front:
                        if j == 4:
                            copy_front_t(i + 1, 0)
                            copy_front_t(i + 1, 1)
                        for t in {5: (0,), 6: (1,), 7: (2, 3), 8: (4, 5), 10: (6, 7), 11: (8, 9)}.get(j, ()):
                            copy_product(i + 1, o, t)
                        if j == 8:
                            silu(i + 1, o)
                    if back and j == 11:
                        copy_back_t(i - 1, 0)
                        copy_back_t(i - 1, 1)
                if front:
                    softplus_a(i + 1)
                    softplus_b(i + 1)

            act.wait_ge(s_dve0, CLEAR)
            copy_front_t(0, 0)
            copy_front_t(0, 1)
            for t in range(10):
                if t == 6:
                    silu(0, 0)
                copy_product(0, 0, t)
            softplus_a(0)
            softplus_b(0)
            for i in range(4):
                body(i, i % 2, True)
            with act.Fori(4, PAIRS - 3, 2) as i:
                body(i, 0, True)
                body(i + 1, 1, True)
            body(PAIRS - 2, 0, True)
            body(PAIRS - 1, 1, False)
            copy_residual(PAIRS - 1, 1)
            copy_back_t(PAIRS - 1, 0)
            copy_back_t(PAIRS - 1, 1)

            act.wait_ge(s_exin, 1)
            act.activation(ex, ex, ACT.Exp).then_inc(s_exout, 1)

            def tile_copies(k, r):
                act.wait_ge(s_mtr, k + 1)
                need(act, s_m1, KF * (k - 1))
                act.activation(g_lo[r], ps_t[:, 0:TS], ACT.Copy)
                act.activation(g_hi[r], ps_t[0:DLO, TS:2 * TS], ACT.Copy).then_inc(s_mtc, 1)

            def gelus(k, r):
                b1 = wp[r][:, FF + KF * DIM:]
                need(act, s_m2, 2 * (k - 1))
                for f in range(KF):
                    act.wait_ge(s_m1, KF * k + f + 1)
                    act.activation(hid[r][:, f, :], (ps_y + ps_g[0:1])[f % 4][:, 0:TS], ACT.Gelu,
                                   bias=b1[:, f:f + 1]).then_inc(s_hid, 1)

            tile_copies(0, 0)
            for k in range(2):
                gelus(k, k)
                tile_copies(k + 1, 1 - k)
            with act.Fori(2, TILES - 2, 2) as k:
                gelus(k, 0)
                tile_copies(k + 1, 1)
                gelus(k + 1, 1)
                tile_copies(k + 2, 0)
            gelus(TILES - 1, 0)

        @block.tensor
        def _(pe):
            pe.wait_ge(s_taps, 32)
            n = 0
            for k in range(TAPS):
                for lo, m in ((0, P), (P, DLO)):
                    need(pe, s_vcopy, n - 1)
                    for c in range(MB):
                        mm = pe.matmul(ps_g[n % 2][0:m, 0:INNER], raw_win[:, c, lo:lo + m], raw_taps[:, k, c, :],
                                       start=(c == 0), stop=(c == MB - 1))
                    mm.then_inc(s_vmm, 1)
                    n += 1
            VPROD = n

            def tok(n, b):
                if b == 0:
                    pe.wait_ge(s_patch, 16 * (n + 1))
                    need(pe, s_h, n)
                    need(pe, s_opread, n - 2)
                for f in range(2):
                    for c in range(KP):
                        mm = pe.matmul(ps_k[b][0:H0, f * DIM:(f + 1) * DIM], patches[:, c, b, f * HSTEP:f * HSTEP + H0],
                                       wtok[:, c, :], start=(c == 0), stop=(c == KP - 1))
                mm.then_inc(s_tokmm, 1)

            def front_t(n, b):
                if b == 0:
                    pe.wait_ge(s_hn, n + 1)
                    need(pe, s_trb_copied, 2 * (n - 2))
                need(pe, s_trf_copied, 2 * n + b)
                for f in (1, 0):
                    c = f * HSTEP
                    pe.transpose(ps_t[:, c:c + H0], hn[:, 2 * b + f, 0:P], ident[0:H0, 0:H0])
                    mm = pe.transpose(ps_t[0:DLO, L + 1 + c:L + 1 + c + H0], hn[:, 2 * b + f, P:DIM], ident[0:H0, 0:H0])
                mm.then_inc(s_trf, 1)

            def product(n, r, t):
                o = ps_g[t % 2]
                if t == 0:
                    pe.wait_ge(s_trf_copied, 2 * (n + 1))
                    need(pe, s_lg, n - 2)
                if t == 6:
                    pe.wait_ge(s_xz, n + 1)
                need(pe, s_gev, 10 * n + t - 1)
                if t < MB:
                    c = slice(t * P, (t + 1) * P)
                    for k in range(TAPS):
                        pe.matmul(o[:, 0:N2], v_lo[:, k, c], t_lo[:, :, k:k + L], start=(k == 0), stop=False)
                    for k in range(2):
                        mm = pe.matmul(o[:, 0:N2], v_hi[:, k, c], t_hi[:, :, 2 * k:2 * k + L], start=False, stop=(k == 1))
                elif t < 2 * MB:
                    c = slice((t - MB) * P, (t - MB + 1) * P)
                    pe.matmul(o[:, 0:N2], wz_lo[:, c], t_lo[:, :, 1:L + 1], start=True, stop=False)
                    mm = pe.matmul(o[:, 0:N2], wz_hi[:, c], t_hi[0:DLO, :, 1:L + 1], start=False, stop=True)
                elif t == 6:
                    for k in range(MB):
                        mm = pe.matmul(o[0:2 * NS, 0:N2], wx[:, k, :], xz[r][:, k, :], start=(k == 0), stop=(k == MB - 1))
                else:
                    for k in range(MB):
                        mm = pe.matmul(o[:, 0:N2], wdt[:, k, (t - 7) * P:(t - 6) * P], xz[r][:, k, :],
                                       start=(k == 0), stop=(k == MB - 1))
                mm.then_inc(s_gmm, 1)

            def state_sum(n, j):
                q, m, b = j // MB, j % MB, j % B_BUFS
                if q == 0:
                    need(pe, s_yev, MB * (n - 1) + m + 1)
                pe.wait_ge(s_p, UNITS * n + j + 1)
                for s in range(SQ // 2):
                    mm = pe.matmul(ps_y[m][:, 0:N2], ident[:, :], hb[b][:, s, :], start=(q == 0 and s == 0),
                                   stop=(q == NQ - 1 and s == SQ // 2 - 1))
                mm.then_inc(s_ysum, 1)

            def out_product(n, b):
                if b == 0:
                    pe.wait_ge(s_ysz, n + 1)
                    pe.wait_ge(s_h, min(n + 3, PAIRS) if isinstance(n, int) else n + 3)
                    need(pe, s_opread, n)
                for f in range(2):
                    c = b * L + f * HSTEP
                    for k in range(MB):
                        mm = pe.matmul(ps_k[b][0:H0, f * DIM:(f + 1) * DIM], y[:, k, c:c + H0], wout[:, k, :],
                                       start=(k == 0), stop=(k == MB - 1))
                mm.then_inc(s_opmm, 1)

            def back_t(n, b):
                if b == 0:
                    pe.wait_ge(s_rows, n + 1)
                    pe.wait_ge(s_trf_copied, min(2 * (n + 3), 2 * PAIRS) if isinstance(n, int) else 2 * (n + 3))
                need(pe, s_trb_copied, 2 * n + b)
                for f in range(2):
                    src = rows[n_par(n)][:, 2 * b + f, DIM:2 * DIM]
                    pe.transpose(ps_t[:, f * H0:(f + 1) * H0], src[:, 0:P], ident[0:H0, 0:H0])
                    mm = pe.transpose(ps_t[0:DLO, (2 + f) * H0:(3 + f) * H0], src[:, P:DIM], ident[0:H0, 0:H0])
                mm.then_inc(s_trb, 1)

            par = [0]

            def n_par(n):
                return par[0]

            def router(n):
                pe.wait_ge(s_trb_copied, 2 * (n + 1))
                pe.wait_ge(s_gev, min(10 * (n + 3), 10 * PAIRS) if isinstance(n, int) else 10 * (n + 3))
                need(pe, s_lg, n)
                for c in range(4):
                    o = ps_g[0][0:H0, c * E:(c + 1) * E]
                    pe.matmul(o, h2_lo[:, c, :], sww_lo[:, :], start=True, stop=False)
                    mm = pe.matmul(o, h2_hi[:, c, :], sww_hi[:, :], start=False, stop=True)
                mm.then_inc(s_lgmm, 1)

            def body(i, r, front, tokens):
                back = not isinstance(i, int) or i >= 1
                o = 1 - r
                par[0] = o
                for j in range(UNITS):
                    if j:
                        state_sum(i, j - 1)
                    elif back:
                        state_sum(i - 1, UNITS - 1)
                    if back and j == 3:
                        out_product(i - 1, 0)
                        out_product(i - 1, 1)
                    if front:
                        if j == 3:
                            front_t(i + 1, 0)
                            front_t(i + 1, 1)
                        for t in {4: (0,), 5: (1,), 6: (2,), 7: (3, 4, 5), 9: (6, 7), 10: (8, 9)}.get(j, ()):
                            product(i + 1, o, t)
                    if tokens and j == 8:
                        tok(i + 2, 0)
                    if tokens and j == 9:
                        tok(i + 2, 1)
                    if back and j == 11:
                        back_t(i - 1, 0)
                        back_t(i - 1, 1)
                        router(i - 1)

            pe.wait_ge(s_const, 16 * 17)
            pe.wait_ge(s_pool0, 3)
            pe.wait_ge(s_dve0, CLEAR)
            pe.wait_ge(s_vcopy, VPROD + 2)
            tok(0, 0)
            tok(0, 1)
            front_t(0, 0)
            front_t(0, 1)
            for t in range(10):
                product(0, 0, t)
            tok(1, 0)
            tok(1, 1)
            for i in range(4):
                body(i, i % 2, True, True)
            with pe.Fori(4, PAIRS - 3, 2) as i:
                body(i, 0, True, True)
                body(i + 1, 1, True, True)
            body(PAIRS - 2, 0, True, False)
            body(PAIRS - 1, 1, False, False)
            n = PAIRS - 1
            state_sum(n, UNITS - 1)
            out_product(n, 0)
            out_product(n, 1)
            par[0] = 1
            back_t(n, 0)
            back_t(n, 1)
            router(n)

            def rank(src):
                for half in range(2):
                    v = src.rearrange("p e c -> p (e c)")[:, half * 512:(half + 1) * 512]
                    pe.matmul(ps_k[half][0:H0, :], before, v, start=True, stop=True)
                    mm = pe.matmul(ps_g[half][0:H0, :], every, v, start=True, stop=True)
                mm.then_inc(s_ranked, 1)

            pe.wait_ge(s_pool0, 3 + POOL_SET + 2)
            pe.wait_ge(s_lg, PAIRS)
            pe.wait_ge(s_ohr, 1)
            rank(oh)
            with pe.Fori(0, BISECT, 1) as t:
                pe.wait_ge(s_cnt, t + 1)
                pe.matmul(ps_y[0][0:H0, 0:E], every, cnt, start=True, stop=True).then_inc(s_bis, 1)
            pe.wait_ge(s_cnt, BISECT + 1)
            pe.matmul(ps_y[0][0:H0, 0:E], every, cnt, start=True, stop=True).then_inc(s_bis, 1)
            pe.wait_ge(s_tie, 1)
            rank(sel)

            def tile_t(k, g):
                pe.wait_ge(s_gat[g], 64 * ((k - g) // GRING + 1) if isinstance(k, int) else 64 // GRING * (k - g) + 64)
                need(pe, s_mtc, k)
                for f in range(2):
                    pe.transpose(ps_t[:, f * P:(f + 1) * P], grow[g][:, f, DIM:DIM + P], ident[:, :])
                    mm = pe.transpose(ps_t[0:DLO, TS + f * P:TS + (f + 1) * P], grow[g][:, f, DIM + P:2 * DIM], ident[:, :])
                mm.then_inc(s_mtr, 1)

            def hidden(k, r):
                pe.wait_ge(s_w[r], 48 * ((k - r) // 2 + 1) if isinstance(k, int) else 24 * (k - r) + 48)
                pe.wait_ge(s_mtc, k + 1)
                for f in range(KF):
                    o = (ps_y + ps_g[0:1])[f % 4][:, 0:TS]
                    need(pe, s_hid, KF * k + f - 3)
                    c = slice(f * P, (f + 1) * P)
                    pe.matmul(o, wp[r][:, c], g_lo[r], start=True, stop=False)
                    pe.matmul(o, w1h[r][:, c], g_hi[r], start=False, stop=True).then_inc(s_m1, 1)

            def expert_out(k, r):
                w2 = wp[r][:, FF:FF + KF * DIM].rearrange("p (f d) -> p f d", f=KF)
                need(pe, s_mbias, k)
                for f in range(2):
                    for c in range(KF):
                        if f == 0:
                            pe.wait_ge(s_hid, KF * k + c + 1)
                        mm = pe.matmul(ps_k[f][:, 0:DIM], hid[r][:, c, f * P:(f + 1) * P], w2[:, c, :], start=(c == 0),
                                       stop=(c == KF - 1))
                    mm.then_inc(s_m2, 1)

            pe.wait_ge(s_gate, 1)

            def ring(k, tiles=GRING):
                for g in range(tiles):
                    hidden(k + g, g % 2)
                    if g + 1 < tiles or tiles == GRING:
                        tile_t(k + g + 1, (g + 1) % GRING)
                    expert_out(k + g, g % 2)

            tile_t(0, 0)
            ring(0)
            with pe.Fori(GRING, FULL - GRING + 1, GRING) as k:
                ring(k)
            ring(FULL, TILES - FULL)

        @block.vector
        def _(dve):
            dve.memset(patches[:, :, :, 0:1], 0.0).then_inc(s_dve0, 1)
            dve.memset(t_lo[:, :, :], 0.0).then_inc(s_dve0, 1)
            dve.memset(t_hi[:, :, :], 0.0).then_inc(s_dve0, 1)
            for b in range(A_BUFS):
                ins = dve.memset(decay[b][:, :, :, 0:1], 0.0)
            ins.then_inc(s_dve0, 1)
            n = 0
            for k in range(TAPS):
                dve.wait_ge(s_vmm, n + 1)
                dve.tensor_copy(v_lo[:, k, :], ps_g[n % 2][:, 0:INNER]).then_inc(s_vcopy, 1)
                n += 1
                dve.wait_ge(s_vmm, n + 1)
                o = v_hi[0:DLO, k // 2, :] if k % 2 == 0 else v_hi[DLO:P, k // 2, :]
                dve.tensor_copy(o, ps_g[n % 2][0:DLO, 0:INNER]).then_inc(s_vcopy, 1)
                n += 1
            dve.wait_ge(s_const, 16 * 17)
            dve.wait_ge(s_clsrow, 16)
            dve.memset(rows[0][:, :, :], 0.0).then_inc(s_vcopy, 1)
            dve.memset(rows[1][:, :, :], 0.0).then_inc(s_vcopy, 1)
            dve.tensor_copy(hn[:, 0, 0:2], tok_bias[:, 0, 0:2]).then_inc(s_dve0, 1)

            def embed(n, r):
                need(dve, s_hres, n - 1)
                for b in range(2):
                    dve.wait_ge(s_tokmm, 2 * n + b + 1)
                    ins = dve.tensor_tensor(h[r][:, 2 * b:2 * b + 2, :], ps_k[b][0:H0, 0:2 * DIM].rearrange(
                        "p (f d) -> p f d", f=2), tok_bias[:, :, :], ALU.add)
                ins.then_inc(s_h, 1)

            def stats(n, src, st, mv, s_in, s_st, s_mv, s_ve):
                if s_in is not None:
                    dve.wait_ge(s_in, n + 1)
                for c in range(4):
                    ins = dve.bn_stats(st[:, c, :], src(c))
                ins.then_inc(s_st, 1)
                dve.wait_ge(s_clsrow, 16)
                dve.wait_ge(s_st, n + 1)
                for c in range(4):
                    ins = dve.bn_aggr(mv[:, c, :], st[:, c, :])
                ins.then_inc(s_mv, 1)
                dve.wait_ge(s_mv, n + 1)
                dve.tensor_scalar(mv[:, :, 1], mv[:, :, 1], EPS, None, ALU.add).then_inc(s_ve, 1)

            def normalise(n, dst, src, mv, rs, s_rs, s_out):
                dve.wait_ge(s_rs, n + 1)
                for c in range(4):
                    ins = dve.tensor_scalar(dst(c), src(c), mv[:, c, 0:1], rs[:, c:c + 1], ALU.subtract, ALU.mult)
                ins.then_inc(s_out, 1)

            def front_stats(n, r):
                embed(n, r)
                stats(n, lambda c: h[r][:, c, :], st1, mv1, s_h, s_st1, s_mv1, s_ve1)

            def front_norm(n, r):
                need(dve, s_trf, 2 * n)
                normalise(n, lambda c: hn[:, c, :], lambda c: h[r][:, c, :], mv1, rs1, s_rs1, s_hn)

            def scan(n, j):
                b, a = j % B_BUFS, j % A_BUFS
                dve.wait_ge(s_a, UNITS * n + j + 1)
                dve.wait_ge(s_bx, UNITS * n + j + 1)
                v = hb[b].rearrange("p s t -> p (s t)")
                dve.tensor_tensor_scan(v, decay[a].rearrange("p s b t -> p (s b t)"), v, 0.0, ALU.mult,
                                       ALU.add).then_inc(s_scan, 1)

            def times_c(n, j):
                q, b = j // MB, j % B_BUFS
                dve.wait_ge(s_scan, UNITS * n + j + 1)
                dve.wait_ge(s_bcq[q % 2], 16 * (2 * n + q // 2 + 1))
                dve.tensor_tensor(hb[b][:, :, :], hb[b][:, :, :], bcq[q % 2][:, 1, :, :], ALU.mult).then_inc(s_mul, 1)

            def fold(n, j):
                b = j % B_BUFS
                dve.wait_ge(s_mul, UNITS * n + j + 1)
                dve.tensor_tensor(hb[b][:, 0:SQ // 2, :], hb[b][:, 0:SQ // 2, :], hb[b][:, SQ // 2:SQ, :],
                                  ALU.add).then_inc(s_p, 1)

            def take_y(n, r, m):
                dve.wait_ge(s_ysum, UNITS * (n + 1) - MB + m + 1)
                if m == 0:
                    need(dve, s_opmm, 2 * n)
                dve.scalar_tensor_tensor(out=y[:, m, :], in0=xz[r][:, m, :], scalar=dsk[:, m:m + 1],
                                         in1=ps_y[m][:, 0:N2], op0=ALU.mult, op1=ALU.add).then_inc(s_yev, 1)

            def o_tile(c):
                return ps_k[c // 2][0:H0, (c % 2) * DIM:(c % 2 + 1) * DIM]

            def out_stats(n):
                dve.wait_ge(s_opmm, 2 * (n + 1))
                stats(n, o_tile, st2, mv2, None, s_st2, s_mv2, s_ve2)

            def out_norm(n, r):
                need(dve, s_stored[r], 16 * (n - r))
                need(dve, s_trb, 2 * (n - 1))
                normalise(n, lambda c: rows[r][:, c, 0:DIM], o_tile, mv2, rs2, s_rs2, s_opread)
                dve.wait_ge(s_opread, n + 1)
                v = rows[r][:, :, 0:DIM]
                dve.tensor_tensor(v, v, gam[:, :].unsqueeze(1).to_broadcast([H0, 4, DIM]), ALU.mult).then_inc(s_gam, 1)

            def row_stats(n, r):
                stats(n, lambda c: rows[r][:, c, 0:DIM], st3, mv3, s_h2, s_st3, s_mv3, s_ve3)

            def row_norm(n, r):
                normalise(n, lambda c: rows[r][:, c, DIM:2 * DIM], lambda c: rows[r][:, c, 0:DIM], mv3, rs3, s_rs3, s_rows)

            def take_logits(n):
                dve.wait_ge(s_lgmm, n + 1)
                dve.tensor_tensor(logits[:, ds(4 * n, 4), :], ps_g[0][0:H0, 0:4 * E].rearrange("p (c e) -> p c e", c=4),
                                  swb[:, :].unsqueeze(1).to_broadcast([H0, 4, E]), ALU.add).then_inc(s_lg, 1)

            def softplus_t(n):
                dve.wait_ge(s_spe, n + 1)
                need(dve, s_delta, n)
                dve.tensor_scalar(spt[:, :, :], spe[:, :, :], 1.0, -1.0, ALU.add, ALU.add).then_inc(s_spt, 1)

            def softplus_sum(n):
                dve.wait_ge(s_spl, n + 1)
                dve.scalar_tensor_tensor(out=spv[:, :, :].rearrange("p a b -> p (a b)"),
                                         in0=spv[:, :, :].rearrange("p a b -> p (a b)"), scalar=0.0,
                                         in1=spe[:, :, :].rearrange("p a b -> p (a b)"), op0=ALU.max,
                                         op1=ALU.add).then_inc(s_spd, 1)

            def body(i, r, front):
                back = not isinstance(i, int) or i >= 1
                o = 1 - r
                for j in range(UNITS):
                    scan(i, j)
                    if j:
                        fold(i, j - 1)
                    elif back:
                        fold(i - 1, UNITS - 1)
                    times_c(i, j)
                    if j == 0 and front:
                        front_stats(i + 1, o)
                    if j == 1 and back:
                        for m in range(MB):
                            take_y(i - 1, o, m)
                    if j == 2 and front:
                        front_norm(i + 1, o)
                    if back and j == 4:
                        out_stats(i - 1)
                    if back and j == 6:
                        out_norm(i - 1, o)
                    if back and j == 7:
                        row_stats(i - 1, o)
                    if back and j == 9:
                        row_norm(i - 1, o)
                if front:
                    softplus_t(i + 1)
                    softplus_sum(i + 1)
                if back:
                    take_logits(i - 1)

            front_stats(0, 0)
            front_norm(0, 0)
            softplus_t(0)
            softplus_sum(0)
            for i in range(4):
                body(i, i % 2, True)
            with dve.Fori(4, PAIRS - 3, 2) as i:
                body(i, 0, True)
                body(i + 1, 1, True)
            body(PAIRS - 2, 0, True)
            body(PAIRS - 1, 1, False)
            n = PAIRS - 1
            fold(n, UNITS - 1)
            for m in range(MB):
                take_y(n, 1, m)
            out_stats(n)
            out_norm(n, 1)
            row_stats(n, 1)
            row_norm(n, 1)
            take_logits(n)

            steps = [0]

            def link(ins):
                steps[0] += 1
                ins.then_inc(s_d, 1)
                dve.wait_ge(s_d, steps[0])

            def by_column(v):
                return v.unsqueeze(1).to_broadcast([H0, E, COLS])

            def by_expert(v):
                return v.unsqueeze(2).to_broadcast([H0, E, COLS])

            def last(v):
                return v.unsqueeze(2).to_broadcast([H0, COLS, E])

            dve.wait_ge(s_stored[0], 16 * PAIRS)
            dve.wait_ge(s_stored[1], 16 * PAIRS)
            dve.wait_ge(s_pool0, 3 + POOL_SET + 2)
            dve.wait_ge(s_lg, PAIRS)
            link(dve.tensor_reduce(exv, logits[:, :, :], AX.X, ALU.max))
            dve.tensor_tensor(ex, logits[:, :, :], last(exv), ALU.subtract).then_inc(s_exin, 1)
            dve.wait_ge(s_exout, 1)
            link(dve.tensor_reduce(exv, ex, AX.X, ALU.max))
            link(dve.tensor_reduce(rsum, ex, AX.X, ALU.add))
            link(dve.reciprocal(rsum, rsum))
            link(dve.tensor_tensor(prob, exv, rsum, ALU.mult))
            sel_c = sel.rearrange("p e c -> p (e c)").rearrange("p (c e) -> p c e", e=E)
            link(dve.tensor_tensor(sel_c, ex, last(exv), ALU.is_ge))
            link(dve.tensor_tensor(sel_c, sel_c, weights8.unsqueeze(1).to_broadcast([H0, COLS, E]), ALU.mult))
            link(dve.tensor_reduce(vmax, sel_c, AX.X, ALU.max))
            link(dve.tensor_tensor(oh, sel_c.rearrange("p c e -> p e c"), by_column(vmax), ALU.is_equal))
            link(dve.tensor_tensor(oh, oh, by_column(valid), ALU.mult))
            dve.tensor_tensor(member, oh, by_column(prob), ALU.mult).then_inc(s_ohr, 1)

            def ranks(times):
                dve.wait_ge(s_ranked, times)
                for e in range(E):
                    c = (e % 4) * COLS
                    ins = dve.tensor_tensor_scan(tot[:, e, :], one_cols, ps_g[e // 4][0:H0, c:c + COLS], 0.0, ALU.mult,
                                                 ALU.add)
                link(ins)
                for half in range(2):
                    v = slice(half * 4, half * 4 + 4)
                    ins = dve.tensor_tensor(place[:, v, :], tot[:, v, :], ps_g[half][0:H0, :].rearrange(
                        "p (e c) -> p e c", e=4), ALU.subtract)
                link(ins)
                for half in range(2):
                    v = slice(half * 4, half * 4 + 4)
                    ins = dve.tensor_tensor(place[:, v, :], place[:, v, :], ps_k[half][0:H0, :].rearrange(
                        "p (e c) -> p e c", e=4), ALU.add)
                link(ins)

            ranks(1)
            link(dve.tensor_copy(n_i, tot[:, :, COLS - 1]))
            link(dve.tensor_copy(n_e, n_i))
            link(dve.tensor_scalar(n_e, n_e, float(TS - 1), None, ALU.add))
            link(dve.tensor_copy(n_i, n_e))
            link(dve.tensor_scalar(n_i, n_i, TS.bit_length() - 1, None, ALU.logical_shift_right))
            link(dve.tensor_copy(tiles_e, n_i))
            link(dve.tensor_tensor_scan(tile_end, one_cols[:, 0:E], tiles_e, 0.0, ALU.mult, ALU.add))
            link(dve.tensor_tensor(base_e, tile_end, tiles_e, ALU.subtract))
            link(dve.tensor_scalar(base_e, base_e, float(TS), None, ALU.mult))
            link(dve.tensor_tensor(place, place, by_expert(base_e), ALU.add))
            link(dve.tensor_tensor(place, place, oh, ALU.mult))
            link(dve.tensor_reduce(destf, place.rearrange("p e c -> p c e"), AX.X, ALU.add))
            link(dve.tensor_copy(desti, destf))
            link(dve.tensor_scalar(dlo_i, desti, P - 1, None, ALU.bitwise_and))
            link(dve.tensor_scalar(dhi_i, desti, P.bit_length() - 1, None, ALU.logical_shift_right))
            link(dve.tensor_copy(destf, dlo_i))
            link(dve.tensor_copy(vmax, dhi_i))
            link(dve.scalar_tensor_tensor(out=destf, in0=destf, scalar=float(SC), in1=vmax, op0=ALU.mult, op1=ALU.add))
            link(dve.tensor_scalar(vmax, valid, -65536.0, 65536.0, ALU.mult, ALU.add))
            link(dve.tensor_tensor(destf, destf, vmax, ALU.add))
            link(dve.tensor_copy(desti, destf))

            link(dve.tensor_tensor(tile_cmp, tile_no.unsqueeze(2).to_broadcast([1, TILES, E]),
                                   tile_end[0:1, :].unsqueeze(1).to_broadcast([1, TILES, E]), ALU.is_ge))
            link(dve.tensor_reduce(tile_no, tile_cmp, AX.X, ALU.add))
            link(dve.tensor_scalar(tile_no, tile_no, float(E - 1), None, ALU.min))
            dve.tensor_copy(tile_ex, tile_no).then_inc(s_tex, 1)

            def batch(t, r):
                need(dve, s_scat[r], 16 * 8 * ((t - r) // 2) if isinstance(t, int) else 64 * (t - r))
                dve.tensor_copy(sidx[r], desti[:, ds(t * 8, 8)])
                dve.tensor_copy(sval[r], ids[:, ds(t * 8, 8)]).then_inc(s_dest[r], 1)

            batch(0, 0)
            batch(1, 1)

            dve.memset(lo_t, 0.0).then_inc(s_d, 1)
            dve.memset(hi_t, 2.0).then_inc(s_d, 1)
            steps[0] += 2
            dve.wait_ge(s_d, steps[0])
            base = steps[0]
            PER = 5

            def halve(t):
                c = [base + PER * t]

                def chain(ins):
                    c[0] = c[0] + 1
                    ins.then_inc(s_d, 1)
                    dve.wait_ge(s_d, c[0])

                chain(dve.tensor_tensor(mid_t, lo_t, hi_t, ALU.add))
                chain(dve.tensor_scalar(mid_t, mid_t, 0.5, None, ALU.mult))
                chain(dve.tensor_tensor(sel, member, by_expert(mid_t), ALU.is_ge))
                dve.tensor_reduce(cnt, sel, AX.X, ALU.add).then_inc(s_cnt, 1)
                dve.wait_ge(s_bis, t + 1)
                total = ps_y[0][0:H0, 0:E]
                dve.scalar_tensor_tensor(out=lo_c, in0=total, scalar=float(CAP), in1=mid_t, op0=ALU.is_ge, op1=ALU.mult)
                chain(dve.scalar_tensor_tensor(out=hi_c, in0=total, scalar=float(CAP), in1=mid_t, op0=ALU.is_ge,
                                               op1=ALU.add))
                dve.tensor_tensor(lo_t, lo_t, lo_c, ALU.max)
                chain(dve.tensor_tensor(hi_t, hi_t, hi_c, ALU.min))

            halve(0)
            HALF = COLS // 8
            with dve.Fori(1, HALF // 2, 1) as t:
                halve(t)
                batch(2 * t, 0)
                batch(2 * t + 1, 1)
            with dve.Fori(HALF // 2, BISECT, 1) as t:
                halve(t)
            steps[0] = base + PER * BISECT

            link(dve.tensor_tensor(sel, member, by_expert(lo_t), ALU.is_gt))
            dve.tensor_reduce(cnt, sel, AX.X, ALU.add).then_inc(s_cnt, 1)
            dve.wait_ge(s_bis, BISECT + 1)
            link(dve.tensor_scalar(room, ps_y[0][0:H0, 0:E], -1.0, float(CAP), ALU.mult, ALU.add))
            link(dve.tensor_tensor(sel, member, by_expert(lo_t), ALU.is_equal))
            dve.tensor_tensor(sel, sel, oh, ALU.mult).then_inc(s_tie, 1)
            ranks(2)
            link(dve.tensor_tensor(place, place, by_expert(room), ALU.is_lt))
            link(dve.tensor_tensor(place, place, sel, ALU.mult))
            link(dve.tensor_tensor(sel, member, by_expert(lo_t), ALU.is_gt))
            link(dve.tensor_tensor(place, place, sel, ALU.add))
            link(dve.tensor_reduce(vmax, place.rearrange("p e c -> p c e"), AX.X, ALU.add))
            link(dve.tensor_tensor(gates[:, :, 0], prob, vmax, ALU.mult))
            link(dve.tensor_scalar(vmax, vmax, -1.0, 1.0, ALU.mult, ALU.add))
            dve.tensor_tensor(gates[:, :, 1], prob, vmax, ALU.mult).then_inc(s_gate, 1)

            def gather_ids(k, g):
                if isinstance(k, int) and k < GRING:
                    done = s_gidx0
                else:
                    done = s_gidx[g]
                    dve.wait_ge(s_mtr, k - GRING + 1)
                dve.tensor_copy(gidx[g], slot_id[:, ds(2 * k, 2)]).then_inc(done, 1)

            def kept_input(k, g, r):
                dve.wait_ge(s_gat[g], 64 * ((k - g) // GRING + 1) if isinstance(k, int) else 64 // GRING * (k - g) + 64)
                for f in range(2):
                    ins = dve.scalar_tensor_tensor(out=mt[r][:, f, :], in0=grow[g][:, f, DIM:2 * DIM],
                                                   scalar=ggate[g][:, f, 1:2], in1=grow[g][:, f, 0:DIM], op0=ALU.mult,
                                                   op1=ALU.add)
                ins.then_inc(s_keepx, 1)

            def finish(k, g, r):
                need(dve, s_put[r], 32 * ((k - r) // 2) if isinstance(k, int) else 16 * (k - r))
                dve.tensor_copy(pidx[r], gidx[g])
                dve.wait_ge(s_w[r], 48 * ((k - r) // 2 + 1) if isinstance(k, int) else 24 * (k - r) + 48)
                for f in range(2):
                    dve.wait_ge(s_m2, 2 * k + f + 1)
                    ins = dve.tensor_tensor(mo[r][:, f, :], ps_k[f][:, 0:DIM], b2r[r], ALU.add)
                ins.then_inc(s_mbias, 1)
                dve.wait_ge(s_mbias, k + 1)
                dve.wait_ge(s_keepx, k + 1)
                for f in range(2):
                    ins = dve.scalar_tensor_tensor(out=mo[r][:, f, :], in0=mo[r][:, f, :], scalar=ggate[g][:, f, 0:1],
                                                   in1=mt[r][:, f, :], op0=ALU.mult, op1=ALU.add)
                ins.then_inc(s_mo[g], 1)

            dve.wait_ge(s_slot, 16)
            for g in range(GRING):
                gather_ids(g, g)

            def tile(k, g, more):
                kept_input(k, g, g % 2)
                finish(k, g, g % 2)
                if more:
                    gather_ids(k + GRING, g)

            for g in range(GRING):
                tile(g, g, True)
            with dve.Fori(GRING, FULL - 2 * GRING + 1, GRING) as k:
                for g in range(GRING):
                    tile(k + g, g, True)
            for t in range(FULL - GRING, TILES):
                tile(t, t % GRING, t + GRING < TILES)


def kernel(x, cls_tok, L0_tok_W, L0_tok_b, L0_attn_W_in, L0_attn_conv_w, L0_attn_conv_b, L0_attn_W_x, L0_attn_W_dt,
           L0_attn_b_dt, L0_attn_A_log, L0_attn_D, L0_attn_W_out, L0_attn_gamma, L0_attn_beta, L0_ffn_switch_w,
           L0_ffn_switch_b, L0_ffn_w1, L0_ffn_b1, L0_ffn_w2, L0_ffn_b2):
    import numpy as np
    import concourse.bacc as bacc
    from concourse.bass_utils import run_bass_kernel_spmd

    a = np.asarray

    def blocks(w, k):
        return a(w).reshape(k, P, -1).transpose(1, 0, 2)

    def column(v, k):
        return a(v).reshape(k, P).T

    w_in = a(L0_attn_W_in)
    w1, w2 = a(L0_ffn_w1), a(L0_ffn_w2)
    w_pack = np.concatenate([
        w1[:, 0:P, :],
        w2.reshape(E, KF, P, DIM).transpose(0, 2, 1, 3).reshape(E, P, KF * DIM),
        a(L0_ffn_b1).reshape(E, KF, P).transpose(0, 2, 1),
    ], axis=2)
    side = 14
    xt = a(x).reshape(PAIRS, 2, 3, side, 16, side, 16).transpose(0, 2, 4, 6, 1, 3, 5)
    xt = xt.reshape(PAIRS, KP, P, 2, PATCHES).transpose(0, 2, 1, 3, 4)
    arrays = {
        "x": xt,
        "cls_tok": a(cls_tok).reshape(1, DIM),
        "tok_w": blocks(a(L0_tok_W).T, KP),
        "tok_b": a(L0_tok_b),
        "w_inx": blocks(w_in[:, 0:INNER].T, MB),
        "w_zlo": w_in[0:P, INNER:],
        "w_zhi": w_in[P:DIM, INNER:],
        "conv_w": a(L0_attn_conv_w).reshape(TAPS, MB, P, INNER).transpose(2, 0, 1, 3),
        "conv_b": column(L0_attn_conv_b, MB),
        "w_x": blocks(L0_attn_W_x, MB),
        "w_dt": blocks(L0_attn_W_dt, MB),
        "b_dt": column(L0_attn_b_dt, MB),
        "a_log": blocks(L0_attn_A_log, MB),
        "d_skip": column(L0_attn_D, MB),
        "w_out": blocks(L0_attn_W_out, MB),
        "gamma": a(L0_attn_gamma),
        "beta": a(L0_attn_beta),
        "sw_w": a(L0_ffn_switch_w),
        "sw_b": a(L0_ffn_switch_b),
        "w_pack": w_pack,
        "w1_hi": w1[:, P:DIM, :],
        "b2": a(L0_ffn_b2),
    }
    arrays = {f"in_{k}": np.ascontiguousarray(v) for k, v in arrays.items()}
    nc = bacc.Bacc("TRN2", target_bir_lowering=False, num_devices=1)
    args = [nc.dram_tensor(k, v.shape, F32, kind="ExternalInput").ap() for k, v in arrays.items()]
    out = nc.dram_tensor("out_tokens", (TOK, DIM), F32, kind="ExternalOutput").ap()
    build(nc, *args, out)
    r = run_bass_kernel_spmd(nc, [arrays], core_ids=[0])
    return r.results[0]["out_tokens"].reshape(IMAGES, L, DIM)
```

```python
from contextlib import ExitStack

import concourse.bass as bass
from concourse import mybir

F32 = mybir.dt.float32
I32 = mybir.dt.int32
BF16 = mybir.dt.bfloat16
U32 = mybir.dt.uint32
ALU = mybir.AluOpType
ACT = mybir.ActivationFunctionType
AX = mybir.AxisListType
ds = bass.ds

P = 128
IMAGES = 64
PAIRS = IMAGES // 2
PATCHES = 196
L = PATCHES + 1
TOK = IMAGES * L
N2 = 2 * L
H0 = 99
HSTEP = L - H0
DIM = 192
DLO = DIM - P
PD = 768
KP = PD // P
INNER = 384
MB = INNER // P
NS = 16
LEAD = 3
TAPS = 4
E = 8
FF = 768
KF = FF // P
CAP = int(1.25 * TOK / E)
COLS = 2 * IMAGES
TS = 256
TILES = TOK // TS + E
SLOTS = TILES * TS
GRING = 4
FULL = TILES // GRING * GRING
SC = SLOTS // P
NOBODY = 1 << 15
BISECT = 29
EPS = 1e-5
A_BUFS, B_BUFS = 4, 4
PIECES = (0, 2, 3)
POOL_SET = 8 + 2 * GRING


def need(eng, sem, count):
    if not isinstance(count, int) or count > 0:
        eng.wait_ge(sem, count)


def build(nc, x, cls_tok, tok_w, tok_b, w_inx, w_zlo, w_zhi, conv_w, conv_b, w_x, w_dt, b_dt, a_log, d_skip, w_out, gamma,
          beta, sw_w, sw_b, w_pack, w1_hi, b2, out):
    rows_dram = nc.dram_tensor("rows_scratch", (TOK, 2 * DIM), F32, kind="Internal").ap()
    slot_dram = nc.dram_tensor("slot_scratch", (SLOTS, 1), I32, kind="Internal").ap()
    gate_dram = nc.dram_tensor("gate_scratch", (TOK, 2), F32, kind="Internal").ap()

    with ExitStack() as ctx:
        def sb(name, shape, dt=F32):
            return ctx.enter_context(nc.sbuf_tensor(name, shape, dt))

        def sem(name):
            return ctx.enter_context(nc.semaphore(name))

        ident = sb("ident", [P, P])
        wtok = sb("wtok", [P, KP, DIM])
        v_lo = sb("v_lo", [P, TAPS, INNER])
        v_hi = sb("v_hi", [P, 2, INNER])
        wz_lo = sb("wz_lo", [P, INNER])
        wz_hi = sb("wz_hi", [DLO, INNER])
        wx = sb("wx", [P, MB, 4, 2 * NS])
        pick = sb("pick", [P, 2 * NS, P], BF16)
        wdt = sb("wdt", [P, MB, INNER])
        wout = sb("wout", [P, MB, DIM])
        cb = sb("cb", [P, MB])
        bdt = sb("bdt", [P, MB])
        dsk = sb("dsk", [P, MB])
        neg_a = sb("neg_a", [P, MB, NS])
        tok_bias = sb("tok_bias", [H0, 2, DIM])
        gam = sb("gam", [H0, DIM])
        bet = sb("bet", [H0, DIM])
        sww_lo = sb("sww_lo", [P, E])
        sww_hi = sb("sww_hi", [DLO, E])
        swb = sb("swb", [H0, E])
        minus_half = sb("minus_half", [P, 4])
        logits = sb("logits", [H0, COLS, E])

        arena = sb("arena", [P, 42500])
        at = [0]

        def carve(parts, *shape):
            n = 1
            for k in shape:
                n *= k
            v = arena[0:parts, at[0]:at[0] + n]
            at[0] += n + n % 2
            if len(shape) == 2:
                v = v.rearrange("p (a b) -> p a b", a=shape[0])
            elif len(shape) == 3:
                v = v.rearrange("p (a b c) -> p a b c", a=shape[0], b=shape[1])
            elif len(shape) == 4:
                v = v.rearrange("p (a b c d) -> p a b c d", a=shape[0], b=shape[1], c=shape[2])
            return v

        patches = carve(P, KP, 2, L)
        h = [carve(H0, 4, DIM) for _ in range(2)]
        hn = carve(H0, 4, DIM)
        hres = carve(H0, 4, DIM)
        t_lo = carve(P, 2, L + 3)
        t_hi = carve(P, 2, L + 3)
        xz = [carve(P, 2 * MB, N2) for _ in range(2)]
        spv = carve(P, MB, N2)
        spe = carve(P, MB, N2)
        spl = carve(P, MB, N2)
        spt = carve(P, MB, N2)
        delta = [carve(P, MB, N2) for _ in range(2)]
        du = [carve(P, MB, N2) for _ in range(2)]
        bcf = carve(P, N2)
        bc3 = [carve(P, L).bitcast(BF16) for _ in range(2)]
        y = carve(P, MB, N2)
        decay = [carve(P, MB, 2, L) for _ in range(A_BUFS)]
        hb_at = at[0]
        hb = [carve(P, MB, N2) for _ in range(B_BUFS)]
        rows = [carve(H0, 4, 2 * DIM) for _ in range(2)]
        h2_lo = carve(P, 4, H0)
        h2_hi = carve(DLO, 4, H0)
        st1, st2, st3 = (carve(H0, 4, 6) for _ in range(3))
        mv1, mv2, mv3 = (carve(H0, 4, 2) for _ in range(3))
        rs1, rs2, rs3 = (carve(H0, 4) for _ in range(3))
        raw_taps = arena[:, hb_at:hb_at + TAPS * MB * INNER].rearrange("p (t k n) -> p t k n", t=TAPS, k=MB)
        raw_win = y.rearrange("p a b -> p (a b)")[:, 0:MB * DIM].rearrange("p (k n) -> p k n", k=MB)
        a_end = at[0]

        at[0] = 0
        ex = carve(H0, COLS, E)
        oh = carve(H0, E, COLS)
        member = carve(H0, E, COLS)
        place = carve(H0, E, COLS)
        sel = carve(H0, E, COLS)
        tot = carve(H0, E, COLS)
        exv = carve(H0, COLS)
        prob = carve(H0, COLS)
        rsum = carve(H0, COLS)
        vmax = carve(H0, COLS)
        valid = carve(H0, COLS)
        destf = carve(H0, COLS)
        desti = carve(H0, COLS).bitcast(I32)
        dlo_i = carve(H0, COLS).bitcast(I32)
        dhi_i = carve(H0, COLS).bitcast(I32)
        ids = carve(H0, COLS).bitcast(I32)
        one_cols = carve(H0, COLS)
        weights8 = carve(H0, E)
        before = carve(H0, H0)
        every = carve(H0, H0)
        n_e = carve(H0, E)
        n_i = carve(H0, E).bitcast(I32)
        tiles_e = carve(H0, E)
        tile_end = carve(H0, E)
        base_e = carve(H0, E)
        lo_t, hi_t, mid_t, cnt, room = (carve(H0, E) for _ in range(5))
        lo_c, hi_c = carve(H0, E), carve(H0, E)
        gates = carve(H0, COLS, 2)
        tile_no = carve(1, TILES)
        tile_cmp = carve(1, TILES, E)
        tile_ex = carve(1, TILES).bitcast(I32)
        slot_id = carve(P, SC).bitcast(I32)
        sidx = [carve(H0, 8).bitcast(I32) for _ in range(2)]
        sval = [carve(H0, 8).bitcast(I32) for _ in range(2)]
        gidx = [carve(P, 2).bitcast(I32) for _ in range(GRING)]
        pidx = [carve(P, 2).bitcast(I32) for _ in range(2)]
        grow = [carve(P, 2, 2 * DIM) for _ in range(GRING)]
        ggate = [carve(P, 2, 2) for _ in range(GRING)]
        wp = [carve(P, FF + KF * DIM + KF) for _ in range(2)]
        w1h = [carve(DLO, FF) for _ in range(2)]
        b2r = [carve(P, DIM) for _ in range(2)]
        g_lo = [carve(P, TS) for _ in range(2)]
        g_hi = [carve(DLO, TS) for _ in range(2)]
        hid = [carve(P, KF, TS) for _ in range(2)]
        mo = [carve(P, 2, DIM) for _ in range(2)]
        mt = [carve(P, 2, DIM) for _ in range(2)]
        assert max(a_end, at[0]) <= 42500, (a_end, at[0])

        pb = [ctx.enter_context(nc.psum_tensor(f"bank{i}", [P, 512], F32)) for i in range(8)]
        ps_y = pb[0:3]
        ps_b, ps_c = pb[3:5]
        ps_k = pb[5:7]
        ps_t = pb[7]
        ps_g = pb[3:5]

        s_const = sem("consts_landed")
        s_taps = sem("raw_taps_landed")
        s_pool0 = sem("pool_consts_set")
        s_dve0 = sem("dve_consts_set")
        s_nega = sem("neg_a_ready")
        s_clsrow = sem("class_row_landed")
        s_pick = sem("pick_clear")
        s_vmm = sem("tap_product_done")
        s_vcopy = sem("tap_copied")
        s_patch = sem("patches_landed")
        s_tokmm = sem("tok_product_done")
        s_hres = sem("residual_copied")
        s_h = sem("h_ready")
        s_st1 = sem("stats1_ready")
        s_mv1 = sem("meanvar1_ready")
        s_ve1 = sem("vareps1_ready")
        s_rs1 = sem("rstd1_ready")
        s_hn = sem("hn_ready")
        s_trf = sem("front_transposed")
        s_trf_copied = sem("front_transposes_copied")
        s_gmm = sem("front_product_done")
        s_gev = sem("front_product_copied")
        s_x = sem("x_ready")
        s_z = sem("z_ready")
        s_bcrest = sem("bc_rest_ready")
        s_bcmid = sem("bc_second_part_ready")
        s_bc3 = sem("bc_parts_ready")
        s_bb = sem("b_spread")
        s_cb = sem("c_spread")
        s_spa = sem("softplus_abs")
        s_spe = sem("softplus_exp")
        s_spt = sem("softplus_rounded")
        s_spc = sem("softplus_rest")
        s_spl = sem("softplus_ln")
        s_spd = sem("softplus_sum")
        s_delta = sem("delta_ready")
        s_du = sem("du_ready")
        s_a = sem("decay_ready")
        s_bx = sem("bx_ready")
        s_scan = sem("scan_done")
        s_mul = sem("hc_ready")
        s_ysum = sem("state_sum_done")
        s_yev = sem("y_ready")
        s_ysz = sem("y_gated")
        s_opmm = sem("out_product_done")
        s_st2 = sem("stats2_ready")
        s_mv2 = sem("meanvar2_ready")
        s_ve2 = sem("vareps2_ready")
        s_rs2 = sem("rstd2_ready")
        s_opread = sem("out_product_read")
        s_gam = sem("gamma_applied")
        s_hbeta = sem("residual_beta_ready")
        s_h2 = sem("h2_ready")
        s_st3 = sem("stats3_ready")
        s_mv3 = sem("meanvar3_ready")
        s_ve3 = sem("vareps3_ready")
        s_rs3 = sem("rstd3_ready")
        s_rows = sem("rows_ready")
        s_stored = [sem(f"rows_stored{i}") for i in range(2)]
        s_trb = sem("back_transposed")
        s_trb_copied = sem("back_transposes_copied")
        s_lgmm = sem("logits_product_done")
        s_lg = sem("logits_ready")
        s_d = sem("dve_step")
        s_exin = sem("router_shifted")
        s_exout = sem("router_exp_ready")
        s_ohr = sem("route_ready")
        s_ranked = sem("rank_products_done")
        s_tie = sem("ties_ready")
        s_cnt = sem("bisect_counts_ready")
        s_bis = sem("bisect_totals_ready")
        s_fill = sem("slots_cleared")
        s_dest = [sem(f"slot_batch_ready{i}") for i in range(2)]
        s_scat = [sem(f"slot_ids_scattered{i}") for i in range(2)]
        s_tex = sem("tile_experts_ready")
        s_slot = sem("slot_ids_landed")
        s_gate = sem("gates_ready")
        s_gated = sem("gates_stored")
        s_w = [sem(f"expert_weights_landed{i}") for i in range(2)]
        s_gidx0 = sem("first_gather_ids_ready")
        s_gidx = [sem(f"gather_ids_ready{i}") for i in range(GRING)]
        s_gat = [sem(f"rows_gathered{i}") for i in range(GRING)]
        s_mtr = sem("tile_transposed")
        s_mtc = sem("tile_transposes_copied")
        s_m1 = sem("hidden_product_done")
        s_hid = sem("hidden_ready")
        s_m2 = sem("expert_product_done")
        s_keepx = sem("kept_input_ready")
        s_mbias = sem("expert_bias_added")
        s_mo = [sem(f"tile_rows_ready{i}") for i in range(GRING)]
        s_put = [sem(f"tile_rows_stored{i}") for i in range(2)]

        CLEAR = 5
        CONSTS = 20

        BC, DT, Z = MB, MB + 1, 2 * MB + 1

        def bank(t):
            return ps_k[t - Z] if Z <= t < Z + 2 else ps_t

        block = ctx.enter_context(nc.Block())

        @block.sync
        def _(sp):
            for dst, src in (
                (wtok[:, :, :], tok_w), (wz_lo[:, :], w_zlo), (wz_hi[:, :], w_zhi), (wdt[:, :, :], w_dt),
                (wout[:, :, :], w_out), (cb[:, :], conv_b), (bdt[:, :], b_dt), (dsk[:, :], d_skip), (neg_a[:, :, :], a_log),
                (tok_bias[:, 0, :], tok_b.partition_broadcast(H0)), (tok_bias[:, 1, :], tok_b.partition_broadcast(H0)),
                (gam[:, :], gamma.partition_broadcast(H0)), (bet[:, :], beta.partition_broadcast(H0)),
                (sww_lo[:, :], sw_w[0:P, :]), (sww_hi[:, :], sw_w[P:DIM, :]), (swb[:, :], sw_b.partition_broadcast(H0)),
                *((wx[:, :, c, :], w_x) for c in range(4)),
            ):
                sp.dma_start(dst, src).then_inc(s_const, 16)
            sp.dma_start(raw_taps, conv_w).then_inc(s_taps, 16)
            sp.dma_start(raw_win, w_inx).then_inc(s_taps, 16)
            sp.wait_ge(s_const, 16 * CONSTS)
            sp.dma_start(tok_bias[0:1, 0, :], cls_tok).then_inc(s_clsrow, 16)

            def load_patches(n):
                need(sp, s_tokmm, 2 * n)
                sp.dma_start(patches[:, :, :, 1:L], x[ds(n, 1)].rearrange("o p k b n -> (o p) k b n")
                             if not isinstance(n, int) else x[n]).then_inc(s_patch, 16)

            def store_rows(n, r):
                sp.wait_ge(s_rows, n + 1)
                t = rows_dram[ds(n * N2, N2), :].rearrange("(b t) d -> t b d", b=2)
                v = rows[r].rearrange("p (b f) d -> p b f d", f=2)
                sp.dma_start(t[0:H0], v[:, :, 0, :]).then_inc(s_stored[r], 16)
                sp.dma_start(t[H0:L], v[1:H0, :, 1, :]).then_inc(s_stored[r], 16)

            def body(i, r, tok):
                if tok:
                    load_patches(i + 2)
                if not isinstance(i, int) or i >= 1:
                    store_rows(i - 1, 1 - r)

            sp.wait_ge(s_dve0, 1)
            load_patches(0)
            load_patches(1)
            for i in range(4):
                body(i, i % 2, True)
            with sp.Fori(4, PAIRS - 3, 2) as i:
                body(i, 0, True)
                body(i + 1, 1, True)
            body(PAIRS - 2, 0, False)
            body(PAIRS - 1, 1, False)
            store_rows(PAIRS - 1, 1)

            for b in range(2):
                sp.wait_ge(s_scat[b], 16 * COLS // 2)
            sp.wait_ge(s_fill, 16)
            sp.dma_start(slot_id, slot_dram.rearrange("(p c) o -> p (c o)", p=P)).then_inc(s_slot, 16)

            def load_expert(k, r):
                need(sp, s_m2, 2 * (k - 1))
                need(sp, s_mbias, k - 1)
                e = sp.value_load(tile_ex[0:1, ds(k, 1)], min_val=0, max_val=E - 1)
                sp.dma_start(wp[r], w_pack[ds(e, 1)].rearrange("o p n -> (o p) n")).then_inc(s_w[r], 16)
                sp.dma_start(w1h[r], w1_hi[ds(e, 1)].rearrange("o p n -> (o p) n")).then_inc(s_w[r], 16)
                sp.dma_start(b2r[r], b2[ds(e, 1), :].rearrange("o n -> (o n)").partition_broadcast(P)).then_inc(s_w[r], 16)

            sp.wait_ge(s_tex, 1)
            load_expert(0, 0)
            load_expert(1, 1)

            def gates_out():
                sp.wait_ge(s_gate, 1)
                g = gate_dram.rearrange("(b t) w -> t b w", t=L)
                v = gates.rearrange("p (b f) w -> p b f w", f=2)
                sp.dma_start(g[0:H0], v[:, :, 0, :]).then_inc(s_gated, 16)
                sp.dma_start(g[H0:L], v[1:H0, :, 1, :]).then_inc(s_gated, 16)

            gates_out()
            with sp.Fori(2, TILES - 2, 2) as k:
                load_expert(k, 0)
                load_expert(k + 1, 1)
            load_expert(TILES - 1, 0)
            for r in range(2):
                sp.wait_ge(s_stored[r], 16 * PAIRS)
                sp.wait_ge(s_put[r], 32 * ((TILES + 1 - r) // 2))
            sp.wait_ge(s_gated, 32)

        @block.gpsimd
        def _(pool):
            pool.memset(ident[:, :], 0.0).then_inc(s_pool0, 1)
            pool.memset(minus_half[:, :], -0.5).then_inc(s_pool0, 1)
            pool.wait_ge(s_pool0, 2)
            pool.affine_select(out=ident[:, :], in_=ident[:, :], compare_op=ALU.not_equal, fill=1.0, base=0,
                               pattern=[[-1, P]], channel_multiplier=1).then_inc(s_pool0, 1)

            def rstd(n, s_in, mv, rs, s_out):
                pool.wait_ge(s_in, n + 1)
                pool.tensor_tensor(rs[:, :], mv[:, :, 1], minus_half[0:H0, :], ALU.pow).then_inc(s_out, 1)

            def gate_y(n, r):
                pool.wait_ge(s_yev, MB * (n + 1))
                pool.wait_ge(s_z, n + 1)
                pool.tensor_tensor(y[:, :, :], y[:, :, :], xz[r][:, MB:2 * MB, :], ALU.mult).then_inc(s_ysz, 1)

            def add_beta(n):
                pool.wait_ge(s_hres, n + 1)
                pool.tensor_tensor(hres[:, :, :], hres[:, :, :], bet[:, :].unsqueeze(1).to_broadcast([H0, 4, DIM]),
                                   ALU.add).then_inc(s_hbeta, 1)

            def add_residual(n, r):
                need(pool, s_stored[r], 16 * (n - r))
                pool.wait_ge(s_gam, n + 1)
                pool.wait_ge(s_hbeta, n + 1)
                pool.tensor_tensor(rows[r][:, :, 0:DIM], rows[r][:, :, 0:DIM], hres[:, :, :], ALU.add).then_inc(s_h2, 1)

            def softplus_rest(n):
                pool.wait_ge(s_spt, n + 1)
                pool.tensor_tensor(spt[:, :, :], spe[:, :, :], spt[:, :, :], ALU.subtract).then_inc(s_spc, 1)

            def make_du(n, r):
                pool.wait_ge(s_delta, n + 1)
                need(pool, s_bx, NS * (n - 1))
                pool.tensor_tensor(du[r][:, :, :], delta[r][:, :, :], xz[r][:, 0:MB, :], ALU.mult).then_inc(s_du, 1)

            def body(i, r, front, tokens):
                o = 1 - r
                if not isinstance(i, int) or i >= 1:
                    gate_y(i - 1, o)
                    add_beta(i - 1)
                    rstd(i - 1, s_ve2, mv2, rs2, s_rs2)
                    add_residual(i - 1, o)
                    rstd(i - 1, s_ve3, mv3, rs3, s_rs3)
                if front:
                    softplus_rest(i + 1)
                    make_du(i + 1, o)
                if tokens:
                    rstd(i + 2, s_ve1, mv1, rs1, s_rs1)

            pool.wait_ge(s_dve0, CLEAR)
            rstd(0, s_ve1, mv1, rs1, s_rs1)
            softplus_rest(0)
            make_du(0, 0)
            rstd(1, s_ve1, mv1, rs1, s_rs1)
            for i in range(4):
                body(i, i % 2, True, True)
            with pool.Fori(4, PAIRS - 3, 2) as i:
                body(i, 0, True, True)
                body(i + 1, 1, True, True)
            body(PAIRS - 2, 0, True, False)
            body(PAIRS - 1, 1, False, False)
            n = PAIRS - 1
            gate_y(n, 1)
            add_beta(n)
            rstd(n, s_ve2, mv2, rs2, s_rs2)
            add_residual(n, 1)
            rstd(n, s_ve3, mv3, rs3, s_rs3)

            pool.wait_ge(s_stored[0], 16 * PAIRS)
            pool.wait_ge(s_stored[1], 16 * PAIRS)
            pool.wait_ge(s_lg, PAIRS)
            pool.memset(before, 1.0).then_inc(s_pool0, 1)
            pool.memset(every, 1.0).then_inc(s_pool0, 1)
            pool.memset(valid, 1.0).then_inc(s_pool0, 1)
            pool.memset(one_cols, 1.0).then_inc(s_pool0, 1)
            pool.iota(slot_id, [[0, SC]], base=NOBODY, channel_multiplier=0).then_inc(s_pool0, 1)
            pool.iota(ids.rearrange("p (b f) -> p b f", f=2), [[L, IMAGES], [HSTEP, 2]], base=0,
                      channel_multiplier=1).then_inc(s_pool0, 1)
            pool.iota(weights8, [[-1, E]], base=E, channel_multiplier=0,
                      allow_small_or_imprecise_dtypes=True).then_inc(s_pool0, 1)
            pool.iota(tile_no, [[1, TILES]], base=0, channel_multiplier=0,
                      allow_small_or_imprecise_dtypes=True).then_inc(s_pool0, 1)
            for r in range(GRING):
                pool.memset(grow[r], 0.0).then_inc(s_pool0, 1)
                pool.memset(ggate[r], 0.0).then_inc(s_pool0, 1)
            pool.wait_ge(s_pool0, 3 + POOL_SET)
            pool.affine_select(out=before, in_=before, compare_op=ALU.is_gt, fill=0.0, base=0, pattern=[[1, H0]],
                               channel_multiplier=-1).then_inc(s_pool0, 1)
            pool.affine_select(out=valid.rearrange("p (b f) -> p b f", f=2), in_=valid.rearrange("p (b f) -> p b f", f=2),
                               compare_op=ALU.is_ge, fill=0.0, base=0, pattern=[[0, IMAGES], [-1, 2]],
                               channel_multiplier=2).then_inc(s_pool0, 1)
            pool.dma_start(slot_dram.rearrange("(p c) o -> p (c o)", p=P), slot_id).then_inc(s_fill, 16)

            last_slot, last_token = pool.to_reg(SLOTS - 1), pool.to_reg(TOK - 1)

            def scatter(u, r):
                pool.wait_ge(s_fill, 16)
                pool.wait_ge(s_dest[r], u)
                for c in range(8):
                    pool.indirect_dma_start(
                        out=slot_dram, out_offset=bass.IndirectOffsetOnAxis(ap=sidx[r][:, c:c + 1].bitcast(U32), axis=0),
                        in_=sval[r][:, c:c + 1], in_offset=None, bounds_check=last_slot, oob_is_err=False,
                    ).then_inc(s_scat[r], 16)

            with pool.Fori(1, COLS // 16 + 1, 1) as u:
                scatter(u, 0)
                scatter(u, 1)

            def gather(g, u):
                pool.wait_ge(s_gated, 32)
                if isinstance(u, int) and u == 0:
                    pool.wait_ge(s_gidx0, g + 1)
                else:
                    pool.wait_ge(s_gidx[g], u)
                for f in range(2):
                    i = bass.IndirectOffsetOnAxis(ap=gidx[g][:, f:f + 1].bitcast(U32), axis=0)
                    pool.indirect_dma_start(out=grow[g][:, f, :], out_offset=None, in_=rows_dram, in_offset=i,
                                            bounds_check=last_token, oob_is_err=False).then_inc(s_gat[g], 16)
                    pool.indirect_dma_start(out=ggate[g][:, f, :], out_offset=None, in_=gate_dram, in_offset=i,
                                            bounds_check=last_token, oob_is_err=False).then_inc(s_gat[g], 16)

            def put(g, u):
                r = g % 2
                pool.wait_ge(s_gated, 32)
                pool.wait_ge(s_mo[g], u)
                for f in range(2):
                    pool.indirect_dma_start(
                        out=out, out_offset=bass.IndirectOffsetOnAxis(ap=pidx[r][:, f:f + 1].bitcast(U32), axis=0),
                        in_=mo[r][:, f, :], in_offset=None, bounds_check=last_token, oob_is_err=False,
                    ).then_inc(s_put[r], 16)

            for g in range(GRING):
                gather(g, 0)
            with pool.Fori(1, TILES // GRING, 1) as u:
                for g in range(GRING):
                    put(g, u)
                    gather(g, u)
            for t in range(FULL - GRING, TILES):
                put(t % GRING, t // GRING + 1)
                if t + GRING < TILES:
                    gather(t % GRING, t // GRING + 1)

        @block.scalar
        def _(act):
            act.wait_ge(s_const, 16 * CONSTS)
            act.activation(neg_a[:, :, :], neg_a[:, :, :], ACT.Exp).then_inc(s_nega, 1)
            act.wait_ge(s_nega, 1)
            act.activation(neg_a[:, :, :], neg_a[:, :, :], ACT.Copy, scale=-1.0).then_inc(s_nega, 1)

            def decays(n, r, s):
                b = s % A_BUFS
                if s == 0:
                    act.wait_ge(s_delta, n + 1)
                need(act, s_scan, NS * n + s - A_BUFS + 1)
                for m in range(MB):
                    d = delta[r][:, m, :].rearrange("p (b t) -> p b t", b=2)[:, :, 1:L]
                    ins = act.activation(decay[b][:, m, :, 1:L], d, ACT.Exp, scale=neg_a[:, m, s:s + 1])
                ins.then_inc(s_a, 1)

            def copy_residual(n, r):
                need(act, s_h2, n)
                act.wait_ge(s_h, n + 1)
                act.activation(hres[:, :, :], h[r][:, :, :], ACT.Copy).then_inc(s_hres, 1)

            def copy_front_t(n, b):
                act.wait_ge(s_trf, 2 * n + b + 1)
                if b == 0:
                    need(act, s_gmm, 10 * n)
                act.activation(t_lo[:, b, 1:L + 1], ps_k[b][:, 0:L], ACT.Copy)
                act.activation(t_hi[0:DLO, b, 1:L + 1], ps_k[b][0:DLO, L:2 * L], ACT.Copy)
                act.activation(t_hi[DLO:P, b, 0:L], ps_k[b][0:DLO, L:2 * L], ACT.Copy).then_inc(s_trf_copied, 1)

            def copy_product(n, r, t):
                act.wait_ge(s_gmm, 10 * n + t + 1)
                src = bank(t)[:, 0:N2]
                if t < BC:
                    if t == 0:
                        need(act, s_yev, MB * (n - 1))
                        need(act, s_du, n - 1)
                    ins = act.activation(xz[r][:, t, :], src, ACT.Identity, bias=cb[:, t:t + 1])
                elif t == BC:
                    need(act, s_cb, NS * (n - 1))
                    need(act, s_bc3, n)
                    act.activation(bcf, src, ACT.Copy)
                    ins = act.activation(bc3[r], src, ACT.Copy)
                elif t < Z:
                    m = t - DT
                    if m == 0:
                        need(act, s_delta, n)
                    act.activation(spv[:, m, :], src, ACT.Identity, bias=bdt[:, m:m + 1])
                    ins = act.activation(spe[:, m, :], src, ACT.Abs, bias=bdt[:, m:m + 1])
                else:
                    if t == Z:
                        need(act, s_ysz, n - 1)
                    ins = act.activation(xz[r][:, MB + t - Z, :], src, ACT.Copy)
                ins.then_inc(s_gev, 1)

            def silu_x(n, r):
                act.wait_ge(s_gev, 10 * n + BC)
                act.activation(xz[r][:, 0:MB, :], xz[r][:, 0:MB, :], ACT.Silu).then_inc(s_x, 1)

            def silu_z(n, r):
                act.wait_ge(s_gev, 10 * (n + 1))
                act.activation(xz[r][:, MB:2 * MB, :], xz[r][:, MB:2 * MB, :], ACT.Silu).then_inc(s_z, 1)

            def softplus(n):
                act.wait_ge(s_gev, 10 * n + Z)
                act.activation(spe[:, :, :], spe[:, :, :], ACT.Exp, scale=-1.0).then_inc(s_spe, 1)
                act.wait_ge(s_spe, n + 1)
                act.activation(spl[:, :, :], spe[:, :, :], ACT.Ln, bias=1.0).then_inc(s_spl, 1)

            def copy_back_t(n, b):
                act.wait_ge(s_trb, 2 * n + b + 1)
                if b == 0:
                    need(act, s_lgmm, n)
                act.activation(h2_lo[:, 2 * b:2 * b + 2, :], ps_t[:, 0:2 * H0], ACT.Copy)
                act.activation(h2_hi[:, 2 * b:2 * b + 2, :], ps_t[0:DLO, 2 * H0:4 * H0], ACT.Copy).then_inc(s_trb_copied, 1)

            def body(i, r, front, tokens):
                back = not isinstance(i, int) or i >= 1
                o = 1 - r
                n = i + 1
                for j in range(NS):
                    if j == 0:
                        copy_product(i, r, Z + 2)
                        if front:
                            copy_front_t(n, 0)
                            copy_front_t(n, 1)
                    if front:
                        for t in {2: (0,), 5: (1,), 7: (2,), 9: (BC,), 10: (DT,), 11: (DT + 1,), 12: (DT + 2,),
                                  15: (Z, Z + 1)}.get(j, ()):
                            copy_product(n, o, t)
                        if j == 7:
                            silu_x(n, o)
                        if j == 12:
                            softplus(n)
                    if j == 7:
                        silu_z(i, r)
                    if j == 9:
                        copy_residual(i, r)
                    if back and j == 13:
                        copy_back_t(i - 1, 0)
                    if back and j == 14:
                        copy_back_t(i - 1, 1)
                    if j + LEAD < NS:
                        decays(i, r, j + LEAD)
                    elif front:
                        decays(n, o, j + LEAD - NS)

            act.wait_ge(s_dve0, CLEAR)
            copy_front_t(0, 0)
            copy_front_t(0, 1)
            for t in range(Z + 2):
                if t == BC:
                    silu_x(0, 0)
                copy_product(0, 0, t)
            softplus(0)
            for s in range(LEAD):
                decays(0, 0, s)
            for i in range(4):
                body(i, i % 2, True, True)
            with act.Fori(4, PAIRS - 3, 2) as i:
                body(i, 0, True, True)
                body(i + 1, 1, True, True)
            body(PAIRS - 2, 0, True, False)
            body(PAIRS - 1, 1, False, False)
            copy_back_t(PAIRS - 1, 0)
            copy_back_t(PAIRS - 1, 1)

            act.wait_ge(s_exin, 1)
            act.activation(ex, ex, ACT.Exp).then_inc(s_exout, 1)

            def tile_copies(k, r):
                act.wait_ge(s_mtr, k + 1)
                need(act, s_m1, KF * (k - 1))
                act.activation(g_lo[r], ps_t[:, 0:TS], ACT.Copy)
                act.activation(g_hi[r], ps_t[0:DLO, TS:2 * TS], ACT.Copy).then_inc(s_mtc, 1)

            def gelus(k, r):
                b1 = wp[r][:, FF + KF * DIM:]
                need(act, s_m2, 2 * (k - 1))
                for f in range(KF):
                    act.wait_ge(s_m1, KF * k + f + 1)
                    act.activation(hid[r][:, f, :], (ps_y + ps_g[0:1])[f % 4][:, 0:TS], ACT.Gelu,
                                   bias=b1[:, f:f + 1]).then_inc(s_hid, 1)

            tile_copies(0, 0)
            for k in range(2):
                gelus(k, k)
                tile_copies(k + 1, 1 - k)
            with act.Fori(2, TILES - 2, 2) as k:
                gelus(k, 0)
                tile_copies(k + 1, 1)
                gelus(k + 1, 1)
                tile_copies(k + 2, 0)
            gelus(TILES - 1, 0)

        @block.tensor
        def _(pe):
            pe.wait_ge(s_taps, 32)
            n = 0
            for k in range(TAPS):
                for lo, m in ((0, P), (P, DLO)):
                    need(pe, s_vcopy, n - 1)
                    for c in range(MB):
                        mm = pe.matmul(ps_g[n % 2][0:m, 0:INNER], raw_win[:, c, lo:lo + m], raw_taps[:, k, c, :],
                                       start=(c == 0), stop=(c == MB - 1))
                    mm.then_inc(s_vmm, 1)
                    n += 1
            VPROD = n

            def tok(n, b, first, last):
                if first == 0:
                    if b == 0:
                        pe.wait_ge(s_patch, 16 * (n + 1))
                    need(pe, s_trf_copied, 2 * n)
                    need(pe, s_opread, n - 2)
                for a in range(first, last):
                    f, c = a // KP, a % KP
                    mm = pe.matmul(ps_k[b][0:H0, f * DIM:(f + 1) * DIM], patches[:, c, b, f * HSTEP:f * HSTEP + H0],
                                   wtok[:, c, :], start=(c == 0), stop=(c == KP - 1))
                if last == 2 * KP:
                    mm.then_inc(s_tokmm, 1)

            def front_t(n, b):
                if b == 0:
                    pe.wait_ge(s_hn, n + 1)
                need(pe, s_gev, 10 * (n - 1) + Z + 1 + b)
                for f in (1, 0):
                    c = f * HSTEP
                    pe.transpose(ps_k[b][:, c:c + H0], hn[:, 2 * b + f, 0:P], ident[0:H0, 0:H0])
                    mm = pe.transpose(ps_k[b][0:DLO, L + c:L + c + H0], hn[:, 2 * b + f, P:DIM], ident[0:H0, 0:H0])
                mm.then_inc(s_trf, 1)

            def product(n, r, t, first=0, last=6):
                o = bank(t)
                if first == 0:
                    if t == 0:
                        pe.wait_ge(s_trf_copied, 2 * (n + 1))
                    if t == BC:
                        pe.wait_ge(s_x, n + 1)
                    if t in (Z, Z + 1):
                        need(pe, s_h, min(n + 2, PAIRS) if isinstance(n, int) else n + 2)
                    elif t == Z + 2:
                        need(pe, s_lg, n - 1)
                        pe.wait_ge(s_gev, 10 * n + Z)
                    else:
                        need(pe, s_gev, 10 * n + t)
                if t < BC:
                    c = slice(t * P, (t + 1) * P)
                    for k in range(first, last):
                        if k < TAPS:
                            mm = pe.matmul(o[:, 0:N2], v_lo[:, k, c], t_lo[:, :, k:k + L], start=(k == 0), stop=False)
                        else:
                            k2 = k - TAPS
                            mm = pe.matmul(o[:, 0:N2], v_hi[:, k2, c], t_hi[:, :, 2 * k2:2 * k2 + L], start=False,
                                           stop=(k2 == 1))
                elif t == BC:
                    for k in range(MB):
                        mm = pe.matmul(o[:, 0:N2], wx[:, k].rearrange("p c n -> p (c n)"), xz[r][:, k, :], start=(k == 0),
                                       stop=(k == MB - 1))
                elif t < Z:
                    for k in range(MB):
                        mm = pe.matmul(o[:, 0:N2], wdt[:, k, (t - DT) * P:(t - DT + 1) * P], xz[r][:, k, :],
                                       start=(k == 0), stop=(k == MB - 1))
                else:
                    c = slice((t - Z) * P, (t - Z + 1) * P)
                    pe.matmul(o[:, 0:N2], wz_lo[:, c], t_lo[:, :, 1:L + 1], start=True, stop=False)
                    mm = pe.matmul(o[:, 0:N2], wz_hi[:, c], t_hi[0:DLO, :, 1:L + 1], start=False, stop=True)
                if last == 6:
                    mm.then_inc(s_gmm, 1)

            def spread_b(n, r, s):
                if s == 0:
                    pe.wait_ge(s_bc3, n + 1)
                need(pe, s_bx, NS * n + s)
                pe.matmul(ps_b[:, 0:N2], pick[:, s, :], bc3[r], start=True, stop=True).then_inc(s_bb, 1)

            def spread_c(n, r, s):
                need(pe, s_mul, NS * n + s)
                pe.matmul(ps_c[:, 0:N2], pick[:, NS + s, :], bc3[r], start=True, stop=True).then_inc(s_cb, 1)

            def state_sum(n, s):
                if s == 0:
                    need(pe, s_yev, MB * n)
                pe.wait_ge(s_mul, NS * n + s + 1)
                for m in range(MB):
                    mm = pe.matmul(ps_y[m][:, 0:N2], ident[:, :], hb[s % B_BUFS][:, m, :], start=(s == 0),
                                   stop=(s == NS - 1))
                mm.then_inc(s_ysum, 1)

            def out_product(n, b):
                if b == 0:
                    pe.wait_ge(s_ysz, n + 1)
                    if isinstance(n, int) and n >= PAIRS - 2:
                        pe.wait_ge(s_gev, 10 * PAIRS)
                        pe.wait_ge(s_opread, n)
                    else:
                        pe.wait_ge(s_trf_copied, 2 * (n + 3))
                for f in range(2):
                    c = b * L + f * HSTEP
                    for k in range(MB):
                        mm = pe.matmul(ps_k[b][0:H0, f * DIM:(f + 1) * DIM], y[:, k, c:c + H0], wout[:, k, :],
                                       start=(k == 0), stop=(k == MB - 1))
                mm.then_inc(s_opmm, 1)

            def back_t(n, r, b):
                if b == 0:
                    pe.wait_ge(s_rows, n + 1)
                    pe.wait_ge(s_gev, min(10 * (n + 2) + Z, 10 * PAIRS) if isinstance(n, int) else 10 * (n + 2) + Z)
                need(pe, s_trb_copied, 2 * n + b)
                for f in range(2):
                    src = rows[r][:, 2 * b + f, DIM:2 * DIM]
                    pe.transpose(ps_t[:, f * H0:(f + 1) * H0], src[:, 0:P], ident[0:H0, 0:H0])
                    mm = pe.transpose(ps_t[0:DLO, (2 + f) * H0:(3 + f) * H0], src[:, P:DIM], ident[0:H0, 0:H0])
                mm.then_inc(s_trb, 1)

            def router(n):
                pe.wait_ge(s_trb_copied, 2 * (n + 1))
                for c in range(4):
                    o = ps_t[0:H0, c * E:(c + 1) * E]
                    pe.matmul(o, h2_lo[:, c, :], sww_lo[:, :], start=True, stop=False)
                    mm = pe.matmul(o, h2_hi[:, c, :], sww_hi[:, :], start=False, stop=True)
                mm.then_inc(s_lgmm, 1)

            def body(i, r, front, tokens):
                back = not isinstance(i, int) or i >= 1
                o = 1 - r
                n = i + 1
                for j in range(NS):
                    if back and j == 2:
                        out_product(i - 1, 0)
                    if back and j == 3:
                        out_product(i - 1, 1)
                    if back and j == 14:
                        router(i - 1)
                    if front:
                        for args in {0: ((0, 0, 3),), 1: ((0, 3, 6),), 2: ((1, 0, 1),), 3: ((1, 1, 2),), 4: ((1, 2, 6),),
                                     5: ((2, 0, 3),), 6: ((2, 3, 6),), 8: ((BC,),), 9: ((DT,),), 10: ((DT + 1,),),
                                     11: ((DT + 2,),), 14: ((Z,), (Z + 1,)), 15: ((Z + 2,),)}.get(j, ()):
                            product(n, o, *args)
                    if tokens:
                        for args in {7: ((0, 0, 8),), 8: ((0, 8, 10),), 9: ((0, 10, 12),), 10: ((1, 0, 2),),
                                     11: ((1, 2, 4),), 12: ((1, 4, 12),)}.get(j, ()):
                            tok(i + 2, *args)
                    if back and j == 12:
                        back_t(i - 1, o, 0)
                    if back and j == 13:
                        back_t(i - 1, o, 1)
                    if tokens and j == 15:
                        front_t(i + 2, 0)
                        front_t(i + 2, 1)
                    if j + 2 < NS:
                        spread_b(i, r, j + 2)
                    elif front:
                        spread_b(n, o, j + 2 - NS)
                    if j + 1 < NS:
                        spread_c(i, r, j + 1)
                    elif front:
                        spread_c(n, o, 0)
                    state_sum(i, j)

            pe.wait_ge(s_const, 16 * CONSTS)
            pe.wait_ge(s_pool0, 3)
            pe.wait_ge(s_dve0, CLEAR)
            pe.wait_ge(s_vcopy, VPROD + 2)
            tok(0, 0, 0, 2 * KP)
            tok(0, 1, 0, 2 * KP)
            front_t(0, 0)
            front_t(0, 1)
            tok(1, 0, 0, 2 * KP)
            tok(1, 1, 0, 2 * KP)
            for t in range(10):
                product(0, 0, t)
            front_t(1, 0)
            front_t(1, 1)
            spread_b(0, 0, 0)
            spread_c(0, 0, 0)
            spread_b(0, 0, 1)
            for i in range(4):
                body(i, i % 2, True, True)
            with pe.Fori(4, PAIRS - 3, 2) as i:
                body(i, 0, True, True)
                body(i + 1, 1, True, True)
            body(PAIRS - 2, 0, True, False)
            body(PAIRS - 1, 1, False, False)
            n = PAIRS - 1
            out_product(n, 0)
            out_product(n, 1)
            back_t(n, 1, 0)
            back_t(n, 1, 1)
            router(n)

            def rank(src):
                for half in range(2):
                    v = src.rearrange("p e c -> p (e c)")[:, half * 512:(half + 1) * 512]
                    pe.matmul(ps_k[half][0:H0, :], before, v, start=True, stop=True)
                    mm = pe.matmul(ps_g[half][0:H0, :], every, v, start=True, stop=True)
                mm.then_inc(s_ranked, 1)

            pe.wait_ge(s_pool0, 3 + POOL_SET + 2)
            pe.wait_ge(s_lg, PAIRS)
            pe.wait_ge(s_ohr, 1)
            rank(oh)
            with pe.Fori(0, BISECT, 1) as t:
                pe.wait_ge(s_cnt, t + 1)
                pe.matmul(ps_y[0][0:H0, 0:E], every, cnt, start=True, stop=True).then_inc(s_bis, 1)
            pe.wait_ge(s_cnt, BISECT + 1)
            pe.matmul(ps_y[0][0:H0, 0:E], every, cnt, start=True, stop=True).then_inc(s_bis, 1)
            pe.wait_ge(s_tie, 1)
            rank(sel)

            def tile_t(k, g):
                pe.wait_ge(s_gat[g], 64 * ((k - g) // GRING + 1) if isinstance(k, int) else 64 // GRING * (k - g) + 64)
                need(pe, s_mtc, k)
                for f in range(2):
                    pe.transpose(ps_t[:, f * P:(f + 1) * P], grow[g][:, f, DIM:DIM + P], ident[:, :])
                    mm = pe.transpose(ps_t[0:DLO, TS + f * P:TS + (f + 1) * P], grow[g][:, f, DIM + P:2 * DIM], ident[:, :])
                mm.then_inc(s_mtr, 1)

            def hidden(k, r):
                pe.wait_ge(s_w[r], 48 * ((k - r) // 2 + 1) if isinstance(k, int) else 24 * (k - r) + 48)
                pe.wait_ge(s_mtc, k + 1)
                for f in range(KF):
                    o = (ps_y + ps_g[0:1])[f % 4][:, 0:TS]
                    need(pe, s_hid, KF * k + f - 3)
                    c = slice(f * P, (f + 1) * P)
                    pe.matmul(o, wp[r][:, c], g_lo[r], start=True, stop=False)
                    pe.matmul(o, w1h[r][:, c], g_hi[r], start=False, stop=True).then_inc(s_m1, 1)

            def expert_out(k, r):
                w2 = wp[r][:, FF:FF + KF * DIM].rearrange("p (f d) -> p f d", f=KF)
                need(pe, s_mbias, k)
                for f in range(2):
                    for c in range(KF):
                        if f == 0:
                            pe.wait_ge(s_hid, KF * k + c + 1)
                        mm = pe.matmul(ps_k[f][:, 0:DIM], hid[r][:, c, f * P:(f + 1) * P], w2[:, c, :], start=(c == 0),
                                       stop=(c == KF - 1))
                    mm.then_inc(s_m2, 1)

            pe.wait_ge(s_gate, 1)

            def ring(k, tiles=GRING):
                for g in range(tiles):
                    hidden(k + g, g % 2)
                    if g + 1 < tiles or tiles == GRING:
                        tile_t(k + g + 1, (g + 1) % GRING)
                    expert_out(k + g, g % 2)

            tile_t(0, 0)
            ring(0)
            with pe.Fori(GRING, FULL - GRING + 1, GRING) as k:
                ring(k)
            ring(FULL, TILES - FULL)

        @block.vector
        def _(dve):
            dve.memset(patches[:, :, :, 0:1], 0.0).then_inc(s_dve0, 1)
            dve.memset(t_lo[:, :, :], 0.0).then_inc(s_dve0, 1)
            dve.memset(t_hi[:, :, :], 0.0).then_inc(s_dve0, 1)
            for b in range(A_BUFS):
                ins = dve.memset(decay[b][:, :, :, 0:1], 0.0)
            ins.then_inc(s_dve0, 1)
            n = 0
            for k in range(TAPS):
                dve.wait_ge(s_vmm, n + 1)
                dve.tensor_copy(v_lo[:, k, :], ps_g[n % 2][:, 0:INNER]).then_inc(s_vcopy, 1)
                n += 1
                dve.wait_ge(s_vmm, n + 1)
                o = v_hi[0:DLO, k // 2, :] if k % 2 == 0 else v_hi[DLO:P, k // 2, :]
                dve.tensor_copy(o, ps_g[n % 2][0:DLO, 0:INNER]).then_inc(s_vcopy, 1)
                n += 1
            dve.wait_ge(s_const, 16 * CONSTS)
            dve.wait_ge(s_clsrow, 16)
            dve.memset(rows[0][:, :, :], 0.0).then_inc(s_vcopy, 1)
            dve.memset(rows[1][:, :, :], 0.0).then_inc(s_vcopy, 1)
            dve.memset(pick[:, :, :], 0.0).then_inc(s_pick, 1)
            dve.wait_ge(s_pool0, 3)
            dve.wait_ge(s_pick, 1)
            for q in PIECES:
                v = slice(q * 2 * NS, (q + 1) * 2 * NS)
                ins = dve.tensor_copy(pick[v, :, :], ident[v, v].unsqueeze(2).to_broadcast([2 * NS, 2 * NS, P]))
            ins.then_inc(s_dve0, 1)

            def embed(n, r):
                need(dve, s_hres, n - 1)
                for b in range(2):
                    dve.wait_ge(s_tokmm, 2 * n + b + 1)
                    ins = dve.tensor_tensor(h[r][:, 2 * b:2 * b + 2, :], ps_k[b][0:H0, 0:2 * DIM].rearrange(
                        "p (f d) -> p f d", f=2), tok_bias[:, :, :], ALU.add)
                ins.then_inc(s_h, 1)

            def stats(n, src, st, mv, s_in, s_st, s_mv, s_ve):
                if s_in is not None:
                    dve.wait_ge(s_in, n + 1)
                for c in range(4):
                    ins = dve.bn_stats(st[:, c, :], src(c))
                ins.then_inc(s_st, 1)
                dve.wait_ge(s_clsrow, 16)
                dve.wait_ge(s_st, n + 1)
                for c in range(4):
                    ins = dve.bn_aggr(mv[:, c, :], st[:, c, :])
                ins.then_inc(s_mv, 1)
                dve.wait_ge(s_mv, n + 1)
                dve.tensor_scalar(mv[:, :, 1], mv[:, :, 1], EPS, None, ALU.add).then_inc(s_ve, 1)

            def normalise(n, dst, src, mv, rs, s_rs, s_out):
                dve.wait_ge(s_rs, n + 1)
                for c in range(4):
                    ins = dve.tensor_scalar(dst(c), src(c), mv[:, c, 0:1], rs[:, c:c + 1], ALU.subtract, ALU.mult)
                ins.then_inc(s_out, 1)

            def front_stats(n, r):
                embed(n, r)
                stats(n, lambda c: h[r][:, c, :], st1, mv1, s_h, s_st1, s_mv1, s_ve1)

            def front_norm(n, r):
                need(dve, s_trf, 2 * n)
                normalise(n, lambda c: hn[:, c, :], lambda c: h[r][:, c, :], mv1, rs1, s_rs1, s_hn)

            def bx(n, r, s):
                if s == 0:
                    dve.wait_ge(s_du, n + 1)
                dve.wait_ge(s_bb, NS * n + s + 1)
                need(dve, s_ysum, NS * n + s - B_BUFS + 1)
                dve.tensor_tensor(hb[s % B_BUFS][:, :, :], du[r][:, :, :],
                                  ps_b[:, 0:N2].unsqueeze(1).to_broadcast([P, MB, N2]), ALU.mult).then_inc(s_bx, 1)

            def scan(n, s):
                b, a = s % B_BUFS, s % A_BUFS
                dve.wait_ge(s_a, NS * n + s + 1)
                dve.wait_ge(s_bx, NS * n + s + 1)
                v = hb[b].rearrange("p m t -> p (m t)")
                dve.tensor_tensor_scan(v, decay[a].rearrange("p m b t -> p (m b t)"), v, 0.0, ALU.mult,
                                       ALU.add).then_inc(s_scan, 1)

            def times_c(n, s):
                dve.wait_ge(s_scan, NS * n + s + 1)
                dve.wait_ge(s_cb, NS * n + s + 1)
                dve.tensor_tensor(hb[s % B_BUFS][:, :, :], hb[s % B_BUFS][:, :, :],
                                  ps_c[:, 0:N2].unsqueeze(1).to_broadcast([P, MB, N2]), ALU.mult).then_inc(s_mul, 1)

            def split_bc(n, r, step):
                half, last = slice(DLO, P), slice(P - 2 * NS, P)
                if step == 0:
                    dve.wait_ge(s_gev, 10 * n + BC + 1)
                    dve.tensor_tensor(bcf[half], bcf[half], bc3[r][half], ALU.subtract).then_inc(s_bcrest, 1)
                elif step == 1:
                    dve.wait_ge(s_bcrest, n + 1)
                    dve.tensor_copy(bc3[r][half], bcf[half]).then_inc(s_bcmid, 1)
                else:
                    dve.wait_ge(s_bcmid, n + 1)
                    dve.tensor_tensor(bc3[r][last], bcf[last], bc3[r][last], ALU.subtract).then_inc(s_bc3, 1)

            def take_y(n, r, m):
                dve.wait_ge(s_ysum, NS * (n + 1))
                if m == 0:
                    need(dve, s_opmm, 2 * n)
                dve.scalar_tensor_tensor(out=y[:, m, :], in0=xz[r][:, m, :], scalar=dsk[:, m:m + 1],
                                         in1=ps_y[m][:, 0:N2], op0=ALU.mult, op1=ALU.add).then_inc(s_yev, 1)

            def o_tile(c):
                return ps_k[c // 2][0:H0, (c % 2) * DIM:(c % 2 + 1) * DIM]

            def out_stats(n):
                dve.wait_ge(s_opmm, 2 * (n + 1))
                stats(n, o_tile, st2, mv2, None, s_st2, s_mv2, s_ve2)

            def out_norm(n, r):
                need(dve, s_stored[r], 16 * (n - r))
                need(dve, s_trb, 2 * (n - 1))
                normalise(n, lambda c: rows[r][:, c, 0:DIM], o_tile, mv2, rs2, s_rs2, s_opread)
                dve.wait_ge(s_opread, n + 1)
                v = rows[r][:, :, 0:DIM]
                dve.tensor_tensor(v, v, gam[:, :].unsqueeze(1).to_broadcast([H0, 4, DIM]), ALU.mult).then_inc(s_gam, 1)

            def row_stats(n, r):
                stats(n, lambda c: rows[r][:, c, 0:DIM], st3, mv3, s_h2, s_st3, s_mv3, s_ve3)

            def row_norm(n, r):
                normalise(n, lambda c: rows[r][:, c, DIM:2 * DIM], lambda c: rows[r][:, c, 0:DIM], mv3, rs3, s_rs3, s_rows)

            def take_logits(n):
                dve.wait_ge(s_lgmm, n + 1)
                dve.tensor_tensor(logits[:, ds(4 * n, 4), :], ps_t[0:H0, 0:4 * E].rearrange("p (c e) -> p c e", c=4),
                                  swb[:, :].unsqueeze(1).to_broadcast([H0, 4, E]), ALU.add).then_inc(s_lg, 1)

            def softplus_t(n):
                dve.wait_ge(s_spe, n + 1)
                need(dve, s_delta, n)
                dve.tensor_scalar(spt[:, :, :], spe[:, :, :], 1.0, -1.0, ALU.add, ALU.add).then_inc(s_spt, 1)

            def softplus_sum(n, r):
                dve.wait_ge(s_spl, n + 1)
                dve.scalar_tensor_tensor(out=spv[:, :, :].rearrange("p a b -> p (a b)"),
                                         in0=spv[:, :, :].rearrange("p a b -> p (a b)"), scalar=0.0,
                                         in1=spl[:, :, :].rearrange("p a b -> p (a b)"), op0=ALU.max,
                                         op1=ALU.add).then_inc(s_spd, 1)
                dve.wait_ge(s_spd, n + 1)
                dve.wait_ge(s_spc, n + 1)
                need(dve, s_a, NS * (n - 1))
                dve.tensor_tensor(delta[r][:, :, :], spv[:, :, :], spt[:, :, :], ALU.add).then_inc(s_delta, 1)

            def body(i, r, front, tokens):
                back = not isinstance(i, int) or i >= 1
                o = 1 - r
                for j in range(NS):
                    scan(i, j)
                    if j + 1 < NS:
                        bx(i, r, j + 1)
                    elif front:
                        bx(i + 1, o, 0)
                    times_c(i, j)
                    if back:
                        if j == 0:
                            for m in range(MB):
                                take_y(i - 1, o, m)
                        if j == 4:
                            out_stats(i - 1)
                        if j == 5:
                            out_norm(i - 1, o)
                        if j == 7:
                            row_stats(i - 1, o)
                        if j == 8:
                            row_norm(i - 1, o)
                        if j == 14:
                            take_logits(i - 1)
                    if front:
                        if 9 <= j < 12:
                            split_bc(i + 1, o, j - 9)
                        if j == 12:
                            softplus_t(i + 1)
                        if j == 13:
                            softplus_sum(i + 1, o)
                    if tokens and j == 13:
                        front_stats(i + 2, r)
                    if tokens and j == 14:
                        front_norm(i + 2, r)

            front_stats(0, 0)
            front_norm(0, 0)
            front_stats(1, 1)
            for step in range(3):
                split_bc(0, 0, step)
            softplus_t(0)
            softplus_sum(0, 0)
            front_norm(1, 1)
            bx(0, 0, 0)
            for i in range(4):
                body(i, i % 2, True, True)
            with dve.Fori(4, PAIRS - 3, 2) as i:
                body(i, 0, True, True)
                body(i + 1, 1, True, True)
            body(PAIRS - 2, 0, True, False)
            body(PAIRS - 1, 1, False, False)
            n = PAIRS - 1
            for m in range(MB):
                take_y(n, 1, m)
            out_stats(n)
            out_norm(n, 1)
            row_stats(n, 1)
            row_norm(n, 1)
            take_logits(n)

            steps = [0]

            def link(ins):
                steps[0] += 1
                ins.then_inc(s_d, 1)
                dve.wait_ge(s_d, steps[0])

            def by_column(v):
                return v.unsqueeze(1).to_broadcast([H0, E, COLS])

            def by_expert(v):
                return v.unsqueeze(2).to_broadcast([H0, E, COLS])

            def last(v):
                return v.unsqueeze(2).to_broadcast([H0, COLS, E])

            dve.wait_ge(s_stored[0], 16 * PAIRS)
            dve.wait_ge(s_stored[1], 16 * PAIRS)
            dve.wait_ge(s_pool0, 3 + POOL_SET + 2)
            dve.wait_ge(s_lg, PAIRS)
            link(dve.tensor_reduce(exv, logits[:, :, :], AX.X, ALU.max))
            dve.tensor_tensor(ex, logits[:, :, :], last(exv), ALU.subtract).then_inc(s_exin, 1)
            dve.wait_ge(s_exout, 1)
            link(dve.tensor_reduce(exv, ex, AX.X, ALU.max))
            link(dve.tensor_reduce(rsum, ex, AX.X, ALU.add))
            link(dve.reciprocal(rsum, rsum))
            link(dve.tensor_tensor(prob, exv, rsum, ALU.mult))
            sel_c = sel.rearrange("p e c -> p (e c)").rearrange("p (c e) -> p c e", e=E)
            link(dve.tensor_tensor(sel_c, ex, last(exv), ALU.is_ge))
            link(dve.tensor_tensor(sel_c, sel_c, weights8.unsqueeze(1).to_broadcast([H0, COLS, E]), ALU.mult))
            link(dve.tensor_reduce(vmax, sel_c, AX.X, ALU.max))
            link(dve.tensor_tensor(oh, sel_c.rearrange("p c e -> p e c"), by_column(vmax), ALU.is_equal))
            link(dve.tensor_tensor(oh, oh, by_column(valid), ALU.mult))
            dve.tensor_tensor(member, oh, by_column(prob), ALU.mult).then_inc(s_ohr, 1)

            def ranks(times):
                dve.wait_ge(s_ranked, times)
                for e in range(E):
                    c = (e % 4) * COLS
                    ins = dve.tensor_tensor_scan(tot[:, e, :], one_cols, ps_g[e // 4][0:H0, c:c + COLS], 0.0, ALU.mult,
                                                 ALU.add)
                link(ins)
                for half in range(2):
                    v = slice(half * 4, half * 4 + 4)
                    ins = dve.tensor_tensor(place[:, v, :], tot[:, v, :], ps_g[half][0:H0, :].rearrange(
                        "p (e c) -> p e c", e=4), ALU.subtract)
                link(ins)
                for half in range(2):
                    v = slice(half * 4, half * 4 + 4)
                    ins = dve.tensor_tensor(place[:, v, :], place[:, v, :], ps_k[half][0:H0, :].rearrange(
                        "p (e c) -> p e c", e=4), ALU.add)
                link(ins)

            ranks(1)
            link(dve.tensor_copy(n_i, tot[:, :, COLS - 1]))
            link(dve.tensor_copy(n_e, n_i))
            link(dve.tensor_scalar(n_e, n_e, float(TS - 1), None, ALU.add))
            link(dve.tensor_copy(n_i, n_e))
            link(dve.tensor_scalar(n_i, n_i, TS.bit_length() - 1, None, ALU.logical_shift_right))
            link(dve.tensor_copy(tiles_e, n_i))
            link(dve.tensor_tensor_scan(tile_end, one_cols[:, 0:E], tiles_e, 0.0, ALU.mult, ALU.add))
            link(dve.tensor_tensor(base_e, tile_end, tiles_e, ALU.subtract))
            link(dve.tensor_scalar(base_e, base_e, float(TS), None, ALU.mult))
            link(dve.tensor_tensor(place, place, by_expert(base_e), ALU.add))
            link(dve.tensor_tensor(place, place, oh, ALU.mult))
            link(dve.tensor_reduce(destf, place.rearrange("p e c -> p c e"), AX.X, ALU.add))
            link(dve.tensor_copy(desti, destf))
            link(dve.tensor_scalar(dlo_i, desti, P - 1, None, ALU.bitwise_and))
            link(dve.tensor_scalar(dhi_i, desti, P.bit_length() - 1, None, ALU.logical_shift_right))
            link(dve.tensor_copy(destf, dlo_i))
            link(dve.tensor_copy(vmax, dhi_i))
            link(dve.scalar_tensor_tensor(out=destf, in0=destf, scalar=float(SC), in1=vmax, op0=ALU.mult, op1=ALU.add))
            link(dve.tensor_scalar(vmax, valid, -65536.0, 65536.0, ALU.mult, ALU.add))
            link(dve.tensor_tensor(destf, destf, vmax, ALU.add))
            link(dve.tensor_copy(desti, destf))

            link(dve.tensor_tensor(tile_cmp, tile_no.unsqueeze(2).to_broadcast([1, TILES, E]),
                                   tile_end[0:1, :].unsqueeze(1).to_broadcast([1, TILES, E]), ALU.is_ge))
            link(dve.tensor_reduce(tile_no, tile_cmp, AX.X, ALU.add))
            link(dve.tensor_scalar(tile_no, tile_no, float(E - 1), None, ALU.min))
            dve.tensor_copy(tile_ex, tile_no).then_inc(s_tex, 1)

            def batch(t, r):
                need(dve, s_scat[r], 16 * 8 * ((t - r) // 2) if isinstance(t, int) else 64 * (t - r))
                dve.tensor_copy(sidx[r], desti[:, ds(t * 8, 8)])
                dve.tensor_copy(sval[r], ids[:, ds(t * 8, 8)]).then_inc(s_dest[r], 1)

            batch(0, 0)
            batch(1, 1)

            dve.memset(lo_t, 0.0).then_inc(s_d, 1)
            dve.memset(hi_t, 2.0).then_inc(s_d, 1)
            steps[0] += 2
            dve.wait_ge(s_d, steps[0])
            base = steps[0]
            PER = 5

            def halve(t):
                c = [base + PER * t]

                def chain(ins):
                    c[0] = c[0] + 1
                    ins.then_inc(s_d, 1)
                    dve.wait_ge(s_d, c[0])

                chain(dve.tensor_tensor(mid_t, lo_t, hi_t, ALU.add))
                chain(dve.tensor_scalar(mid_t, mid_t, 0.5, None, ALU.mult))
                chain(dve.tensor_tensor(sel, member, by_expert(mid_t), ALU.is_ge))
                dve.tensor_reduce(cnt, sel, AX.X, ALU.add).then_inc(s_cnt, 1)
                dve.wait_ge(s_bis, t + 1)
                total = ps_y[0][0:H0, 0:E]
                dve.scalar_tensor_tensor(out=lo_c, in0=total, scalar=float(CAP), in1=mid_t, op0=ALU.is_ge, op1=ALU.mult)
                chain(dve.scalar_tensor_tensor(out=hi_c, in0=total, scalar=float(CAP), in1=mid_t, op0=ALU.is_ge,
                                               op1=ALU.add))
                dve.tensor_tensor(lo_t, lo_t, lo_c, ALU.max)
                chain(dve.tensor_tensor(hi_t, hi_t, hi_c, ALU.min))

            halve(0)
            HALF = COLS // 8
            with dve.Fori(1, HALF // 2, 1) as t:
                halve(t)
                batch(2 * t, 0)
                batch(2 * t + 1, 1)
            with dve.Fori(HALF // 2, BISECT, 1) as t:
                halve(t)
            steps[0] = base + PER * BISECT

            link(dve.tensor_tensor(sel, member, by_expert(lo_t), ALU.is_gt))
            dve.tensor_reduce(cnt, sel, AX.X, ALU.add).then_inc(s_cnt, 1)
            dve.wait_ge(s_bis, BISECT + 1)
            link(dve.tensor_scalar(room, ps_y[0][0:H0, 0:E], -1.0, float(CAP), ALU.mult, ALU.add))
            link(dve.tensor_tensor(sel, member, by_expert(lo_t), ALU.is_equal))
            dve.tensor_tensor(sel, sel, oh, ALU.mult).then_inc(s_tie, 1)
            ranks(2)
            link(dve.tensor_tensor(place, place, by_expert(room), ALU.is_lt))
            link(dve.tensor_tensor(place, place, sel, ALU.mult))
            link(dve.tensor_tensor(sel, member, by_expert(lo_t), ALU.is_gt))
            link(dve.tensor_tensor(place, place, sel, ALU.add))
            link(dve.tensor_reduce(vmax, place.rearrange("p e c -> p c e"), AX.X, ALU.add))
            link(dve.tensor_tensor(gates[:, :, 0], prob, vmax, ALU.mult))
            link(dve.tensor_scalar(vmax, vmax, -1.0, 1.0, ALU.mult, ALU.add))
            dve.tensor_tensor(gates[:, :, 1], prob, vmax, ALU.mult).then_inc(s_gate, 1)

            def gather_ids(k, g):
                if isinstance(k, int) and k < GRING:
                    done = s_gidx0
                else:
                    done = s_gidx[g]
                    dve.wait_ge(s_mtr, k - GRING + 1)
                dve.tensor_copy(gidx[g], slot_id[:, ds(2 * k, 2)]).then_inc(done, 1)

            def kept_input(k, g, r):
                dve.wait_ge(s_gat[g], 64 * ((k - g) // GRING + 1) if isinstance(k, int) else 64 // GRING * (k - g) + 64)
                for f in range(2):
                    ins = dve.scalar_tensor_tensor(out=mt[r][:, f, :], in0=grow[g][:, f, DIM:2 * DIM],
                                                   scalar=ggate[g][:, f, 1:2], in1=grow[g][:, f, 0:DIM], op0=ALU.mult,
                                                   op1=ALU.add)
                ins.then_inc(s_keepx, 1)

            def finish(k, g, r):
                need(dve, s_put[r], 32 * ((k - r) // 2) if isinstance(k, int) else 16 * (k - r))
                dve.tensor_copy(pidx[r], gidx[g])
                dve.wait_ge(s_w[r], 48 * ((k - r) // 2 + 1) if isinstance(k, int) else 24 * (k - r) + 48)
                for f in range(2):
                    dve.wait_ge(s_m2, 2 * k + f + 1)
                    ins = dve.tensor_tensor(mo[r][:, f, :], ps_k[f][:, 0:DIM], b2r[r], ALU.add)
                ins.then_inc(s_mbias, 1)
                dve.wait_ge(s_mbias, k + 1)
                dve.wait_ge(s_keepx, k + 1)
                for f in range(2):
                    ins = dve.scalar_tensor_tensor(out=mo[r][:, f, :], in0=mo[r][:, f, :], scalar=ggate[g][:, f, 0:1],
                                                   in1=mt[r][:, f, :], op0=ALU.mult, op1=ALU.add)
                ins.then_inc(s_mo[g], 1)

            dve.wait_ge(s_slot, 16)
            for g in range(GRING):
                gather_ids(g, g)

            def tile(k, g, more):
                kept_input(k, g, g % 2)
                finish(k, g, g % 2)
                if more:
                    gather_ids(k + GRING, g)

            for g in range(GRING):
                tile(g, g, True)
            with dve.Fori(GRING, FULL - 2 * GRING + 1, GRING) as k:
                for g in range(GRING):
                    tile(k + g, g, True)
            for t in range(FULL - GRING, TILES):
                tile(t, t % GRING, t + GRING < TILES)


def kernel(x, cls_tok, L0_tok_W, L0_tok_b, L0_attn_W_in, L0_attn_conv_w, L0_attn_conv_b, L0_attn_W_x, L0_attn_W_dt,
           L0_attn_b_dt, L0_attn_A_log, L0_attn_D, L0_attn_W_out, L0_attn_gamma, L0_attn_beta, L0_ffn_switch_w,
           L0_ffn_switch_b, L0_ffn_w1, L0_ffn_b1, L0_ffn_w2, L0_ffn_b2):
    import numpy as np
    import concourse.bacc as bacc
    from concourse.bass_utils import run_bass_kernel_spmd

    a = np.asarray

    def blocks(w, k):
        return a(w).reshape(k, P, -1).transpose(1, 0, 2)

    def column(v, k):
        return a(v).reshape(k, P).T

    w_in = a(L0_attn_W_in)
    w1, w2 = a(L0_ffn_w1), a(L0_ffn_w2)
    w_pack = np.concatenate([
        w1[:, 0:P, :],
        w2.reshape(E, KF, P, DIM).transpose(0, 2, 1, 3).reshape(E, P, KF * DIM),
        a(L0_ffn_b1).reshape(E, KF, P).transpose(0, 2, 1),
    ], axis=2)
    side = 14
    xt = a(x).reshape(PAIRS, 2, 3, side, 16, side, 16).transpose(0, 2, 4, 6, 1, 3, 5)
    xt = xt.reshape(PAIRS, KP, P, 2, PATCHES).transpose(0, 2, 1, 3, 4)
    arrays = {
        "x": xt,
        "cls_tok": a(cls_tok).reshape(1, DIM),
        "tok_w": blocks(a(L0_tok_W).T, KP),
        "tok_b": a(L0_tok_b),
        "w_inx": blocks(w_in[:, 0:INNER].T, MB),
        "w_zlo": w_in[0:P, INNER:],
        "w_zhi": w_in[P:DIM, INNER:],
        "conv_w": a(L0_attn_conv_w).reshape(TAPS, MB, P, INNER).transpose(2, 0, 1, 3),
        "conv_b": column(L0_attn_conv_b, MB),
        "w_x": blocks(L0_attn_W_x, MB),
        "w_dt": blocks(L0_attn_W_dt, MB),
        "b_dt": column(L0_attn_b_dt, MB),
        "a_log": blocks(L0_attn_A_log, MB),
        "d_skip": column(L0_attn_D, MB),
        "w_out": blocks(L0_attn_W_out, MB),
        "gamma": a(L0_attn_gamma),
        "beta": a(L0_attn_beta),
        "sw_w": a(L0_ffn_switch_w),
        "sw_b": a(L0_ffn_switch_b),
        "w_pack": w_pack,
        "w1_hi": w1[:, P:DIM, :],
        "b2": a(L0_ffn_b2),
    }
    arrays = {f"in_{k}": np.ascontiguousarray(v) for k, v in arrays.items()}
    nc = bacc.Bacc("TRN2", target_bir_lowering=False, num_devices=1)
    args = [nc.dram_tensor(k, v.shape, F32, kind="ExternalInput").ap() for k, v in arrays.items()]
    out = nc.dram_tensor("out_tokens", (TOK, DIM), F32, kind="ExternalOutput").ap()
    build(nc, *args, out)
    r = run_bass_kernel_spmd(nc, [arrays], core_ids=[0])
    return r.results[0]["out_tokens"].reshape(IMAGES, L, DIM)
```

```python
from contextlib import ExitStack

import concourse.bass as bass
from concourse import mybir

F32 = mybir.dt.float32
I32 = mybir.dt.int32
BF16 = mybir.dt.bfloat16
U32 = mybir.dt.uint32
ALU = mybir.AluOpType
ACT = mybir.ActivationFunctionType
AX = mybir.AxisListType
ds = bass.ds

P = 128
IMAGES = 64
PAIRS = IMAGES // 2
PATCHES = 196
L = PATCHES + 1
TOK = IMAGES * L
N2 = 2 * L
H0 = 99
HSTEP = L - H0
DIM = 192
DLO = DIM - P
PD = 768
KP = PD // P
INNER = 384
MB = INNER // P
NS = 16
LEAD = 3
TAPS = 4
E = 8
FF = 768
KF = FF // P
CAP = int(1.25 * TOK / E)
COLS = 2 * IMAGES
TS = 256
TILES = TOK // TS + E
SLOTS = TILES * TS
GRING = 4
FULL = TILES // GRING * GRING
SC = SLOTS // P
NOBODY = 1 << 15
BISECT = 29
EPS = 1e-5
A_BUFS, B_BUFS = 4, 8
FOLDED = range(6)
SUMS = NS - len(FOLDED)
C_ON_POOL = (0, 2, 4, 6, 8, 10)
C_ON_DVE = tuple(s for s in range(NS) if s not in C_ON_POOL)
PIECES = (0, 2, 3)
POOL_SET = 8 + 2 * GRING


def need(eng, sem, count):
    if not isinstance(count, int) or count > 0:
        eng.wait_ge(sem, count)


def sums_until(s):
    return s + 1 - sum(1 for k in FOLDED if 2 * k <= s)


def build(nc, x, cls_tok, tok_w, tok_b, w_inx, w_zlo, w_zhi, conv_w, conv_b, w_x, w_dt, b_dt, a_log, d_skip, w_out, gamma,
          beta, sw_w, sw_b, w_pack, w1_hi, b2, out):
    rows_dram = nc.dram_tensor("rows_scratch", (TOK, 2 * DIM), F32, kind="Internal").ap()
    slot_dram = nc.dram_tensor("slot_scratch", (SLOTS, 1), I32, kind="Internal").ap()
    gate_dram = nc.dram_tensor("gate_scratch", (TOK, 2), F32, kind="Internal").ap()

    with ExitStack() as ctx:
        def sb(name, shape, dt=F32):
            return ctx.enter_context(nc.sbuf_tensor(name, shape, dt))

        def sem(name):
            return ctx.enter_context(nc.semaphore(name))

        ident = sb("ident", [P, P])
        wtok = sb("wtok", [P, KP, DIM])
        v_lo = sb("v_lo", [P, TAPS, INNER])
        v_hi = sb("v_hi", [P, 2, INNER])
        wz_lo = sb("wz_lo", [P, INNER])
        wz_hi = sb("wz_hi", [DLO, INNER])
        wx = sb("wx", [P, MB, 4, 2 * NS])
        pick = sb("pick", [P, 2 * NS, P], BF16)
        wdt = sb("wdt", [P, MB, INNER])
        wout = sb("wout", [P, MB, DIM])
        cb = sb("cb", [P, MB])
        bdt = sb("bdt", [P, MB])
        dsk = sb("dsk", [P, MB])
        neg_a = sb("neg_a", [P, MB, NS])
        tok_bias = sb("tok_bias", [H0, 2, DIM])
        gam = sb("gam", [H0, DIM])
        bet = sb("bet", [H0, DIM])
        sww_lo = sb("sww_lo", [P, E])
        sww_hi = sb("sww_hi", [DLO, E])
        swb = sb("swb", [H0, E])
        minus_half = sb("minus_half", [P, 4])
        logits = sb("logits", [H0, COLS, E])

        arena = sb("arena", [P, 42400])
        at = [0]

        def carve(parts, *shape):
            n = 1
            for k in shape:
                n *= k
            v = arena[0:parts, at[0]:at[0] + n]
            at[0] += n + n % 2
            if len(shape) == 2:
                v = v.rearrange("p (a b) -> p a b", a=shape[0])
            elif len(shape) == 3:
                v = v.rearrange("p (a b c) -> p a b c", a=shape[0], b=shape[1])
            elif len(shape) == 4:
                v = v.rearrange("p (a b c d) -> p a b c d", a=shape[0], b=shape[1], c=shape[2])
            return v

        patches = carve(P, KP, 2, L)
        h = [carve(H0, 4, DIM) for _ in range(2)]
        hn = carve(H0, 4, DIM)
        hres = carve(H0, 4, DIM)
        t_lo = carve(P, 2, L + 3)
        t_hi = carve(P, 2, L + 3)
        xz = [carve(P, 2 * MB, N2) for _ in range(2)]
        spv = carve(P, MB, N2)
        spe = carve(P, MB, N2)
        delta = [carve(P, MB, N2) for _ in range(2)]
        du = [carve(P, MB, N2) for _ in range(2)]
        bcf = carve(P, N2)
        c_copy = [carve(P, N2) for _ in C_ON_POOL]
        bc3 = [carve(P, L).bitcast(BF16) for _ in range(2)]
        y = carve(P, MB, N2)
        decay = [carve(P, MB, 2, L) for _ in range(A_BUFS)]
        hb_at = at[0]
        hb = [carve(P, MB, N2) for _ in range(B_BUFS)]
        rows = [carve(H0, 4, 2 * DIM) for _ in range(2)]
        h2_lo = carve(P, 4, H0)
        h2_hi = carve(DLO, 4, H0)
        st1, st2, st3 = (carve(H0, 4, 6) for _ in range(3))
        mv1, mv2, mv3 = (carve(H0, 4, 2) for _ in range(3))
        rs1, rs2, rs3 = (carve(H0, 4) for _ in range(3))
        nb1, nb2, nb3 = (carve(H0, 4) for _ in range(3))
        raw_taps = arena[:, hb_at:hb_at + TAPS * MB * INNER].rearrange("p (t k n) -> p t k n", t=TAPS, k=MB)
        raw_win = y.rearrange("p a b -> p (a b)")[:, 0:MB * DIM].rearrange("p (k n) -> p k n", k=MB)
        a_end = at[0]

        at[0] = 0
        ex = carve(H0, COLS, E)
        oh = carve(H0, E, COLS)
        member = carve(H0, E, COLS)
        place = carve(H0, E, COLS)
        sel = carve(H0, E, COLS)
        tot = carve(H0, E, COLS)
        exv = carve(H0, COLS)
        prob = carve(H0, COLS)
        rsum = carve(H0, COLS)
        vmax = carve(H0, COLS)
        valid = carve(H0, COLS)
        destf = carve(H0, COLS)
        desti = carve(H0, COLS).bitcast(I32)
        dlo_i = carve(H0, COLS).bitcast(I32)
        dhi_i = carve(H0, COLS).bitcast(I32)
        ids = carve(H0, COLS).bitcast(I32)
        one_cols = carve(H0, COLS)
        weights8 = carve(H0, E)
        before = carve(H0, H0)
        every = carve(H0, H0)
        n_e = carve(H0, E)
        n_i = carve(H0, E).bitcast(I32)
        tiles_e = carve(H0, E)
        tile_end = carve(H0, E)
        base_e = carve(H0, E)
        lo_t, hi_t, mid_t, cnt, room = (carve(H0, E) for _ in range(5))
        lo_c, hi_c = carve(H0, E), carve(H0, E)
        gates = carve(H0, COLS, 2)
        tile_no = carve(1, TILES)
        tile_cmp = carve(1, TILES, E)
        tile_ex = carve(1, TILES).bitcast(I32)
        slot_id = carve(P, SC).bitcast(I32)
        sidx = [carve(H0, 8).bitcast(I32) for _ in range(2)]
        sval = [carve(H0, 8).bitcast(I32) for _ in range(2)]
        gidx = [carve(P, 2).bitcast(I32) for _ in range(GRING)]
        pidx = [carve(P, 2).bitcast(I32) for _ in range(2)]
        grow = [carve(P, 2, 2 * DIM) for _ in range(GRING)]
        ggate = [carve(P, 2, 2) for _ in range(GRING)]
        wp = [carve(P, FF + KF * DIM + KF) for _ in range(2)]
        w1h = [carve(DLO, FF) for _ in range(2)]
        b2r = [carve(P, DIM) for _ in range(2)]
        g_lo = [carve(P, TS) for _ in range(2)]
        g_hi = [carve(DLO, TS) for _ in range(2)]
        hid = [carve(P, KF, TS) for _ in range(2)]
        mo = [carve(P, 2, DIM) for _ in range(2)]
        mt = [carve(P, 2, DIM) for _ in range(2)]
        assert max(a_end, at[0]) <= 42400, (a_end, at[0])

        pb = [ctx.enter_context(nc.psum_tensor(f"bank{i}", [P, 512], F32)) for i in range(8)]
        ps_y = pb[0:3]
        ps_b, ps_c = pb[3:5]
        ps_k = pb[5:7]
        ps_t = pb[7]
        ps_g = pb[3:5]

        s_const = sem("consts_landed")
        s_taps = sem("raw_taps_landed")
        s_pool0 = sem("pool_consts_set")
        s_dve0 = sem("dve_consts_set")
        s_nega = sem("neg_a_ready")
        s_clsrow = sem("class_row_landed")
        s_pick = sem("pick_clear")
        s_vmm = sem("tap_product_done")
        s_vcopy = sem("tap_copied")
        s_patch = sem("patches_landed")
        s_tokmm = sem("tok_product_done")
        s_hres = sem("residual_copied")
        s_h = sem("h_ready")
        s_st1 = sem("stats1_ready")
        s_mv1 = sem("meanvar1_ready")
        s_ve1 = sem("vareps1_ready")
        s_rs1 = sem("rstd1_ready")
        s_hn = sem("hn_ready")
        s_trf = sem("front_transposed")
        s_trf_copied = sem("front_transposes_copied")
        s_gmm = sem("front_product_done")
        s_gev = sem("front_product_copied")
        s_x = sem("x_ready")
        s_z = sem("z_ready")
        s_bcrest = sem("bc_rest_ready")
        s_bcmid = sem("bc_second_part_ready")
        s_bc3 = sem("bc_parts_ready")
        s_bb = sem("b_spread")
        s_cb = sem("c_spread")
        s_spa = sem("softplus_abs")
        s_spe = sem("softplus_exp")
        s_spt = sem("softplus_rounded")
        s_spc = sem("softplus_rest")
        s_spl = sem("softplus_ln")
        s_spd = sem("softplus_sum")
        s_delta = sem("delta_ready")
        s_du = sem("du_ready")
        s_a = sem("decay_ready")
        s_bx = sem("bx_ready")
        s_scan = sem("scan_done")
        s_mul = sem("hc_ready")
        s_mulp = sem("hc_by_gpsimd_ready")
        s_cc = sem("c_copied")
        s_fold = sem("hc_folded")
        s_pow = [sem(f"deviation_ready{i}") for i in range(3)]
        s_onorm = sem("out_normalised")
        s_ysum = sem("state_sum_done")
        s_yev = sem("y_ready")
        s_ysz = sem("y_gated")
        s_opmm = sem("out_product_done")
        s_st2 = sem("stats2_ready")
        s_mv2 = sem("meanvar2_ready")
        s_ve2 = sem("vareps2_ready")
        s_rs2 = sem("rstd2_ready")
        s_gam = sem("gamma_applied")
        s_hbeta = sem("residual_beta_ready")
        s_h2 = sem("h2_ready")
        s_st3 = sem("stats3_ready")
        s_mv3 = sem("meanvar3_ready")
        s_ve3 = sem("vareps3_ready")
        s_rs3 = sem("rstd3_ready")
        s_rows = sem("rows_ready")
        s_stored = [sem(f"rows_stored{i}") for i in range(2)]
        s_trb = sem("back_transposed")
        s_trb_copied = sem("back_transposes_copied")
        s_lgmm = sem("logits_product_done")
        s_lg = sem("logits_ready")
        s_d = sem("dve_step")
        s_exin = sem("router_shifted")
        s_exout = sem("router_exp_ready")
        s_ohr = sem("route_ready")
        s_ranked = sem("rank_products_done")
        s_tie = sem("ties_ready")
        s_cnt = sem("bisect_counts_ready")
        s_bis = sem("bisect_totals_ready")
        s_fill = sem("slots_cleared")
        s_desti = sem("slots_of_tokens_ready")
        s_dest = [sem(f"slot_batch_ready{i}") for i in range(2)]
        s_scat = [sem(f"slot_ids_scattered{i}") for i in range(2)]
        s_tex = sem("tile_experts_ready")
        s_slot = sem("slot_ids_landed")
        s_gate = sem("gates_ready")
        s_gated = sem("gates_stored")
        s_w = [sem(f"expert_weights_landed{i}") for i in range(2)]
        s_gidx0 = sem("first_gather_ids_ready")
        s_gidx = [sem(f"gather_ids_ready{i}") for i in range(GRING)]
        s_gat = [sem(f"rows_gathered{i}") for i in range(GRING)]
        s_mtr = sem("tile_transposed")
        s_mtc = sem("tile_transposes_copied")
        s_m1 = sem("hidden_product_done")
        s_hid = sem("hidden_ready")
        s_m2 = sem("expert_product_done")
        s_keepx = sem("kept_input_ready")
        s_mbias = sem("expert_bias_added")
        s_mo = [sem(f"tile_rows_ready{i}") for i in range(GRING)]
        s_put = [sem(f"tile_rows_stored{i}") for i in range(2)]

        CLEAR = 5
        CONSTS = 20

        BC, DT, Z = MB, MB + 1, 2 * MB + 1

        def bank(t):
            return ps_k[t - Z] if Z <= t < Z + 2 else ps_t

        def o_tile(c):
            return ps_k[c // 2][0:H0, (c % 2) * DIM:(c % 2 + 1) * DIM]

        def c_used(eng, n, s):
            if s in C_ON_POOL:
                need(eng, s_cc, len(C_ON_POOL) * n + C_ON_POOL.index(s) + 1)
            else:
                need(eng, s_mul, len(C_ON_DVE) * n + C_ON_DVE.index(s) + 1)

        def c_applied(eng, n, s):
            if s in C_ON_POOL:
                need(eng, s_mulp, len(C_ON_POOL) * n + C_ON_POOL.index(s) + 1)
            else:
                need(eng, s_mul, len(C_ON_DVE) * n + C_ON_DVE.index(s) + 1)

        block = ctx.enter_context(nc.Block())

        @block.sync
        def _(sp):
            for dst, src in (
                (wtok[:, :, :], tok_w), (wz_lo[:, :], w_zlo), (wz_hi[:, :], w_zhi), (wdt[:, :, :], w_dt),
                (wout[:, :, :], w_out), (cb[:, :], conv_b), (bdt[:, :], b_dt), (dsk[:, :], d_skip), (neg_a[:, :, :], a_log),
                (tok_bias[:, 0, :], tok_b.partition_broadcast(H0)), (tok_bias[:, 1, :], tok_b.partition_broadcast(H0)),
                (gam[:, :], gamma.partition_broadcast(H0)), (bet[:, :], beta.partition_broadcast(H0)),
                (sww_lo[:, :], sw_w[0:P, :]), (sww_hi[:, :], sw_w[P:DIM, :]), (swb[:, :], sw_b.partition_broadcast(H0)),
                *((wx[:, :, c, :], w_x) for c in range(4)),
            ):
                sp.dma_start(dst, src).then_inc(s_const, 16)
            sp.dma_start(raw_taps, conv_w).then_inc(s_taps, 16)
            sp.dma_start(raw_win, w_inx).then_inc(s_taps, 16)
            sp.wait_ge(s_const, 16 * CONSTS)
            sp.dma_start(tok_bias[0:1, 0, :], cls_tok).then_inc(s_clsrow, 16)

            def load_patches(n):
                need(sp, s_tokmm, 2 * n)
                sp.dma_start(patches[:, :, :, 1:L], x[ds(n, 1)].rearrange("o p k b n -> (o p) k b n")
                             if not isinstance(n, int) else x[n]).then_inc(s_patch, 16)

            def store_rows(n, r):
                sp.wait_ge(s_rows, n + 1)
                t = rows_dram[ds(n * N2, N2), :].rearrange("(b t) d -> t b d", b=2)
                v = rows[r].rearrange("p (b f) d -> p b f d", f=2)
                sp.dma_start(t[0:H0], v[:, :, 0, :]).then_inc(s_stored[r], 16)
                sp.dma_start(t[H0:L], v[1:H0, :, 1, :]).then_inc(s_stored[r], 16)

            def body(i, r, tok):
                if tok:
                    load_patches(i + 2)
                if not isinstance(i, int) or i >= 1:
                    store_rows(i - 1, 1 - r)

            sp.wait_ge(s_dve0, 1)
            load_patches(0)
            load_patches(1)
            for i in range(4):
                body(i, i % 2, True)
            with sp.Fori(4, PAIRS - 3, 2) as i:
                body(i, 0, True)
                body(i + 1, 1, True)
            body(PAIRS - 2, 0, False)
            body(PAIRS - 1, 1, False)
            store_rows(PAIRS - 1, 1)

            for b in range(2):
                sp.wait_ge(s_scat[b], 16 * COLS // 2)
            sp.wait_ge(s_fill, 16)
            sp.dma_start(slot_id, slot_dram.rearrange("(p c) o -> p (c o)", p=P)).then_inc(s_slot, 16)

            def load_expert(k, r):
                need(sp, s_m2, 2 * (k - 1))
                need(sp, s_mbias, k - 1)
                e = sp.value_load(tile_ex[0:1, ds(k, 1)], min_val=0, max_val=E - 1)
                sp.dma_start(wp[r], w_pack[ds(e, 1)].rearrange("o p n -> (o p) n")).then_inc(s_w[r], 16)
                sp.dma_start(w1h[r], w1_hi[ds(e, 1)].rearrange("o p n -> (o p) n")).then_inc(s_w[r], 16)
                sp.dma_start(b2r[r], b2[ds(e, 1), :].rearrange("o n -> (o n)").partition_broadcast(P)).then_inc(s_w[r], 16)

            sp.wait_ge(s_tex, 1)
            load_expert(0, 0)
            load_expert(1, 1)

            def gates_out():
                sp.wait_ge(s_gate, 1)
                g = gate_dram.rearrange("(b t) w -> t b w", t=L)
                v = gates.rearrange("p (b f) w -> p b f w", f=2)
                sp.dma_start(g[0:H0], v[:, :, 0, :]).then_inc(s_gated, 16)
                sp.dma_start(g[H0:L], v[1:H0, :, 1, :]).then_inc(s_gated, 16)

            gates_out()
            with sp.Fori(2, TILES - 2, 2) as k:
                load_expert(k, 0)
                load_expert(k + 1, 1)
            load_expert(TILES - 1, 0)
            for r in range(2):
                sp.wait_ge(s_stored[r], 16 * PAIRS)
                sp.wait_ge(s_put[r], 32 * ((TILES + 1 - r) // 2))
            sp.wait_ge(s_gated, 32)

        @block.gpsimd
        def _(pool):
            pool.memset(ident[:, :], 0.0).then_inc(s_pool0, 1)
            pool.memset(minus_half[:, :], -0.5).then_inc(s_pool0, 1)
            pool.wait_ge(s_pool0, 2)
            pool.affine_select(out=ident[:, :], in_=ident[:, :], compare_op=ALU.not_equal, fill=1.0, base=0,
                               pattern=[[-1, P]], channel_multiplier=1).then_inc(s_pool0, 1)

            def rstd(n, which):
                s_in, mv, rs, nb, s_out = ((s_ve1, mv1, rs1, nb1, s_rs1), (s_ve2, mv2, rs2, nb2, s_rs2),
                                           (s_ve3, mv3, rs3, nb3, s_rs3))[which - 1]
                pool.wait_ge(s_in, n + 1)
                pool.tensor_tensor(rs[:, :], mv[:, :, 1], minus_half[0:H0, :], ALU.pow).then_inc(s_pow[which - 1], 1)
                pool.wait_ge(s_pow[which - 1], n + 1)
                pool.tensor_tensor(nb[:, :], mv[:, :, 0], rs[:, :], ALU.mult).then_inc(s_out, 1)

            def times_c(n, s):
                x = C_ON_POOL.index(s)
                pool.wait_ge(s_scan, NS * n + s + 1)
                pool.wait_ge(s_cc, len(C_ON_POOL) * n + x + 1)
                v = hb[s % B_BUFS]
                pool.tensor_tensor(v[:, :, :], v[:, :, :], c_copy[x].unsqueeze(1).to_broadcast([P, MB, N2]),
                                   ALU.mult).then_inc(s_mulp, 1)

            def rest_bc(n, r):
                pool.wait_ge(s_gev, 10 * n + BC + 1)
                pool.tensor_tensor(bcf, bcf, bc3[r], ALU.subtract).then_inc(s_bcrest, 1)

            def fold(n, k):
                c_applied(pool, n, 2 * k)
                c_applied(pool, n, 2 * k + 1)
                a, b = hb[2 * k % B_BUFS], hb[(2 * k + 1) % B_BUFS]
                pool.tensor_tensor(b[:, :, :], a[:, :, :], b[:, :, :], ALU.add).then_inc(s_fold, 1)

            def apply_gamma(n, r):
                pool.wait_ge(s_onorm, n + 1)
                v = rows[r][:, :, 0:DIM]
                pool.tensor_tensor(v, v, gam[:, :].unsqueeze(1).to_broadcast([H0, 4, DIM]), ALU.mult).then_inc(s_gam, 1)

            def gate_y(n, r):
                pool.wait_ge(s_yev, MB * (n + 1))
                pool.wait_ge(s_z, n + 1)
                pool.tensor_tensor(y[:, :, :], y[:, :, :], xz[r][:, MB:2 * MB, :], ALU.mult).then_inc(s_ysz, 1)

            def add_beta(n):
                pool.wait_ge(s_hres, n + 1)
                pool.tensor_tensor(hres[:, :, :], hres[:, :, :], bet[:, :].unsqueeze(1).to_broadcast([H0, 4, DIM]),
                                   ALU.add).then_inc(s_hbeta, 1)

            def add_residual(n, r):
                pool.wait_ge(s_gam, n + 1)
                pool.wait_ge(s_hbeta, n + 1)
                pool.tensor_tensor(rows[r][:, :, 0:DIM], rows[r][:, :, 0:DIM], hres[:, :, :], ALU.add).then_inc(s_h2, 1)

            def softplus_rest(n, r):
                pool.wait_ge(s_spe, n + 1)
                pool.tensor_tensor(spv[:, :, :], spv[:, :, :], spe[:, :, :], ALU.add).then_inc(s_spd, 1)
                pool.wait_ge(s_spd, n + 1)
                pool.wait_ge(s_spt, n + 1)
                pool.tensor_tensor(spv[:, :, :], spv[:, :, :], delta[r][:, :, :], ALU.subtract).then_inc(s_spc, 1)

            def make_du(n, r):
                pool.wait_ge(s_delta, n + 1)
                need(pool, s_bx, NS * (n - 1))
                pool.tensor_tensor(du[r][:, :, :], delta[r][:, :, :], xz[r][:, 0:MB, :], ALU.mult).then_inc(s_du, 1)

            def body(i, r, front, tokens):
                back = not isinstance(i, int) or i >= 1
                o = 1 - r
                for j in range(NS):
                    if back:
                        if j == 1:
                            gate_y(i - 1, o)
                        if j == 2:
                            add_beta(i - 1)
                        if j == 5:
                            rstd(i - 1, 2)
                        if j == 6:
                            apply_gamma(i - 1, o)
                            add_residual(i - 1, o)
                        if j == 8:
                            rstd(i - 1, 3)
                    if front and j == 10:
                        rest_bc(i + 1, o)
                    if front and j == 13:
                        softplus_rest(i + 1, o)
                    if j in C_ON_POOL:
                        times_c(i, j)
                    if tokens and j == 13:
                        rstd(i + 2, 1)
                    if front and j == 13:
                        make_du(i + 1, o)
                    if j % 2 and j // 2 in FOLDED:
                        fold(i, j // 2)

            pool.wait_ge(s_dve0, CLEAR)
            rstd(0, 1)
            rstd(1, 1)
            rest_bc(0, 0)
            softplus_rest(0, 0)
            make_du(0, 0)
            for i in range(4):
                body(i, i % 2, True, True)
            with pool.Fori(4, PAIRS - 3, 2) as i:
                body(i, 0, True, True)
                body(i + 1, 1, True, True)
            body(PAIRS - 2, 0, True, False)
            body(PAIRS - 1, 1, False, False)
            n = PAIRS - 1
            gate_y(n, 1)
            add_beta(n)
            rstd(n, 2)
            apply_gamma(n, 1)
            add_residual(n, 1)
            rstd(n, 3)

            pool.wait_ge(s_stored[0], 16 * PAIRS)
            pool.wait_ge(s_stored[1], 16 * PAIRS)
            pool.wait_ge(s_lg, PAIRS)
            pool.memset(before, 1.0).then_inc(s_pool0, 1)
            pool.memset(every, 1.0).then_inc(s_pool0, 1)
            pool.memset(valid, 1.0).then_inc(s_pool0, 1)
            pool.memset(one_cols, 1.0).then_inc(s_pool0, 1)
            pool.iota(slot_id, [[0, SC]], base=NOBODY, channel_multiplier=0).then_inc(s_pool0, 1)
            pool.iota(ids.rearrange("p (b f) -> p b f", f=2), [[L, IMAGES], [HSTEP, 2]], base=0,
                      channel_multiplier=1).then_inc(s_pool0, 1)
            pool.iota(weights8, [[-1, E]], base=E, channel_multiplier=0,
                      allow_small_or_imprecise_dtypes=True).then_inc(s_pool0, 1)
            pool.iota(tile_no, [[1, TILES]], base=0, channel_multiplier=0,
                      allow_small_or_imprecise_dtypes=True).then_inc(s_pool0, 1)
            for r in range(GRING):
                pool.memset(grow[r], 0.0).then_inc(s_pool0, 1)
                pool.memset(ggate[r], 0.0).then_inc(s_pool0, 1)
            pool.wait_ge(s_pool0, 3 + POOL_SET)
            pool.affine_select(out=before, in_=before, compare_op=ALU.is_gt, fill=0.0, base=0, pattern=[[1, H0]],
                               channel_multiplier=-1).then_inc(s_pool0, 1)
            pool.affine_select(out=valid.rearrange("p (b f) -> p b f", f=2), in_=valid.rearrange("p (b f) -> p b f", f=2),
                               compare_op=ALU.is_ge, fill=0.0, base=0, pattern=[[0, IMAGES], [-1, 2]],
                               channel_multiplier=2).then_inc(s_pool0, 1)
            pool.dma_start(slot_dram.rearrange("(p c) o -> p (c o)", p=P), slot_id).then_inc(s_fill, 16)

            last_slot, last_token = pool.to_reg(SLOTS - 1), pool.to_reg(TOK - 1)

            def scatter(u, r):
                pool.wait_ge(s_fill, 16)
                pool.wait_ge(s_dest[r], u)
                for c in range(8):
                    pool.indirect_dma_start(
                        out=slot_dram, out_offset=bass.IndirectOffsetOnAxis(ap=sidx[r][:, c:c + 1].bitcast(U32), axis=0),
                        in_=sval[r][:, c:c + 1], in_offset=None, bounds_check=last_slot, oob_is_err=False,
                    ).then_inc(s_scat[r], 16)

            with pool.Fori(1, COLS // 16 + 1, 1) as u:
                scatter(u, 0)
                scatter(u, 1)

            def gather(g, u):
                pool.wait_ge(s_gated, 32)
                if isinstance(u, int) and u == 0:
                    pool.wait_ge(s_gidx0, g + 1)
                else:
                    pool.wait_ge(s_gidx[g], u)
                for f in range(2):
                    i = bass.IndirectOffsetOnAxis(ap=gidx[g][:, f:f + 1].bitcast(U32), axis=0)
                    pool.indirect_dma_start(out=grow[g][:, f, :], out_offset=None, in_=rows_dram, in_offset=i,
                                            bounds_check=last_token, oob_is_err=False).then_inc(s_gat[g], 16)
                    pool.indirect_dma_start(out=ggate[g][:, f, :], out_offset=None, in_=gate_dram, in_offset=i,
                                            bounds_check=last_token, oob_is_err=False).then_inc(s_gat[g], 16)

            def put(g, u):
                r = g % 2
                pool.wait_ge(s_gated, 32)
                pool.wait_ge(s_mo[g], u)
                for f in range(2):
                    pool.indirect_dma_start(
                        out=out, out_offset=bass.IndirectOffsetOnAxis(ap=pidx[r][:, f:f + 1].bitcast(U32), axis=0),
                        in_=mo[r][:, f, :], in_offset=None, bounds_check=last_token, oob_is_err=False,
                    ).then_inc(s_put[r], 16)

            for g in range(GRING):
                gather(g, 0)
            with pool.Fori(1, TILES // GRING, 1) as u:
                for g in range(GRING):
                    put(g, u)
                    gather(g, u)
            for t in range(FULL - GRING, TILES):
                put(t % GRING, t // GRING + 1)
                if t + GRING < TILES:
                    gather(t % GRING, t // GRING + 1)

        @block.scalar
        def _(act):
            act.wait_ge(s_const, 16 * CONSTS)
            act.activation(neg_a[:, :, :], neg_a[:, :, :], ACT.Exp).then_inc(s_nega, 1)
            act.wait_ge(s_nega, 1)
            act.activation(neg_a[:, :, :], neg_a[:, :, :], ACT.Copy, scale=-1.0).then_inc(s_nega, 1)

            def decays(n, r, s):
                b = s % A_BUFS
                if s == 0:
                    act.wait_ge(s_delta, n + 1)
                need(act, s_scan, NS * n + s - A_BUFS + 1)
                for m in range(MB):
                    d = delta[r][:, m, :].rearrange("p (b t) -> p b t", b=2)[:, :, 1:L]
                    ins = act.activation(decay[b][:, m, :, 1:L], d, ACT.Exp, scale=neg_a[:, m, s:s + 1])
                ins.then_inc(s_a, 1)

            def copy_residual(n, r):
                need(act, s_h2, n)
                act.wait_ge(s_h, n + 1)
                act.activation(hres[:, :, :], h[r][:, :, :], ACT.Copy).then_inc(s_hres, 1)

            def normalise(n, dst, src, rs, nb, s_rs, s_out):
                act.wait_ge(s_rs, n + 1)
                for c in range(4):
                    ins = act.activation(dst(c), src(c), ACT.Identity, scale=rs[:, c:c + 1], bias=nb[:, c:c + 1])
                ins.then_inc(s_out, 1)

            def front_norm(n, r):
                need(act, s_trf, 2 * n)
                normalise(n, lambda c: hn[:, c, :], lambda c: h[r][:, c, :], rs1, nb1, s_rs1, s_hn)

            def out_norm(n, r):
                need(act, s_stored[r], 16 * (n - r))
                normalise(n, lambda c: rows[r][:, c, 0:DIM], o_tile, rs2, nb2, s_rs2, s_onorm)

            def row_norm(n, r):
                need(act, s_trb, 2 * (n - 1))
                normalise(n, lambda c: rows[r][:, c, DIM:2 * DIM], lambda c: rows[r][:, c, 0:DIM], rs3, nb3, s_rs3, s_rows)

            def copy_front_t(n, b):
                act.wait_ge(s_trf, 2 * n + b + 1)
                if b == 0:
                    need(act, s_gmm, 10 * n)
                act.activation(t_lo[:, b, 1:L + 1], ps_k[b][:, 0:L], ACT.Copy)
                act.activation(t_hi[0:DLO, b, 1:L + 1], ps_k[b][0:DLO, L:2 * L], ACT.Copy)
                act.activation(t_hi[DLO:P, b, 0:L], ps_k[b][0:DLO, L:2 * L], ACT.Copy).then_inc(s_trf_copied, 1)

            def copy_c(n, s):
                x = C_ON_POOL.index(s)
                act.wait_ge(s_cb, NS * n + s + 1)
                need(act, s_mulp, len(C_ON_POOL) * (n - 1) + x + 1)
                act.activation(c_copy[x], ps_c[:, 0:N2], ACT.Copy).then_inc(s_cc, 1)

            def copy_product(n, r, t):
                act.wait_ge(s_gmm, 10 * n + t + 1)
                src = bank(t)[:, 0:N2]
                if t < BC:
                    if t == 0:
                        need(act, s_yev, MB * (n - 1))
                        need(act, s_du, n - 1)
                    ins = act.activation(xz[r][:, t, :], src, ACT.Identity, bias=cb[:, t:t + 1])
                elif t == BC:
                    need(act, s_cb, NS * (n - 1))
                    need(act, s_bc3, n)
                    act.activation(bcf, src, ACT.Copy)
                    ins = act.activation(bc3[r], src, ACT.Copy)
                elif t < Z:
                    m = t - DT
                    if m == 0:
                        need(act, s_delta, n)
                    act.activation(spv[:, m, :], src, ACT.Relu, bias=bdt[:, m:m + 1])
                    ins = act.activation(spe[:, m, :], src, ACT.Abs, bias=bdt[:, m:m + 1])
                else:
                    if t == Z:
                        need(act, s_ysz, n - 1)
                    ins = act.activation(xz[r][:, MB + t - Z, :], src, ACT.Copy)
                ins.then_inc(s_gev, 1)

            def middle_bc(n, r):
                act.wait_ge(s_bcrest, n + 1)
                act.activation(bc3[r][DLO:P], bcf[DLO:P], ACT.Copy).then_inc(s_bcmid, 1)

            def silu_x(n, r):
                act.wait_ge(s_gev, 10 * n + BC)
                act.activation(xz[r][:, 0:MB, :], xz[r][:, 0:MB, :], ACT.Silu).then_inc(s_x, 1)

            def silu_z(n, r):
                act.wait_ge(s_gev, 10 * (n + 1))
                act.activation(xz[r][:, MB:2 * MB, :], xz[r][:, MB:2 * MB, :], ACT.Silu).then_inc(s_z, 1)

            def softplus(n, r):
                act.wait_ge(s_gev, 10 * n + Z)
                act.activation(spe[:, :, :], spe[:, :, :], ACT.Exp, scale=-1.0).then_inc(s_spe, 1)
                act.wait_ge(s_spe, n + 1)
                need(act, s_bx, NS * (n - 1))
                act.activation(du[r][:, :, :], spe[:, :, :], ACT.Ln, bias=1.0).then_inc(s_spl, 1)

            def copy_back_t(n, b):
                act.wait_ge(s_trb, 2 * n + b + 1)
                if b == 0:
                    need(act, s_lgmm, n)
                act.activation(h2_lo[:, 2 * b:2 * b + 2, :], ps_t[:, 0:2 * H0], ACT.Copy)
                act.activation(h2_hi[:, 2 * b:2 * b + 2, :], ps_t[0:DLO, 2 * H0:4 * H0], ACT.Copy).then_inc(s_trb_copied, 1)

            def body(i, r, front, tokens):
                back = not isinstance(i, int) or i >= 1
                o = 1 - r
                n = i + 1
                for j in range(NS):
                    if j == 0:
                        copy_product(i, r, Z + 2)
                        if front:
                            copy_front_t(n, 0)
                            copy_front_t(n, 1)
                    if front:
                        for t in {2: (0,), 5: (1,), 7: (2,), 9: (BC,), 10: (DT,), 11: (DT + 1,), 12: (DT + 2,),
                                  14: (Z, Z + 1)}.get(j, ()):
                            copy_product(n, o, t)
                        if j == 7:
                            silu_x(n, o)
                        if j == 11:
                            middle_bc(n, o)
                        if j == 12:
                            softplus(n, o)
                    if j == 7:
                        silu_z(i, r)
                    if j == 9:
                        copy_residual(i, r)
                    if back and j == 6:
                        out_norm(i - 1, o)
                    if back and j == 9:
                        row_norm(i - 1, o)
                    if back and j == 13:
                        copy_back_t(i - 1, 0)
                    if back and j == 13:
                        copy_back_t(i - 1, 1)
                    if j in C_ON_POOL:
                        copy_c(i, j)
                    if j + LEAD < NS:
                        decays(i, r, j + LEAD)
                    elif front:
                        decays(n, o, j + LEAD - NS)
                    if tokens and j == 14:
                        front_norm(i + 2, r)

            act.wait_ge(s_dve0, CLEAR)
            front_norm(0, 0)
            copy_front_t(0, 0)
            copy_front_t(0, 1)
            for t in range(Z + 2):
                if t == BC:
                    silu_x(0, 0)
                copy_product(0, 0, t)
            middle_bc(0, 0)
            softplus(0, 0)
            front_norm(1, 1)
            for s in range(LEAD):
                decays(0, 0, s)
            for i in range(4):
                body(i, i % 2, True, True)
            with act.Fori(4, PAIRS - 3, 2) as i:
                body(i, 0, True, True)
                body(i + 1, 1, True, True)
            body(PAIRS - 2, 0, True, False)
            body(PAIRS - 1, 1, False, False)
            out_norm(PAIRS - 1, 1)
            row_norm(PAIRS - 1, 1)
            copy_back_t(PAIRS - 1, 0)
            copy_back_t(PAIRS - 1, 1)

            act.wait_ge(s_exin, 1)
            act.activation(ex, ex, ACT.Exp).then_inc(s_exout, 1)

            def batch(t, r):
                need(act, s_scat[r], 16 * 8 * ((t - r) // 2) if isinstance(t, int) else 64 * (t - r))
                act.activation(sidx[r], desti[:, ds(t * 8, 8)], ACT.Copy)
                act.activation(sval[r], ids[:, ds(t * 8, 8)], ACT.Copy).then_inc(s_dest[r], 1)

            act.wait_ge(s_desti, 1)
            batch(0, 0)
            batch(1, 1)
            with act.Fori(2, COLS // 8 - 1, 2) as t:
                batch(t, 0)
                batch(t + 1, 1)

            def tile_copies(k, r):
                act.wait_ge(s_mtr, k + 1)
                need(act, s_m1, KF * (k - 1))
                act.activation(g_lo[r], ps_t[:, 0:TS], ACT.Copy)
                act.activation(g_hi[r], ps_t[0:DLO, TS:2 * TS], ACT.Copy).then_inc(s_mtc, 1)

            def gelus(k, r):
                b1 = wp[r][:, FF + KF * DIM:]
                need(act, s_m2, 2 * (k - 1))
                for f in range(KF):
                    act.wait_ge(s_m1, KF * k + f + 1)
                    act.activation(hid[r][:, f, :], (ps_y + ps_g[0:1])[f % 4][:, 0:TS], ACT.Gelu,
                                   bias=b1[:, f:f + 1]).then_inc(s_hid, 1)

            tile_copies(0, 0)
            for k in range(2):
                gelus(k, k)
                tile_copies(k + 1, 1 - k)
            with act.Fori(2, TILES - 2, 2) as k:
                gelus(k, 0)
                tile_copies(k + 1, 1)
                gelus(k + 1, 1)
                tile_copies(k + 2, 0)
            gelus(TILES - 1, 0)

        @block.tensor
        def _(pe):
            pe.wait_ge(s_taps, 32)
            n = 0
            for k in range(TAPS):
                for lo, m in ((0, P), (P, DLO)):
                    need(pe, s_vcopy, n - 1)
                    for c in range(MB):
                        mm = pe.matmul(ps_g[n % 2][0:m, 0:INNER], raw_win[:, c, lo:lo + m], raw_taps[:, k, c, :],
                                       start=(c == 0), stop=(c == MB - 1))
                    mm.then_inc(s_vmm, 1)
                    n += 1
            VPROD = n

            def tok(n, b, first, last):
                if first == 0:
                    if b == 0:
                        pe.wait_ge(s_patch, 16 * (n + 1))
                    need(pe, s_trf_copied, 2 * n)
                    need(pe, s_onorm, n - 2)
                for a in range(first, last):
                    f, c = a // KP, a % KP
                    mm = pe.matmul(ps_k[b][0:H0, f * DIM:(f + 1) * DIM], patches[:, c, b, f * HSTEP:f * HSTEP + H0],
                                   wtok[:, c, :], start=(c == 0), stop=(c == KP - 1))
                if last == 2 * KP:
                    mm.then_inc(s_tokmm, 1)

            def front_t(n, b):
                if b == 0:
                    pe.wait_ge(s_hn, n + 1)
                need(pe, s_gev, 10 * (n - 1) + Z + 1 + b)
                for f in (1, 0):
                    c = f * HSTEP
                    pe.transpose(ps_k[b][:, c:c + H0], hn[:, 2 * b + f, 0:P], ident[0:H0, 0:H0])
                    mm = pe.transpose(ps_k[b][0:DLO, L + c:L + c + H0], hn[:, 2 * b + f, P:DIM], ident[0:H0, 0:H0])
                mm.then_inc(s_trf, 1)

            def product(n, r, t, first=0, last=6):
                o = bank(t)
                if first == 0:
                    if t == 0:
                        pe.wait_ge(s_trf_copied, 2 * (n + 1))
                    if t == BC:
                        pe.wait_ge(s_x, n + 1)
                    if t in (Z, Z + 1):
                        need(pe, s_h, min(n + 2, PAIRS) if isinstance(n, int) else n + 2)
                    elif t == Z + 2:
                        need(pe, s_lg, n - 1)
                        pe.wait_ge(s_gev, 10 * n + Z)
                    else:
                        need(pe, s_gev, 10 * n + t)
                if t < BC:
                    c = slice(t * P, (t + 1) * P)
                    for k in range(first, last):
                        if k < TAPS:
                            mm = pe.matmul(o[:, 0:N2], v_lo[:, k, c], t_lo[:, :, k:k + L], start=(k == 0), stop=False)
                        else:
                            k2 = k - TAPS
                            mm = pe.matmul(o[:, 0:N2], v_hi[:, k2, c], t_hi[:, :, 2 * k2:2 * k2 + L], start=False,
                                           stop=(k2 == 1))
                elif t == BC:
                    for k in range(MB):
                        mm = pe.matmul(o[:, 0:N2], wx[:, k].rearrange("p c n -> p (c n)"), xz[r][:, k, :], start=(k == 0),
                                       stop=(k == MB - 1))
                elif t < Z:
                    for k in range(MB):
                        mm = pe.matmul(o[:, 0:N2], wdt[:, k, (t - DT) * P:(t - DT + 1) * P], xz[r][:, k, :],
                                       start=(k == 0), stop=(k == MB - 1))
                else:
                    c = slice((t - Z) * P, (t - Z + 1) * P)
                    pe.matmul(o[:, 0:N2], wz_lo[:, c], t_lo[:, :, 1:L + 1], start=True, stop=False)
                    mm = pe.matmul(o[:, 0:N2], wz_hi[:, c], t_hi[0:DLO, :, 1:L + 1], start=False, stop=True)
                if last == 6:
                    mm.then_inc(s_gmm, 1)

            def spread_b(n, r, s):
                if s == 0:
                    pe.wait_ge(s_bc3, n + 1)
                need(pe, s_bx, NS * n + s)
                pe.matmul(ps_b[:, 0:N2], pick[:, s, :], bc3[r], start=True, stop=True).then_inc(s_bb, 1)

            def spread_c(n, r, s):
                c_used(pe, n if s else n - 1, (s - 1) % NS)
                pe.matmul(ps_c[:, 0:N2], pick[:, NS + s, :], bc3[r], start=True, stop=True).then_inc(s_cb, 1)

            def state_sum(n, s):
                if sums_until(s) == 1:
                    need(pe, s_yev, MB * n)
                if s // 2 in FOLDED:
                    pe.wait_ge(s_fold, len(FOLDED) * n + s // 2 + 1)
                else:
                    c_applied(pe, n, s)
                for m in range(MB):
                    mm = pe.matmul(ps_y[m][:, 0:N2], ident[:, :], hb[s % B_BUFS][:, m, :], start=(sums_until(s) == 1),
                                   stop=(s == NS - 1))
                mm.then_inc(s_ysum, 1)

            def out_product(n, b):
                if b == 0:
                    pe.wait_ge(s_ysz, n + 1)
                    if isinstance(n, int) and n >= PAIRS - 2:
                        pe.wait_ge(s_gev, 10 * PAIRS)
                        pe.wait_ge(s_onorm, n)
                    else:
                        pe.wait_ge(s_trf_copied, 2 * (n + 3))
                for f in range(2):
                    c = b * L + f * HSTEP
                    for k in range(MB):
                        mm = pe.matmul(ps_k[b][0:H0, f * DIM:(f + 1) * DIM], y[:, k, c:c + H0], wout[:, k, :],
                                       start=(k == 0), stop=(k == MB - 1))
                mm.then_inc(s_opmm, 1)

            def back_t(n, r, b):
                if b == 0:
                    pe.wait_ge(s_rows, n + 1)
                    pe.wait_ge(s_gev, min(10 * (n + 2) + Z, 10 * PAIRS) if isinstance(n, int) else 10 * (n + 2) + Z)
                need(pe, s_trb_copied, 2 * n + b)
                for f in range(2):
                    src = rows[r][:, 2 * b + f, DIM:2 * DIM]
                    pe.transpose(ps_t[:, f * H0:(f + 1) * H0], src[:, 0:P], ident[0:H0, 0:H0])
                    mm = pe.transpose(ps_t[0:DLO, (2 + f) * H0:(3 + f) * H0], src[:, P:DIM], ident[0:H0, 0:H0])
                mm.then_inc(s_trb, 1)

            def router(n):
                pe.wait_ge(s_trb_copied, 2 * (n + 1))
                for c in range(4):
                    o = ps_t[0:H0, c * E:(c + 1) * E]
                    pe.matmul(o, h2_lo[:, c, :], sww_lo[:, :], start=True, stop=False)
                    mm = pe.matmul(o, h2_hi[:, c, :], sww_hi[:, :], start=False, stop=True)
                mm.then_inc(s_lgmm, 1)

            def body(i, r, front, tokens):
                back = not isinstance(i, int) or i >= 1
                o = 1 - r
                n = i + 1
                for j in range(NS):
                    def next_b():
                        if j + 2 < NS:
                            spread_b(i, r, j + 2)
                        elif front:
                            spread_b(n, o, j + 2 - NS)

                    if j in (0, NS - 1):
                        next_b()
                    if back and j == 2:
                        out_product(i - 1, 0)
                    if back and j == 3:
                        out_product(i - 1, 1)
                    if back and j == 14:
                        router(i - 1)
                    if front:
                        for args in {0: ((0, 0, 3),), 1: ((0, 3, 6),), 2: ((1, 0, 1),), 3: ((1, 1, 2),), 4: ((1, 2, 6),),
                                     5: ((2, 0, 3),), 6: ((2, 3, 6),), 8: ((BC,),), 9: ((DT,),), 10: ((DT + 1,),),
                                     11: ((DT + 2,),), 13: ((Z,), (Z + 1,)), 15: ((Z + 2,),)}.get(j, ()):
                            product(n, o, *args)
                    if j not in (0, NS - 1):
                        next_b()
                    if tokens:
                        for args in {7: ((0, 0, 9),), 8: ((0, 9, 12),), 9: ((1, 0, 4),), 10: ((1, 4, 8),),
                                     11: ((1, 8, 12),)}.get(j, ()):
                            tok(i + 2, *args)
                    if back and j == 12:
                        back_t(i - 1, o, 0)
                    if back and j == 13:
                        back_t(i - 1, o, 1)
                    if tokens and j == 15:
                        front_t(i + 2, 0)
                        front_t(i + 2, 1)
                    if j + 1 < NS:
                        spread_c(i, r, j + 1)
                    elif front:
                        spread_c(n, o, 0)
                    for s in {2: (1,), 4: (3,), 6: (5,), 8: (7,), 12: (9, 11), 13: (12, 13), 14: (14,), 15: (15,)}.get(j, ()):
                        state_sum(i, s)

            pe.wait_ge(s_const, 16 * CONSTS)
            pe.wait_ge(s_pool0, 3)
            pe.wait_ge(s_dve0, CLEAR)
            pe.wait_ge(s_vcopy, VPROD + 2)
            tok(0, 0, 0, 2 * KP)
            tok(0, 1, 0, 2 * KP)
            front_t(0, 0)
            front_t(0, 1)
            tok(1, 0, 0, 2 * KP)
            tok(1, 1, 0, 2 * KP)
            for t in range(10):
                product(0, 0, t)
            front_t(1, 0)
            front_t(1, 1)
            spread_b(0, 0, 0)
            spread_c(0, 0, 0)
            spread_b(0, 0, 1)
            for i in range(4):
                body(i, i % 2, True, True)
            with pe.Fori(4, PAIRS - 3, 2) as i:
                body(i, 0, True, True)
                body(i + 1, 1, True, True)
            body(PAIRS - 2, 0, True, False)
            body(PAIRS - 1, 1, False, False)
            n = PAIRS - 1
            out_product(n, 0)
            out_product(n, 1)
            back_t(n, 1, 0)
            back_t(n, 1, 1)
            router(n)

            def rank(src):
                for half in range(2):
                    v = src.rearrange("p e c -> p (e c)")[:, half * 512:(half + 1) * 512]
                    pe.matmul(ps_k[half][0:H0, :], before, v, start=True, stop=True)
                    mm = pe.matmul(ps_g[half][0:H0, :], every, v, start=True, stop=True)
                mm.then_inc(s_ranked, 1)

            pe.wait_ge(s_pool0, 3 + POOL_SET + 2)
            pe.wait_ge(s_lg, PAIRS)
            pe.wait_ge(s_ohr, 1)
            rank(oh)
            with pe.Fori(0, BISECT, 1) as t:
                pe.wait_ge(s_cnt, t + 1)
                pe.matmul(ps_y[0][0:H0, 0:E], every, cnt, start=True, stop=True).then_inc(s_bis, 1)
            pe.wait_ge(s_cnt, BISECT + 1)
            pe.matmul(ps_y[0][0:H0, 0:E], every, cnt, start=True, stop=True).then_inc(s_bis, 1)
            pe.wait_ge(s_tie, 1)
            rank(sel)

            def tile_t(k, g):
                pe.wait_ge(s_gat[g], 64 * ((k - g) // GRING + 1) if isinstance(k, int) else 64 // GRING * (k - g) + 64)
                need(pe, s_mtc, k)
                for f in range(2):
                    pe.transpose(ps_t[:, f * P:(f + 1) * P], grow[g][:, f, DIM:DIM + P], ident[:, :])
                    mm = pe.transpose(ps_t[0:DLO, TS + f * P:TS + (f + 1) * P], grow[g][:, f, DIM + P:2 * DIM], ident[:, :])
                mm.then_inc(s_mtr, 1)

            def hidden(k, r):
                pe.wait_ge(s_w[r], 48 * ((k - r) // 2 + 1) if isinstance(k, int) else 24 * (k - r) + 48)
                pe.wait_ge(s_mtc, k + 1)
                for f in range(KF):
                    o = (ps_y + ps_g[0:1])[f % 4][:, 0:TS]
                    need(pe, s_hid, KF * k + f - 3)
                    c = slice(f * P, (f + 1) * P)
                    pe.matmul(o, wp[r][:, c], g_lo[r], start=True, stop=False)
                    pe.matmul(o, w1h[r][:, c], g_hi[r], start=False, stop=True).then_inc(s_m1, 1)

            def expert_out(k, r):
                w2 = wp[r][:, FF:FF + KF * DIM].rearrange("p (f d) -> p f d", f=KF)
                need(pe, s_mbias, k)
                for f in range(2):
                    for c in range(KF):
                        if f == 0:
                            pe.wait_ge(s_hid, KF * k + c + 1)
                        mm = pe.matmul(ps_k[f][:, 0:DIM], hid[r][:, c, f * P:(f + 1) * P], w2[:, c, :], start=(c == 0),
                                       stop=(c == KF - 1))
                    mm.then_inc(s_m2, 1)

            pe.wait_ge(s_gate, 1)

            def ring(k, tiles=GRING):
                for g in range(tiles):
                    hidden(k + g, g % 2)
                    if g + 1 < tiles or tiles == GRING:
                        tile_t(k + g + 1, (g + 1) % GRING)
                    expert_out(k + g, g % 2)

            tile_t(0, 0)
            ring(0)
            with pe.Fori(GRING, FULL - GRING + 1, GRING) as k:
                ring(k)
            ring(FULL, TILES - FULL)

        @block.vector
        def _(dve):
            dve.memset(patches[:, :, :, 0:1], 0.0).then_inc(s_dve0, 1)
            dve.memset(t_lo[:, :, :], 0.0).then_inc(s_dve0, 1)
            dve.memset(t_hi[:, :, :], 0.0).then_inc(s_dve0, 1)
            for b in range(A_BUFS):
                ins = dve.memset(decay[b][:, :, :, 0:1], 0.0)
            ins.then_inc(s_dve0, 1)
            n = 0
            for k in range(TAPS):
                dve.wait_ge(s_vmm, n + 1)
                dve.tensor_copy(v_lo[:, k, :], ps_g[n % 2][:, 0:INNER]).then_inc(s_vcopy, 1)
                n += 1
                dve.wait_ge(s_vmm, n + 1)
                o = v_hi[0:DLO, k // 2, :] if k % 2 == 0 else v_hi[DLO:P, k // 2, :]
                dve.tensor_copy(o, ps_g[n % 2][0:DLO, 0:INNER]).then_inc(s_vcopy, 1)
                n += 1
            dve.wait_ge(s_const, 16 * CONSTS)
            dve.wait_ge(s_clsrow, 16)
            dve.memset(rows[0][:, :, :], 0.0).then_inc(s_vcopy, 1)
            dve.memset(rows[1][:, :, :], 0.0).then_inc(s_vcopy, 1)
            dve.memset(pick[:, :, :], 0.0).then_inc(s_pick, 1)
            dve.wait_ge(s_pool0, 3)
            dve.wait_ge(s_pick, 1)
            for q in PIECES:
                v = slice(q * 2 * NS, (q + 1) * 2 * NS)
                ins = dve.tensor_copy(pick[v, :, :], ident[v, v].unsqueeze(2).to_broadcast([2 * NS, 2 * NS, P]))
            ins.then_inc(s_dve0, 1)

            def embed(n, r):
                need(dve, s_hres, n - 1)
                for b in range(2):
                    dve.wait_ge(s_tokmm, 2 * n + b + 1)
                    ins = dve.tensor_tensor(h[r][:, 2 * b:2 * b + 2, :], ps_k[b][0:H0, 0:2 * DIM].rearrange(
                        "p (f d) -> p f d", f=2), tok_bias[:, :, :], ALU.add)
                ins.then_inc(s_h, 1)

            def stats(n, src, st, mv, s_in, s_st, s_mv, s_ve):
                if s_in is not None:
                    dve.wait_ge(s_in, n + 1)
                for c in range(4):
                    ins = dve.bn_stats(st[:, c, :], src(c))
                ins.then_inc(s_st, 1)
                dve.wait_ge(s_clsrow, 16)
                dve.wait_ge(s_st, n + 1)
                for c in range(4):
                    ins = dve.bn_aggr(mv[:, c, :], st[:, c, :])
                ins.then_inc(s_mv, 1)
                dve.wait_ge(s_mv, n + 1)
                dve.tensor_scalar(mv[:, :, 0], mv[:, :, 0], -1.0, None, ALU.mult)
                dve.tensor_scalar(mv[:, :, 1], mv[:, :, 1], EPS, None, ALU.add).then_inc(s_ve, 1)

            def front_stats(n, r):
                embed(n, r)
                stats(n, lambda c: h[r][:, c, :], st1, mv1, s_h, s_st1, s_mv1, s_ve1)

            def bx(n, r, s):
                if s == 0:
                    dve.wait_ge(s_du, n + 1)
                dve.wait_ge(s_bb, NS * n + s + 1)
                u, m = (s - B_BUFS, n) if s >= B_BUFS else (s - B_BUFS + NS, n - 1)
                if u % 2 == 0 and u // 2 in FOLDED:
                    need(dve, s_fold, len(FOLDED) * m + u // 2 + 1)
                else:
                    need(dve, s_ysum, SUMS * m + sums_until(u))
                dve.tensor_tensor(hb[s % B_BUFS][:, :, :], du[r][:, :, :],
                                  ps_b[:, 0:N2].unsqueeze(1).to_broadcast([P, MB, N2]), ALU.mult).then_inc(s_bx, 1)

            def scan(n, s):
                b, a = s % B_BUFS, s % A_BUFS
                dve.wait_ge(s_a, NS * n + s + 1)
                dve.wait_ge(s_bx, NS * n + s + 1)
                v = hb[b].rearrange("p m t -> p (m t)")
                dve.tensor_tensor_scan(v, decay[a].rearrange("p m b t -> p (m b t)"), v, 0.0, ALU.mult,
                                       ALU.add).then_inc(s_scan, 1)

            def times_c(n, s):
                dve.wait_ge(s_scan, NS * n + s + 1)
                dve.wait_ge(s_cb, NS * n + s + 1)
                dve.tensor_tensor(hb[s % B_BUFS][:, :, :], hb[s % B_BUFS][:, :, :],
                                  ps_c[:, 0:N2].unsqueeze(1).to_broadcast([P, MB, N2]), ALU.mult).then_inc(s_mul, 1)

            def last_bc(n, r):
                v = slice(P - 2 * NS, P)
                dve.wait_ge(s_bcmid, n + 1)
                dve.tensor_tensor(bc3[r][v], bcf[v], bc3[r][v], ALU.subtract).then_inc(s_bc3, 1)

            def take_y(n, r, m):
                dve.wait_ge(s_ysum, SUMS * (n + 1))
                if m == 0:
                    need(dve, s_opmm, 2 * n)
                dve.scalar_tensor_tensor(out=y[:, m, :], in0=xz[r][:, m, :], scalar=dsk[:, m:m + 1],
                                         in1=ps_y[m][:, 0:N2], op0=ALU.mult, op1=ALU.add).then_inc(s_yev, 1)

            def out_stats(n):
                dve.wait_ge(s_opmm, 2 * (n + 1))
                stats(n, o_tile, st2, mv2, None, s_st2, s_mv2, s_ve2)

            def row_stats(n, r):
                stats(n, lambda c: rows[r][:, c, 0:DIM], st3, mv3, s_h2, s_st3, s_mv3, s_ve3)

            def take_logits(n):
                dve.wait_ge(s_lgmm, n + 1)
                dve.tensor_tensor(logits[:, ds(4 * n, 4), :], ps_t[0:H0, 0:4 * E].rearrange("p (c e) -> p c e", c=4),
                                  swb[:, :].unsqueeze(1).to_broadcast([H0, 4, E]), ALU.add).then_inc(s_lg, 1)

            def softplus_t(n, r):
                dve.wait_ge(s_spe, n + 1)
                need(dve, s_a, NS * (n - 1))
                dve.tensor_scalar(delta[r][:, :, :], spe[:, :, :], 1.0, -1.0, ALU.add, ALU.add).then_inc(s_spt, 1)

            def make_delta(n, r):
                dve.wait_ge(s_spl, n + 1)
                dve.wait_ge(s_spc, n + 1)
                dve.tensor_tensor(delta[r][:, :, :], spv[:, :, :], du[r][:, :, :], ALU.add).then_inc(s_delta, 1)

            def body(i, r, front, tokens):
                back = not isinstance(i, int) or i >= 1
                o = 1 - r
                for j in range(NS):
                    scan(i, j)
                    if back and j == 1:
                        for m in range(MB):
                            take_y(i - 1, o, m)
                    if j + 1 < NS:
                        bx(i, r, j + 1)
                    elif front:
                        bx(i + 1, o, 0)
                    if j in C_ON_DVE:
                        times_c(i, j)
                    if back:
                        if j == 4:
                            out_stats(i - 1)
                        if j == 7:
                            row_stats(i - 1, o)
                        if j == 14:
                            take_logits(i - 1)
                    if front:
                        if j == 12:
                            last_bc(i + 1, o)
                        if j == 12:
                            softplus_t(i + 1, o)
                        if j == 13:
                            make_delta(i + 1, o)
                    if tokens and j == 12:
                        front_stats(i + 2, r)

            front_stats(0, 0)
            front_stats(1, 1)
            last_bc(0, 0)
            softplus_t(0, 0)
            make_delta(0, 0)
            bx(0, 0, 0)
            for i in range(4):
                body(i, i % 2, True, True)
            with dve.Fori(4, PAIRS - 3, 2) as i:
                body(i, 0, True, True)
                body(i + 1, 1, True, True)
            body(PAIRS - 2, 0, True, False)
            body(PAIRS - 1, 1, False, False)
            n = PAIRS - 1
            for m in range(MB):
                take_y(n, 1, m)
            out_stats(n)
            row_stats(n, 1)
            take_logits(n)

            steps = [0]

            def link(ins):
                steps[0] += 1
                ins.then_inc(s_d, 1)
                dve.wait_ge(s_d, steps[0])

            def by_column(v):
                return v.unsqueeze(1).to_broadcast([H0, E, COLS])

            def by_expert(v):
                return v.unsqueeze(2).to_broadcast([H0, E, COLS])

            def last(v):
                return v.unsqueeze(2).to_broadcast([H0, COLS, E])

            dve.wait_ge(s_stored[0], 16 * PAIRS)
            dve.wait_ge(s_stored[1], 16 * PAIRS)
            dve.wait_ge(s_pool0, 3 + POOL_SET + 2)
            dve.wait_ge(s_lg, PAIRS)
            link(dve.tensor_reduce(exv, logits[:, :, :], AX.X, ALU.max))
            dve.tensor_tensor(ex, logits[:, :, :], last(exv), ALU.subtract).then_inc(s_exin, 1)
            dve.wait_ge(s_exout, 1)
            link(dve.tensor_reduce(exv, ex, AX.X, ALU.max))
            link(dve.tensor_reduce(rsum, ex, AX.X, ALU.add))
            link(dve.reciprocal(rsum, rsum))
            link(dve.tensor_tensor(prob, exv, rsum, ALU.mult))
            sel_c = sel.rearrange("p e c -> p (e c)").rearrange("p (c e) -> p c e", e=E)
            link(dve.tensor_tensor(sel_c, ex, last(exv), ALU.is_ge))
            link(dve.tensor_tensor(sel_c, sel_c, weights8.unsqueeze(1).to_broadcast([H0, COLS, E]), ALU.mult))
            link(dve.tensor_reduce(vmax, sel_c, AX.X, ALU.max))
            link(dve.tensor_tensor(oh, sel_c.rearrange("p c e -> p e c"), by_column(vmax), ALU.is_equal))
            link(dve.tensor_tensor(oh, oh, by_column(valid), ALU.mult))
            dve.tensor_tensor(member, oh, by_column(prob), ALU.mult).then_inc(s_ohr, 1)

            def ranks(times):
                dve.wait_ge(s_ranked, times)
                for e in range(E):
                    c = (e % 4) * COLS
                    ins = dve.tensor_tensor_scan(tot[:, e, :], one_cols, ps_g[e // 4][0:H0, c:c + COLS], 0.0, ALU.mult,
                                                 ALU.add)
                link(ins)
                for half in range(2):
                    v = slice(half * 4, half * 4 + 4)
                    ins = dve.tensor_tensor(place[:, v, :], tot[:, v, :], ps_g[half][0:H0, :].rearrange(
                        "p (e c) -> p e c", e=4), ALU.subtract)
                link(ins)
                for half in range(2):
                    v = slice(half * 4, half * 4 + 4)
                    ins = dve.tensor_tensor(place[:, v, :], place[:, v, :], ps_k[half][0:H0, :].rearrange(
                        "p (e c) -> p e c", e=4), ALU.add)
                link(ins)

            ranks(1)
            link(dve.tensor_copy(n_i, tot[:, :, COLS - 1]))
            link(dve.tensor_copy(n_e, n_i))
            link(dve.tensor_scalar(n_e, n_e, float(TS - 1), None, ALU.add))
            link(dve.tensor_copy(n_i, n_e))
            link(dve.tensor_scalar(n_i, n_i, TS.bit_length() - 1, None, ALU.logical_shift_right))
            link(dve.tensor_copy(tiles_e, n_i))
            link(dve.tensor_tensor_scan(tile_end, one_cols[:, 0:E], tiles_e, 0.0, ALU.mult, ALU.add))
            link(dve.tensor_tensor(base_e, tile_end, tiles_e, ALU.subtract))
            link(dve.tensor_scalar(base_e, base_e, float(TS), None, ALU.mult))
            link(dve.tensor_tensor(place, place, by_expert(base_e), ALU.add))
            link(dve.tensor_tensor(place, place, oh, ALU.mult))
            link(dve.tensor_reduce(destf, place.rearrange("p e c -> p c e"), AX.X, ALU.add))
            link(dve.tensor_copy(desti, destf))
            link(dve.tensor_scalar(dlo_i, desti, P - 1, None, ALU.bitwise_and))
            link(dve.tensor_scalar(dhi_i, desti, P.bit_length() - 1, None, ALU.logical_shift_right))
            link(dve.tensor_copy(destf, dlo_i))
            link(dve.tensor_copy(vmax, dhi_i))
            link(dve.scalar_tensor_tensor(out=destf, in0=destf, scalar=float(SC), in1=vmax, op0=ALU.mult, op1=ALU.add))
            link(dve.tensor_scalar(vmax, valid, -65536.0, 65536.0, ALU.mult, ALU.add))
            link(dve.tensor_tensor(destf, destf, vmax, ALU.add))
            dve.tensor_copy(desti, destf).then_inc(s_desti, 1)

            link(dve.tensor_tensor(tile_cmp, tile_no.unsqueeze(2).to_broadcast([1, TILES, E]),
                                   tile_end[0:1, :].unsqueeze(1).to_broadcast([1, TILES, E]), ALU.is_ge))
            link(dve.tensor_reduce(tile_no, tile_cmp, AX.X, ALU.add))
            link(dve.tensor_scalar(tile_no, tile_no, float(E - 1), None, ALU.min))
            dve.tensor_copy(tile_ex, tile_no).then_inc(s_tex, 1)

            dve.memset(lo_t, 0.0).then_inc(s_d, 1)
            dve.memset(hi_t, 2.0).then_inc(s_d, 1)
            steps[0] += 2
            dve.wait_ge(s_d, steps[0])
            base = steps[0]
            PER = 5

            def halve(t):
                c = [base + PER * t]

                def chain(ins):
                    c[0] = c[0] + 1
                    ins.then_inc(s_d, 1)
                    dve.wait_ge(s_d, c[0])

                chain(dve.tensor_tensor(mid_t, lo_t, hi_t, ALU.add))
                chain(dve.tensor_scalar(mid_t, mid_t, 0.5, None, ALU.mult))
                chain(dve.tensor_tensor(sel, member, by_expert(mid_t), ALU.is_ge))
                dve.tensor_reduce(cnt, sel, AX.X, ALU.add).then_inc(s_cnt, 1)
                dve.wait_ge(s_bis, t + 1)
                total = ps_y[0][0:H0, 0:E]
                dve.scalar_tensor_tensor(out=lo_c, in0=total, scalar=float(CAP), in1=mid_t, op0=ALU.is_ge, op1=ALU.mult)
                chain(dve.scalar_tensor_tensor(out=hi_c, in0=total, scalar=float(CAP), in1=mid_t, op0=ALU.is_ge,
                                               op1=ALU.add))
                dve.tensor_tensor(lo_t, lo_t, lo_c, ALU.max)
                chain(dve.tensor_tensor(hi_t, hi_t, hi_c, ALU.min))

            halve(0)
            with dve.Fori(1, BISECT, 1) as t:
                halve(t)
            steps[0] = base + PER * BISECT

            link(dve.tensor_tensor(sel, member, by_expert(lo_t), ALU.is_gt))
            dve.tensor_reduce(cnt, sel, AX.X, ALU.add).then_inc(s_cnt, 1)
            dve.wait_ge(s_bis, BISECT + 1)
            link(dve.tensor_scalar(room, ps_y[0][0:H0, 0:E], -1.0, float(CAP), ALU.mult, ALU.add))
            link(dve.tensor_tensor(sel, member, by_expert(lo_t), ALU.is_equal))
            dve.tensor_tensor(sel, sel, oh, ALU.mult).then_inc(s_tie, 1)
            ranks(2)
            link(dve.tensor_tensor(place, place, by_expert(room), ALU.is_lt))
            link(dve.tensor_tensor(place, place, sel, ALU.mult))
            link(dve.tensor_tensor(sel, member, by_expert(lo_t), ALU.is_gt))
            link(dve.tensor_tensor(place, place, sel, ALU.add))
            link(dve.tensor_reduce(vmax, place.rearrange("p e c -> p c e"), AX.X, ALU.add))
            link(dve.tensor_tensor(gates[:, :, 0], prob, vmax, ALU.mult))
            link(dve.tensor_scalar(vmax, vmax, -1.0, 1.0, ALU.mult, ALU.add))
            dve.tensor_tensor(gates[:, :, 1], prob, vmax, ALU.mult).then_inc(s_gate, 1)

            def gather_ids(k, g):
                if isinstance(k, int) and k < GRING:
                    done = s_gidx0
                else:
                    done = s_gidx[g]
                    dve.wait_ge(s_mtr, k - GRING + 1)
                dve.tensor_copy(gidx[g], slot_id[:, ds(2 * k, 2)]).then_inc(done, 1)

            def kept_input(k, g, r):
                dve.wait_ge(s_gat[g], 64 * ((k - g) // GRING + 1) if isinstance(k, int) else 64 // GRING * (k - g) + 64)
                for f in range(2):
                    ins = dve.scalar_tensor_tensor(out=mt[r][:, f, :], in0=grow[g][:, f, DIM:2 * DIM],
                                                   scalar=ggate[g][:, f, 1:2], in1=grow[g][:, f, 0:DIM], op0=ALU.mult,
                                                   op1=ALU.add)
                ins.then_inc(s_keepx, 1)

            def finish(k, g, r):
                need(dve, s_put[r], 32 * ((k - r) // 2) if isinstance(k, int) else 16 * (k - r))
                dve.tensor_copy(pidx[r], gidx[g])
                dve.wait_ge(s_w[r], 48 * ((k - r) // 2 + 1) if isinstance(k, int) else 24 * (k - r) + 48)
                for f in range(2):
                    dve.wait_ge(s_m2, 2 * k + f + 1)
                    ins = dve.tensor_tensor(mo[r][:, f, :], ps_k[f][:, 0:DIM], b2r[r], ALU.add)
                ins.then_inc(s_mbias, 1)
                dve.wait_ge(s_mbias, k + 1)
                dve.wait_ge(s_keepx, k + 1)
                for f in range(2):
                    ins = dve.scalar_tensor_tensor(out=mo[r][:, f, :], in0=mo[r][:, f, :], scalar=ggate[g][:, f, 0:1],
                                                   in1=mt[r][:, f, :], op0=ALU.mult, op1=ALU.add)
                ins.then_inc(s_mo[g], 1)

            dve.wait_ge(s_slot, 16)
            for g in range(GRING):
                gather_ids(g, g)

            def tile(k, g, more):
                kept_input(k, g, g % 2)
                finish(k, g, g % 2)
                if more:
                    gather_ids(k + GRING, g)

            for g in range(GRING):
                tile(g, g, True)
            with dve.Fori(GRING, FULL - 2 * GRING + 1, GRING) as k:
                for g in range(GRING):
                    tile(k + g, g, True)
            for t in range(FULL - GRING, TILES):
                tile(t, t % GRING, t + GRING < TILES)


def kernel(x, cls_tok, L0_tok_W, L0_tok_b, L0_attn_W_in, L0_attn_conv_w, L0_attn_conv_b, L0_attn_W_x, L0_attn_W_dt,
           L0_attn_b_dt, L0_attn_A_log, L0_attn_D, L0_attn_W_out, L0_attn_gamma, L0_attn_beta, L0_ffn_switch_w,
           L0_ffn_switch_b, L0_ffn_w1, L0_ffn_b1, L0_ffn_w2, L0_ffn_b2):
    import numpy as np
    import concourse.bacc as bacc
    from concourse.bass_utils import run_bass_kernel_spmd

    a = np.asarray

    def blocks(w, k):
        return a(w).reshape(k, P, -1).transpose(1, 0, 2)

    def column(v, k):
        return a(v).reshape(k, P).T

    w_in = a(L0_attn_W_in)
    w1, w2 = a(L0_ffn_w1), a(L0_ffn_w2)
    w_pack = np.concatenate([
        w1[:, 0:P, :],
        w2.reshape(E, KF, P, DIM).transpose(0, 2, 1, 3).reshape(E, P, KF * DIM),
        a(L0_ffn_b1).reshape(E, KF, P).transpose(0, 2, 1),
    ], axis=2)
    side = 14
    xt = a(x).reshape(PAIRS, 2, 3, side, 16, side, 16).transpose(0, 2, 4, 6, 1, 3, 5)
    xt = xt.reshape(PAIRS, KP, P, 2, PATCHES).transpose(0, 2, 1, 3, 4)
    arrays = {
        "x": xt,
        "cls_tok": a(cls_tok).reshape(1, DIM),
        "tok_w": blocks(a(L0_tok_W).T, KP),
        "tok_b": a(L0_tok_b),
        "w_inx": blocks(w_in[:, 0:INNER].T, MB),
        "w_zlo": w_in[0:P, INNER:],
        "w_zhi": w_in[P:DIM, INNER:],
        "conv_w": a(L0_attn_conv_w).reshape(TAPS, MB, P, INNER).transpose(2, 0, 1, 3),
        "conv_b": column(L0_attn_conv_b, MB),
        "w_x": blocks(L0_attn_W_x, MB),
        "w_dt": blocks(L0_attn_W_dt, MB),
        "b_dt": column(L0_attn_b_dt, MB),
        "a_log": blocks(L0_attn_A_log, MB),
        "d_skip": column(L0_attn_D, MB),
        "w_out": blocks(L0_attn_W_out, MB),
        "gamma": a(L0_attn_gamma),
        "beta": a(L0_attn_beta),
        "sw_w": a(L0_ffn_switch_w),
        "sw_b": a(L0_ffn_switch_b),
        "w_pack": w_pack,
        "w1_hi": w1[:, P:DIM, :],
        "b2": a(L0_ffn_b2),
    }
    arrays = {f"in_{k}": np.ascontiguousarray(v) for k, v in arrays.items()}
    nc = bacc.Bacc("TRN2", target_bir_lowering=False, num_devices=1)
    args = [nc.dram_tensor(k, v.shape, F32, kind="ExternalInput").ap() for k, v in arrays.items()]
    out = nc.dram_tensor("out_tokens", (TOK, DIM), F32, kind="ExternalOutput").ap()
    build(nc, *args, out)
    r = run_bass_kernel_spmd(nc, [arrays], core_ids=[0])
    return r.results[0]["out_tokens"].reshape(IMAGES, L, DIM)
```
